# Optimizing a Trainium2 kernel written in Bass

```python
import numpy as np
import jax
import jax.numpy as jnp

def _softmax(x, axis=-1):
    return jax.nn.softmax(x, axis=axis)

def _gelu(x):
    return jax.nn.gelu(x, approximate=True)

def _silu(x):
    return jax.nn.silu(x)

def _sigmoid(x):
    return jax.nn.sigmoid(x)

def _layernorm(x, axis=-1, eps=1e-05):
    m = jnp.mean(x, axis=axis, keepdims=True)
    v = jnp.var(x, axis=axis, keepdims=True)
    return (x - m) / jnp.sqrt(v + eps)

def _scatter_add(tgt, idx, src, axis=0):
    return tgt.at[idx].add(src)

def _segment_sum(src, seg, n):
    return jax.ops.segment_sum(src, seg, n)
kernel_name = 'mk_gps_d1_gnn_r8_9b73bc'

def setup_inputs(seed: int=0):
    np.random.seed(seed)
    _w = jnp.asarray

    def _rec_inputs():
        import jax
        import jax.numpy as jnp
        _gk = jax.random.key(seed)
        x = -0.0003929 + 0.9999 * jax.random.normal(jax.random.fold_in(_gk, 1), (1250, 512), jnp.float32)
        _s = jax.random.randint(jax.random.fold_in(_gk, 2), (10000,), 0, 1250, jnp.int32)
        _d = jax.random.randint(jax.random.fold_in(_gk, 3), (10000,), 0, 1250, jnp.int32)
        _loop = jnp.arange(1250, dtype=jnp.int32)
        src = jnp.concatenate([_s, _d, _loop])
        dst = jnp.concatenate([_d, _s, _loop])
        _o = jnp.argsort(dst, stable=True)
        src = src[_o]
        dst = dst[_o]
        return (x, src, dst)
    x, src, dst = _rec_inputs()

    def _L0_gnn_setup():
        import jax, jax.numpy as jnp
        import numpy as np
        N_NODES = 4096
        N_EDGES = 32768
        D = 512
        NUM_EXPERTS = 4
        TOP_K = 2
        LAYERS = 2
        key = jax.random.key(seed)
        ks = jax.random.split(key, 8)
        x = jax.random.normal(ks[0], (N_NODES, D), dtype=jnp.float32)
        edge_index = jax.random.randint(ks[1], (2, N_EDGES), 0, N_NODES, dtype=jnp.int64)
        s = 1.0 / np.sqrt(D)
        gate_W = jax.random.uniform(ks[2], (D, NUM_EXPERTS), jnp.float32, -s, s)
        gate_b = jax.random.uniform(ks[3], (NUM_EXPERTS,), jnp.float32, -s, s)
        Wl = jax.random.uniform(ks[4], (NUM_EXPERTS, LAYERS, D, D), jnp.float32, -s, s)
        bl = jax.random.uniform(ks[5], (NUM_EXPERTS, LAYERS, D), jnp.float32, -s, s)
        Wr = jax.random.uniform(ks[6], (NUM_EXPERTS, LAYERS, D, D), jnp.float32, -s, s)
        return {'x': x, 'gate_W': gate_W, 'gate_b': gate_b, 'Wl': Wl, 'bl': bl, 'Wr': Wr, 'edge_index': edge_index}
    _L0_gnn_all = _L0_gnn_setup()
    _L0_gnn_in = {k: v for k, v in _L0_gnn_all.items() if k in ('gate_W', 'gate_b', 'Wl', 'bl', 'Wr')}
    del _L0_gnn_all

    def _L0_mix_setup():
        import jax, jax.numpy as jnp
        import numpy as np
        DIM = 512
        HEADS = 8
        DIM_HEAD = 64
        INNER = HEADS * DIM_HEAD
        key = jax.random.key(seed)
        k1, k2, k3, k4 = jax.random.split(key, 4)
        x = jax.random.normal(k1, (4, 1024, DIM), dtype=jnp.float32)
        w_qkv = jax.random.normal(k2, (DIM, 3 * INNER), dtype=jnp.float32) / np.sqrt(DIM)
        w_out = jax.random.normal(k3, (INNER, DIM), dtype=jnp.float32) / np.sqrt(INNER)
        b_out = jax.random.normal(k4, (DIM,), dtype=jnp.float32) * 0.01
        return {'x': x, 'w_qkv': w_qkv, 'w_out': w_out, 'b_out': b_out}
    _L0_mix_all = _L0_mix_setup()
    _L0_mix_in = {k: v for k, v in _L0_mix_all.items() if k in ('w_qkv', 'w_out', 'b_out')}
    del _L0_mix_all

    def _L0_ffn_setup():
        import jax, jax.numpy as jnp
        import numpy as np
        D_MODEL = 512
        D_FF = 512
        N_EXPERTS = 16
        TOP_K = 3
        BATCH, SEQ = (1, 256)

        def _swiglu(combined):
            gate, up = jnp.split(combined, 2, axis=-1)
            return jax.nn.silu(gate) * up
        key = jax.random.key(seed)
        ks = jax.random.split(key, 6)
        x = jax.random.normal(ks[0], (BATCH, SEQ, D_MODEL), dtype=jnp.float32)
        gate_w = 0.01 * jax.random.normal(ks[1], (N_EXPERTS, D_MODEL), dtype=jnp.float32)
        expert_bias = jnp.zeros((N_EXPERTS,), dtype=jnp.float32)
        shared_gate_up = 0.02 * jax.random.normal(ks[2], (2 * D_FF, D_MODEL), dtype=jnp.float32)
        shared_down = 0.02 * jax.random.normal(ks[3], (D_MODEL, D_FF), dtype=jnp.float32)
        expert_gate_up = 0.02 * jax.random.normal(ks[4], (N_EXPERTS, 2 * D_FF, D_MODEL), dtype=jnp.float32)
        expert_down = 0.02 * jax.random.normal(ks[5], (N_EXPERTS, D_MODEL, D_FF), dtype=jnp.float32)
        return {'x': x, 'gate_w': gate_w, 'expert_bias': expert_bias, 'shared_gate_up': shared_gate_up, 'shared_down': shared_down, 'expert_gate_up': expert_gate_up, 'expert_down': expert_down}
    _L0_ffn_all = _L0_ffn_setup()
    _L0_ffn_in = {k: v for k, v in _L0_ffn_all.items() if k in ('gate_w', 'expert_bias', 'shared_gate_up', 'shared_down', 'expert_gate_up', 'expert_down')}
    del _L0_ffn_all
    return {'x': x, 'src': src, 'dst': dst, 'L0_gnn_gate_W': _L0_gnn_in['gate_W'], 'L0_gnn_gate_b': _L0_gnn_in['gate_b'], 'L0_gnn_Wl': _L0_gnn_in['Wl'], 'L0_gnn_bl': _L0_gnn_in['bl'], 'L0_gnn_Wr': _L0_gnn_in['Wr'], 'L0_mix_w_qkv': _L0_mix_in['w_qkv'], 'L0_mix_w_out': _L0_mix_in['w_out'], 'L0_mix_b_out': _L0_mix_in['b_out'], 'L0_ffn_gate_w': _L0_ffn_in['gate_w'], 'L0_ffn_expert_bias': _L0_ffn_in['expert_bias'], 'L0_ffn_shared_gate_up': _L0_ffn_in['shared_gate_up'], 'L0_ffn_shared_down': _L0_ffn_in['shared_down'], 'L0_ffn_expert_gate_up': _L0_ffn_in['expert_gate_up'], 'L0_ffn_expert_down': _L0_ffn_in['expert_down']}

def reference(x, src, dst, L0_gnn_gate_W, L0_gnn_gate_b, L0_gnn_Wl, L0_gnn_bl, L0_gnn_Wr, L0_mix_w_qkv, L0_mix_w_out, L0_mix_b_out, L0_ffn_gate_w, L0_ffn_expert_bias, L0_ffn_shared_gate_up, L0_ffn_shared_down, L0_ffn_expert_gate_up, L0_ffn_expert_down):
    import jax
    import jax.numpy as jnp

    def _L0_gnn_ref(x, gate_W, gate_b, Wl, bl, Wr, edge_index):
        import jax, jax.numpy as jnp
        import numpy as np
        N_NODES = 4096
        N_EDGES = 32768
        D = 512
        NUM_EXPERTS = 4
        TOP_K = 2
        LAYERS = 2
        n = x.shape[0]
        src, dst = (edge_index[0], edge_index[1])
        gates = jax.nn.softmax(x @ gate_W + gate_b, axis=-1)
        top_v, top_i = jax.lax.top_k(gates, TOP_K)
        deg = jax.ops.segment_sum(jnp.ones((src.shape[0],), x.dtype), dst, num_segments=n)
        inv_deg = jnp.where(deg > 0, 1.0 / jnp.maximum(deg, 1.0), 0.0)[:, None]

        def sage_conv(h, W_l, b_l, W_r):
            aggr = jax.ops.segment_sum(h[src], dst, num_segments=n) * inv_deg
            return aggr @ W_l + b_l + h @ W_r
        expert_outs = []
        for e in range(NUM_EXPERTS):
            h = x
            for l in range(LAYERS):
                h = sage_conv(h, Wl[e, l], bl[e, l], Wr[e, l])
                h = jax.nn.relu(h)
            expert_outs.append(h)
        expert_outputs = jnp.stack(expert_outs, axis=1)
        sel = jnp.take_along_axis(expert_outputs, top_i[:, :, None], axis=1)
        out = jnp.sum(sel * top_v[:, :, None], axis=1)
        return out

    def _L0_mix_ref(x, w_qkv, w_out, b_out):
        import jax, jax.numpy as jnp
        import numpy as np
        DIM = 512
        HEADS = 8
        DIM_HEAD = 64
        INNER = HEADS * DIM_HEAD
        b, n, d = x.shape
        qkv = x @ w_qkv
        q, k, v = jnp.split(qkv, 3, axis=-1)

        def to_heads(t):
            return t.reshape(b, n, HEADS, DIM_HEAD).transpose(0, 2, 1, 3)
        q, k, v = map(to_heads, (q, k, v))
        q = jax.nn.elu(q) + 1.0
        k = jax.nn.elu(k) + 1.0
        kv = jnp.einsum('bhnd,bhnm->bhdm', k, v)
        z = 1.0 / (jnp.einsum('bhnd,bhd->bhn', q, k.sum(axis=2)) + 1e-06)
        out = jnp.einsum('bhnd,bhdm->bhnm', q, kv) * z[..., None]
        out = out.transpose(0, 2, 1, 3).reshape(b, n, INNER)
        return out @ w_out + b_out

    def _L0_ffn_ref(x, gate_w, expert_bias, shared_gate_up, shared_down, expert_gate_up, expert_down):
        import jax, jax.numpy as jnp
        import numpy as np
        D_MODEL = 512
        D_FF = 512
        N_EXPERTS = 16
        TOP_K = 3
        BATCH, SEQ = (1, 256)

        def _swiglu(combined):
            gate, up = jnp.split(combined, 2, axis=-1)
            return jax.nn.silu(gate) * up
        B, S, D = x.shape
        xf = x.reshape(-1, D)
        shared_out = _swiglu(xf @ shared_gate_up.T) @ shared_down.T
        logits = xf @ gate_w.T
        affinity = jax.nn.sigmoid(logits)
        routing_scores = affinity + expert_bias
        _, sel = jax.lax.top_k(routing_scores, TOP_K)
        sel_aff = jnp.take_along_axis(affinity, sel, axis=1)
        gating = sel_aff / (sel_aff.sum(axis=-1, keepdims=True) + 1e-09)
        combined = jnp.einsum('td,efd->tef', xf, expert_gate_up)
        hidden = _swiglu(combined)
        expert_out = jnp.einsum('tef,edf->ted', hidden, expert_down)
        sel_out = jnp.take_along_axis(expert_out, sel[:, :, None], axis=1)
        routed_out = jnp.einsum('tk,tkd->td', gating, sel_out)
        out = shared_out + routed_out
        return out.reshape(B, S, D)
    edge_index = jnp.stack([src, dst])
    xn = _layernorm(x, axis=-1)
    x = x + _L0_gnn_ref(xn, L0_gnn_gate_W, L0_gnn_gate_b, L0_gnn_Wl, L0_gnn_bl, L0_gnn_Wr, edge_index) + _L0_mix_ref(xn[None], L0_mix_w_qkv, L0_mix_w_out, L0_mix_b_out)[0]
    x = x + _L0_ffn_ref(_layernorm(x, axis=-1)[None], L0_ffn_gate_w, L0_ffn_expert_bias, L0_ffn_shared_gate_up, L0_ffn_shared_down, L0_ffn_expert_gate_up, L0_ffn_expert_down)[0]
    return x

_drawn_inputs = setup_inputs


def setup_inputs(seed=0):
    import zlib

    import numpy as np

    out = dict(_drawn_inputs(seed))
    spreads = {'L0_ffn_expert_bias': (0.0, 0.742)}
    factors = {'L0_gnn_gate_b': 4.764, 'L0_gnn_bl': 5.527, 'L0_mix_b_out': 5.965, 'L0_ffn_gate_w': 8.992}
    for name, (base, spread) in spreads.items():
        noise = np.random.default_rng([zlib.crc32(name.encode()), seed]).standard_normal(out[name].shape)
        drawn = base * np.exp(spread * noise) if base else spread * noise
        out[name] = jnp.asarray(drawn.astype(out[name].dtype))
    for name, factor in factors.items():
        out[name] = (out[name] * factor).astype(out[name].dtype)
    return out
```

```python
import math
from contextlib import ExitStack

import concourse.bass as bass
from concourse import mybir
from concourse.alu_op_type import AluOpType as ALU

F32, F32R, BF16 = mybir.dt.float32, mybir.dt.float32r, mybir.dt.bfloat16
I16, I32, U32 = mybir.dt.int16, mybir.dt.int32, mybir.dt.uint32
ACT = mybir.ActivationFunctionType
AX = mybir.AxisListType

P = 128
N, D, E = 1250, 512, 21250
NT = math.ceil(N / P)
NP = NT * P
LAST = N - (NT - 1) * P
KD = D // P
CHUNKS = [(0, 428), (428, 426), (854, 426)]
EPS = 1e-5

ET = math.ceil(E / P)
EFULL = E // P
ETAIL = E - EFULL * P
WIN = 32
NW = NP // WIN
VISITS = 6
LONG = 3 * NW
ETP = ET + VISITS
KEY = 1312
WC = NT * WIN

PAIR_AFTER_Q = {2 * p + 1: p for p in range(6)}
PAIR_AFTER_KV = {i: 6 + i for i in range(NT)}
PAIR_AFTER_O = {2 * q + 1: 16 + q for q in range(4)}

GE = 4
HP = 4
VW = 130

NE, TOPK, FF = 16, 3, 512
GU = 2 * FF
ROUTED = (TOPK * N + NE * P) // P
TILES = NT + ROUTED
ROW = 528
GCOL, SCOL, TCOL = D, D + 4, D + 8
WB = GU // P + D // P
RB = 4
PREP_BANKS = (4, 6, 7)
DUMP = N


def program(nc, x, src, dst, gate_w, gate_b, wl, bl, wr, w_qkv, w_out, b_out, ffn_gate, ffn_bias,
            sh_gu, sh_dn, ex_gu, ex_dn, out):
    ctx = ExitStack()
    base = (nc.sbuf_base + 63) // 64 * 64

    def at(name, shape, dtype, offset):
        return nc.alloc_sbuf_tensor_at(name, shape, dtype, offset=base + offset)

    size = {F32: 4, F32R: 4, BF16: 2, I16: 2, I32: 4, U32: 4}
    place = [0]

    def here(name, shape, dtype):
        n = size[dtype]
        for s in shape[1:]:
            n *= s
        t = at(name, shape, dtype, place[0])
        place[0] += (n + 31) // 32 * 32
        assert base + place[0] <= nc.sbuf_usable_end, (name, place[0])
        return t

    ident = here("ident", [P, P], F32)
    ones_row = here("ones_row", [1, P], F32)
    valid = here("valid", [P, NT], F32)
    coef = here("coef", [P, NT, GE], F32)
    inv_nat = here("inv_nat", [P, NT], F32)
    stats = here("stats", [P, NT, 6], F32)
    mv = here("mv", [P, NT, 2], F32)
    rstd = here("rstd", [P, 4, NT], F32)
    b1 = here("b1", [P, GE * KD], F32)
    bounds_i = here("bounds_i", [1, 3 * NW + 1], I32)
    ones_r = here("ones_r", [P, 2], F32R)
    fill = here("fill", [P, ROW], F32)
    place[0] = X0 = (place[0] + 255) // 256 * 256
    X = here("X", [P, NT, D], F32)
    XN = here("XN", [P, NT, D], F32)
    XT = here("XT", [P, KD, NP], F32)
    AT = here("AT", [P, NT, NP], I16)
    R0 = place[0]
    XN_L = at("XN_L", [P, NT, D], F32R, X0 + NT * D * 4)

    K = here("K", [P, NT, D], F32)
    V = here("V", [P, NT, HP, VW], F32)
    QT = here("QT", [P, KD, NP], F32)
    W0 = place[0]
    WQKV = here("WQKV", [P, KD, 3 * D], F32)
    WO = at("WO", [P, KD, D], F32, W0)
    expo = [here(f"expo{i}", [P, 512], F32) for i in range(2)]
    KVB = here("KVB", [P, HP, P], F32)
    KSB = here("KSB", [P, HP, P], F32)
    bo = here("bo", [1, D], F32)
    gw = here("gw", [P, KD, GE], F32)
    b1_rows = here("b1_rows", [GE * KD, P], F32)
    gb = here("gb", [P, GE], F32)
    lg = here("lg", [P, NT, 8], F32)
    lt = here("lt", [P, 4, NT], F32)
    top8 = here("top8", [P, NT, 8], F32)
    idx8 = here("idx8", [P, NT, 8], U32)
    idxf = here("idxf", [P, NT, 8], F32)
    io8 = here("io8", [P, 8], F32)
    eq = here("eq", [P, NT, 2, GE], F32)
    keyT = here("keyT", [P, ETP], F32)
    lowT = here("lowT", [P, ETP], F32)
    iota_key = here("iota_key", [P, WC], I16)
    iota_low = here("iota_low", [P, P], I16)
    neg_win = here("neg_win", [P, NW], F32)
    low1 = here("low1", [P, 2, VISITS, P], BF16)
    key1 = here("key1", [P, 2, VISITS, WC], BF16)
    place[0] = R0
    e_raw = here("e_raw", [P, 2, 2, P], I32)
    e_int = here("e_int", [P, 2, 2, P], I32)
    e_f = here("e_f", [P, 2, 4, P], F32)
    e_mm = here("e_mm", [P, 2, 2], F32)
    win = here("win", [NW, 2], F32)
    ok = here("ok", [NW, 3, ET], F32)
    it_t = here("it_t", [NW, 2, ET], F32)
    lohi = here("lohi", [NW, 5], F32)
    row_f = here("row_f", [1, 3 * NW], F32)
    row_d = here("row_d", [1, NW], F32)

    place[0] = R0
    GT = here("GT", [P, KD, NP], F32)
    XN_H = at("XN_H", [P, NT, D], F32R, place[0])
    HT = here("HT", [P, KD, NP], F32)
    place[0] += 512
    W4 = [here(f"W{n}", [P, KD, D], F32) for n in ("l1", "r1", "l2", "r2")]
    b2 = here("b2", [1, D], F32)
    t1 = [here(f"t1_{i}", [P, D], F32) for i in range(2)]
    GH = here("GH", [P, NT, D], F32R)
    GL = at("GL", [P, NT, D], F32R, X0 + NT * D * 4)
    conv = [here(f"conv{i}", [P, NT, P], F32R) for i in range(2)]
    conv_low = here("conv_low", [P, NT, P], F32R)

    place[0] = X0 + NT * D * 4
    GUW = [here(f"GUW{s}", [P, 2, KD, GU], F32R) for s in "HL"]
    DNW = [here(f"DNW{s}", [P, 2, KD, D], F32R) for s in "HL"]
    raw = here("raw", [P, WB, D], F32)
    xg = here("xg", [P, ROW], F32)
    xt = [here(f"xt{s}", [P, KD, P], F32R) for s in "HL"]
    ht = [here(f"ht{s}", [P, KD, P], F32R) for s in "HL"]
    sig = here("sig", [P, FF], F32)
    ug = here("ug", [P, FF], F32)
    hid = here("hid", [P, FF], F32)
    y = here("y", [P, D], F32)
    meta = here("meta", [P, 2, 2], F32)
    y_gate = here("y_gate", [P, 1], F32)
    y_tok = here("y_tok", [P, 1], U32)
    slot = here("slot", [P, 1], F32)
    gprod = here("gprod", [P, 4], F32)
    nt_i = here("nt_i", [P, NE + 1], I32)
    F0 = place[0]
    XR = here("XR", [P, NT, ROW], F32)
    xft = [here(f"xft{i}", [P, KD, P], F32) for i in range(2)]
    fg_raw = here("fg_raw", [NE, D], F32)
    fgT = here("fgT", [P, KD, NE], F32)
    fb = here("fb", [P, NE], F32)
    aff = here("aff", [P, NT, NE], F32)
    score = here("score", [P, NT, NE], F32)
    f8 = here("f8", [P, NT, 8], F32)
    f8i = here("f8i", [P, NT, 8], U32)
    f8f = here("f8f", [P, NT, 8], F32)
    io16 = here("io16", [P, NE], F32)
    pick = here("pick", [P, TOPK, NT, NE], F32)
    M = here("M", [P, NT + 1, NE], F32)
    pref = here("pref", [P, NT, NE], F32)
    tmp16 = here("tmp16", [P, NT, NE], F32)
    gsel = here("gsel", [P, TOPK, NT], F32)
    gsum = here("gsum", [P, 2, NT], F32)
    sl = here("sl", [P, TOPK, NT], F32)
    sl_u = here("sl_u", [P, TOPK, NT], U32)
    cnt = here("cnt", [P, 6, NE], F32)
    cnt_i = here("cnt_i", [P, NE], I32)
    upper = here("upper", [P, P], F32)
    ones2 = here("ones2", [P, P], F32)

    B = [ctx.enter_context(nc.psum_tensor(f"B{i}", [P, 512], F32)) for i in range(8)]

    slots = nc.dram_tensor("slots", [(TILES + 1) * P, ROW], F32, kind="Internal").ap()

    def sem(name):
        return ctx.enter_context(nc.semaphore(name))

    ready = {n: sem(n) for n in (
        "x_in", "edge_fill", "edge_in", "wqkv_in", "small_in", "consts", "chain", "pool_chain",
        "edge_keys", "edge_pe", "edge_bounds", "bounds_out", "xn_done", "var_done", "std_done",
        "xt_pe", "xt_done", "lg_pe", "ex_max", "ex_exp",
        "q_pe", "q_exp", "q_done", "k_pe", "k_exp", "k_done", "v_pe", "v_done", "kv_pe", "kv_done",
        "at_pe", "den_done", "at_done", "o_pe", "o_done", "mix_setup",
        "hot_ready", "lhot_ready", "long_pe", "long_done", "at_ready", "win_pe", "win_done",
        "xn_h", "xn_l", "conv_done", "conv_l", "ag_low_pe", "ag_pe", "ag_inv", "ag_scaled", "ag_tpe", "ag_done",
        "h_pe", "h_done", "g_pe", "g_h", "g_done", "e_pe", "e_scaled", "e_gated", "e_done", "e_chain",
        "f_var", "f_std", "f_xn", "f_tpe", "f_tdone", "f_lg", "f_aff", "f_sel", "f_rank", "f_slots",
        "fill_made", "f_consts", "f_filled", "f_small", "f_placed", "f_shared", "f_base", "fgt_pe", "fgt_done",
        "prep_pe", "prep_h", "prep_l", "xg_in", "xt_tpe", "xt_h", "xt_l", "gate_pe", "up_pe",
        "sig_done", "hid_done", "h_tpe", "ht_h", "ht_l", "dn_pe", "y_done", "y_added", "y_free", "meta_done",
        "t_chain", "xg_read", "f_nt", "waited",
    )}
    w_in = [sem(f"w_in{i}") for i in range(4)]
    raw_in = [sem(f"raw_in{i}") for i in range(WB // RB)]
    S = ready

    block = ctx.enter_context(nc.Block())

    def cols(n):
        return slice(n * P, (n + 1) * P)

    def wait_first(eng, name, value):
        eng.wait_ge(S[name], value)
        eng.sem_inc(S["waited"], 1)

    def bank4(b):
        return B[b][:, :].rearrange("p (k n) -> p k n", k=KD)

    def experts(eng, tile):
        eng.wait_ge(S["f_nt"], 1)
        with eng.Fori(0, NE) as e:
            n = eng.value_load(nt_i[0:1, bass.ds(e, 1)], min_val=1, max_val=NT)
            tile(e, True)
            with eng.If(n > 1):
                with eng.Fori(1, n):
                    tile(e, False)
        n = eng.value_load(nt_i[0:1, NE:NE + 1], min_val=1, max_val=NT)
        with eng.Fori(0, n):
            tile(None, False)

    @block.sync
    def _(sp):
        sp.wait_ge(S["x_in"], 1)
        sp.dma_start(X[:, 0:NT - 1, :], x[0:(NT - 1) * P, :].rearrange("(t p) d -> p t d", p=P)).then_inc(S["x_in"], 16)
        sp.dma_start(X[0:LAST, NT - 1, :], x[(NT - 1) * P:N, :]).then_inc(S["x_in"], 16)
        sp.wait_ge(S["edge_fill"], 1)
        for k, t in enumerate((dst, src)):
            sp.dma_start(e_raw[:, 0, k, :], t[0:P * P].rearrange("(t p) -> t p", p=P)).then_inc(S["edge_in"], 16)
            sp.dma_start(e_raw[0:EFULL - P, 1, k, :],
                         t[P * P:EFULL * P].rearrange("(t p) -> t p", p=P)).then_inc(S["edge_in"], 16)
            sp.dma_start(e_raw[EFULL - P:EFULL - P + 1, 1, k, 0:ETAIL],
                         t[EFULL * P:E].rearrange("(t p) -> t p", t=1)).then_inc(S["edge_in"], 16)
        sp.dma_start(WQKV[:, :, :], w_qkv.rearrange("(k p) n -> p k n", p=P)).then_inc(S["wqkv_in"], 16)
        sp.wait_ge(S["fill_made"], 1)
        sp.dma_start(out[DUMP:DUMP + P, :], fill[:, 0:D]).then_inc(S["f_filled"], 16)
        per = 8
        for t in range(NT, TILES + 1, per):
            n = min(per, TILES + 1 - t)
            sp.dma_start(slots[t * P:(t + n) * P, :].rearrange("(t p) c -> p t c", p=P),
                         fill[:, :].unsqueeze(1).to_broadcast([P, n, ROW])).then_inc(S["f_filled"], 16)
        sp.wait_ge(S["k_pe"], NT)
        sp.wait_ge(S["v_pe"], NT)
        sp.dma_start(WO[:, :, :], w_out.rearrange("(k p) n -> p k n", p=P)).then_inc(S["wqkv_in"], 16)
        mats = [wl[:, 0], wr[:, 0], wl[:, 1], wr[:, 1]]
        sp.wait_ge(S["o_pe"], NT)
        with sp.Fori(0, GE) as e:
            for m, (freed, per) in enumerate((("h_pe", 12), ("h_pe", 12), ("g_pe", NT), ("e_pe", NT))):
                sp.wait_ge(S[freed], e * per + 1)
                sp.dma_start(W4[m][:, :, :], mats[m][bass.ds(e, 1)].rearrange("o (k p) n -> p (o k) n", p=P)).then_inc(w_in[m], 16)
            sp.dma_start(b2[:, :], bl[bass.ds(e, 1), 1, :]).then_inc(w_in[3], 16)
        sp.wait_ge(S["e_done"], GE * NT + 2)
        sp.wait_ge(S["conv_done"], (GE + 1) * NT + 2)
        for r in range(WB // RB):
            w = sh_gu[r * RB * P:(r + 1) * RB * P, :] if r < 2 else sh_dn
            sp.dma_start(raw[:, r * RB:(r + 1) * RB, :], w.rearrange("(q p) d -> p q d", p=P)).then_inc(raw_in[r], 16)
        sp.dma_start(fg_raw[:, :], ffn_gate).then_inc(S["f_small"], 16)
        sp.dma_start(fb[:, :], ffn_bias.partition_broadcast(P)).then_inc(S["f_small"], 16)
        sp.dma_start(out[0:(NT - 1) * P, :].rearrange("(t p) d -> p t d", p=P), X[:, 0:NT - 1, :]).then_inc(S["f_filled"], 16)
        sp.dma_start(out[(NT - 1) * P:N, :], X[0:LAST, NT - 1, :]).then_inc(S["f_filled"], 16)
        sp.wait_ge(S["f_xn"], NT)
        sp.wait_ge(S["f_consts"], 1)
        sp.dma_start(slots[0:NP, :].rearrange("(t p) c -> p t c", p=P), XR[:, :, :]).then_inc(S["f_shared"], 16)

        def raw_blocks(e, r):
            w = ex_gu[bass.ds(e, 1), r * RB * P:(r + 1) * RB * P, :] if r < 2 else ex_dn[bass.ds(e, 1)]
            sp.dma_start(raw[:, r * RB:(r + 1) * RB, :], w.rearrange("o (q p) d -> p (o q) d", p=P)).then_inc(raw_in[r], 16)

        sp.wait_ge(S["f_shared"], 16)
        sp.dma_start(xg[:, :], slots[0:P, :]).then_inc(S["xg_in"], 16)
        for r in range(WB // RB):
            sp.wait_ge(S["prep_pe"], (r + 1) * RB)
            raw_blocks(0, r)
        tile_no = sp.alloc_register("sp_tile")
        sp.reg_mov(tile_no, 0)

        def next_rows():
            g = sp.snap(tile_no, min_val=0, max_val=TILES - 1)
            sp.wait_ge(S["xt_tpe"], g + 1)
            sp.wait_ge(S["xg_read"], g + 1)
            sp.dma_start(xg[:, :], slots[bass.ds(g * P + P, P), :]).then_inc(S["xg_in"], 16)
            sp.reg_add(tile_no, tile_no, 1)

        sp.wait_ge(S["f_nt"], 1)
        for i in range(NT):
            if i == NT - 1:
                sp.wait_ge(S["f_placed"], 16 * NT * TOPK)
            next_rows()
            if i == 0:
                for r in range(WB // RB):
                    sp.wait_ge(S["prep_pe"], WB + (r + 1) * RB)
                    raw_blocks(1, r)
        with sp.Fori(1, NE - 1) as e:
            n = sp.value_load(nt_i[0:1, bass.ds(e, 1)], min_val=1, max_val=NT)
            next_rows()
            for r in range(WB // RB):
                sp.wait_ge(S["prep_pe"], e * WB + (WB + (r + 1) * RB))
                raw_blocks(e + 1, r)
            with sp.If(n > 1):
                with sp.Fori(1, n):
                    next_rows()
        with sp.Fori(NE - 1, NE + 1) as e:
            n = sp.value_load(nt_i[0:1, bass.ds(e, 1)], min_val=1, max_val=NT)
            with sp.Fori(0, n):
                next_rows()

    @block.gpsimd
    def _(pool):
        done = [0]

        def link(ins):
            done[0] += 1
            ins.then_inc(S["pool_chain"], 1)
            pool.wait_ge(S["pool_chain"], done[0])

        imprecise = dict(allow_small_or_imprecise_dtypes=True)
        link(pool.memset(X[96:P, NT - 1, :], 0.0))
        pool.sem_inc(S["x_in"], 1)
        pool.memset(e_raw[:, :, 0, :], N - 1)
        link(pool.memset(e_raw[:, :, 1, :], 8191))
        pool.sem_inc(S["edge_fill"], 1)
        link(pool.memset(ones_r[:, :].bitcast(F32), 1.0))
        link(pool.memset(ident[:, :], 0.0))
        link(pool.affine_select(out=ident[:, :], in_=ident[:, :], compare_op=ALU.not_equal, fill=1.0,
                                base=0, pattern=[[-1, P]], channel_multiplier=1))
        link(pool.memset(valid[:, :], 1.0))
        link(pool.affine_select(out=valid[:, :], in_=valid[:, :], compare_op=ALU.is_ge, fill=0.0,
                                base=N - 1, pattern=[[-P, NT]], channel_multiplier=-1))
        pool.iota(iota_key[:, :].rearrange("p (a w) -> p a w", a=NT), pattern=[[KEY, NT], [1, WIN]], base=0,
                  channel_multiplier=0, **imprecise)
        pool.iota(iota_low[:, :], pattern=[[1, P]], base=0, channel_multiplier=0, **imprecise)
        pool.iota(neg_win[:, :], pattern=[[-WIN, NW]], base=0, channel_multiplier=0, **imprecise)
        pool.iota(win[:, 0:1], pattern=[[0, 1]], base=0, channel_multiplier=WIN, **imprecise)
        pool.iota(win[:, 1:2], pattern=[[0, 1]], base=WIN, channel_multiplier=WIN, **imprecise)
        pool.iota(it_t[:, 0, :], pattern=[[1, ET]], base=1, channel_multiplier=0, **imprecise)
        pool.iota(it_t[:, 1, :], pattern=[[-1, ET]], base=256, channel_multiplier=0, **imprecise)
        pool.iota(io8[:, :], pattern=[[1, 8]], base=0, channel_multiplier=0, **imprecise)
        pool.memset(keyT[:, :], -10000.0)
        pool.memset(lowT[:, :], 0.0)
        link(pool.memset(ones_row[:, :], 1.0))
        pool.sem_inc(S["consts"], 1)
        for e in range(GE):
            pool.dma_start(b1_rows[e * KD:(e + 1) * KD, :],
                           bl[e, 0].rearrange("(k p) -> k p", p=P)).then_inc(S["small_in"], 16)
        pool.dma_start(gw[:, :, :], gate_w.rearrange("(k p) n -> p k n", p=P)).then_inc(S["small_in"], 16)
        pool.dma_start(gb[:, :], gate_b.partition_broadcast(P)).then_inc(S["small_in"], 16)
        pool.dma_start(bo[:, :], b_out.rearrange("(o d) -> o d", o=1)).then_inc(S["small_in"], 16)
        link(pool.memset(fill[:, :], 0.0))
        link(pool.iota(fill[:, TCOL:TCOL + 1], pattern=[[0, 1]], base=DUMP, channel_multiplier=1, **imprecise))
        pool.sem_inc(S["fill_made"], 1)
        pool.memset(lg[:, :, :], -1.0)
        pool.memset(KVB[:, :, :], 0.0)
        link(pool.memset(KSB[:, :, :], 0.0))
        pool.wait_ge(S["bounds_out"], 1)
        for h in range(HP):
            last = pool.tensor_copy(V[:, :, h, P:P + 1], valid[:, :].unsqueeze(2))
        link(last)
        pool.sem_inc(S["mix_setup"], 1)
        for i in range(NT):
            pool.wait_ge(S["xn_h"], i + 1)
            pool.tensor_tensor(XN_L[:, i, :], XN[:, i, :], XN_H[:, i, :].bitcast(F32), ALU.subtract).then_inc(S["xn_l"], 1)
        pool.sem_inc(S["e_done"], 2)
        with pool.Fori(0, GE) as e:
            for i in range(NT):
                pool.wait_ge(S["e_gated"], e * NT + i + 3)
                pool.tensor_tensor(X[:, i, :], X[:, i, :], t1[i % 2][:, :], ALU.add).then_inc(S["e_done"], 1)
        pool.wait_ge(S["e_done"], GE * NT + 2)
        pool.wait_ge(S["conv_done"], (GE + 1) * NT + 2)
        link(pool.memset(XR[:, :, D:ROW], 0.0))
        pool.memset(XR[:, :, GCOL + TOPK:GCOL + TOPK + 1], 1.0)
        pool.iota(XR[:, :, SCOL + TOPK], pattern=[[P, NT]], base=0, channel_multiplier=1, **imprecise)
        link(pool.iota(XR[:, :, TCOL], pattern=[[P, NT]], base=0, channel_multiplier=1, **imprecise))
        pool.sem_inc(S["f_consts"], 1)
        pool.iota(io16[:, :], pattern=[[1, NE]], base=0, channel_multiplier=0, **imprecise)
        pool.iota(slot[:, :], pattern=[[0, 1]], base=0, channel_multiplier=1, **imprecise)
        pool.memset(ones2[:, :], 1.0)
        link(pool.memset(upper[:, :], 1.0))
        link(pool.affine_select(out=upper[:, :], in_=upper[:, :], compare_op=ALU.is_gt, fill=0.0,
                                base=0, pattern=[[1, P]], channel_multiplier=-1))
        for z in [w[:, 1, :, :] for w in DNW] + [h[:, :, :] for h in ht]:
            pool.memset(z.bitcast(F32), 0.0)
        pool.iota(meta[:, :, 1], pattern=[[0, 2]], base=DUMP, channel_multiplier=1, **imprecise)
        pool.memset(nt_i[:, 0:1], NT)
        link(pool.memset(meta[:, :, 0], 0.0))
        pool.sem_inc(S["f_consts"], 1)
        fills = 3 + math.ceil((TILES + 1 - NT) / 8)
        pool.wait_ge(S["f_filled"], 16 * fills)
        pool.wait_ge(S["f_shared"], 16)
        tile_no = pool.alloc_register("pool_tile")
        pool.reg_mov(tile_no, 0)

        def tile(scatter=None):
            g = pool.snap(tile_no, min_val=0, max_val=TILES - 1)
            if scatter is not None:
                r = P if scatter < NT - 1 else LAST
                for k in range(TOPK):
                    pool.indirect_dma_start(
                        out=slots, out_offset=bass.IndirectOffsetOnAxis(ap=sl_u[0:r, k, scatter:scatter + 1], axis=0),
                        in_=XR[0:r, scatter, :], in_offset=None).then_inc(S["f_placed"], 16)
            add_rows(g)
            pool.reg_add(tile_no, tile_no, 1)

        def add_rows(g):
            wait_first(pool, "y_done", g + 2)
            pool.indirect_dma_start(
                out=out, out_offset=bass.IndirectOffsetOnAxis(ap=y_tok[:, 0:1], axis=0),
                in_=y[:, :], in_offset=None, compute_op=ALU.add).then_inc(S["y_added"], 16)
            pool.wait_ge(S["y_added"], g * 16 + 16)
            pool.sem_inc(S["y_free"], 1)

        pool.sem_inc(S["y_free"], 1)
        pool.wait_ge(S["f_slots"], 1)
        for i in range(NT):
            tile(i)
        with pool.Fori(1, NE + 1) as e:
            n = pool.value_load(nt_i[0:1, bass.ds(e, 1)], min_val=1, max_val=NT)
            with pool.Fori(0, n):
                tile()
        add_rows(pool.snap(tile_no, min_val=NT + NE, max_val=TILES))

    @block.scalar
    def _(act):
        act.wait_ge(S["var_done"], 1)
        act.activation(rstd[:, 1, :], rstd[:, 0, :], ACT.Sqrt).then_inc(S["std_done"], 1)
        act.preload_act_table(ACT.Exp)
        for i in range(NT):
            act.wait_ge(S["xt_pe"], i + 1)
            act.activation(XT[:, :, cols(i)], B[i % 2][:, :].rearrange("p (k n) -> p k n", k=KD),
                           ACT.Copy).then_inc(S["xt_done"], 1)
        act.wait_ge(S["ex_max"], 1)
        act.activation(lg[:, :, 0:GE], lg[:, :, 0:GE], ACT.Exp).then_inc(S["ex_exp"], 1)
        def window_pair(p):
            for w in (2 * p, 2 * p + 1):
                act.wait_ge(S["win_pe"], w + 1)
                act.activation(AT[:, :, w * WIN:(w + 1) * WIN],
                               B[6 + w % 2][:, 0:WC].rearrange("p (a w) -> p a w", a=NT), ACT.Copy).then_inc(S["win_done"], 1)

        for n in range(12):
            c, w = CHUNKS[n // KD]
            act.wait_ge(S["q_pe"], n + 1)
            if n >= 2:
                act.wait_ge(S["q_done"], n - 1)
            act.activation(expo[n % 2][:, 0:w], B[n % 2][:, 0:w], ACT.Exp).then_inc(S["q_exp"], 1)
            if n in PAIR_AFTER_Q:
                window_pair(PAIR_AFTER_Q[n])
        for i in range(NT):
            act.wait_ge(S["k_pe"], i + 1)
            if i < 2:
                act.wait_ge(S["q_done"], 11 + i)
            else:
                act.wait_ge(S["k_done"], i - 1)
            act.activation(expo[i % 2][:, :], B[2 + i % 2][:, :], ACT.Exp).then_inc(S["k_exp"], 1)
            act.wait_ge(S["v_pe"], i + 1)
            act.activation(V[:, i, :, 0:P], B[4 + i % 2][:, :].rearrange("p (h m) -> p h m", h=HP),
                           ACT.Copy).then_inc(S["v_done"], 1)
            window_pair(PAIR_AFTER_KV[i])
        act.wait_ge(S["kv_pe"], HP)
        for n in range(12):
            c, w = CHUNKS[n // HP]
            act.wait_ge(S["at_pe"], n + 1)
            if n < 2:
                act.wait_ge(S["k_done"], NT - 1 + n)
            else:
                act.wait_ge(S["at_done"], n - 1)
            act.activation(expo[n % 2][:, 0:w], B[2 + n % 2][:, 0:w], ACT.Copy, bias=1e-6).then_inc(S["den_done"], 1)
            if n < NT:
                act.activation(XN_H[:, n, :], XN[:, n, :], ACT.Copy).then_inc(S["xn_h"], 1)
        for i in sorted(PAIR_AFTER_O):
            window_pair(PAIR_AFTER_O[i])

        act.wait_ge(S["at_ready"], 1)
        for i in range(2):
            act.activation(conv[i][:, :, :], AT[:, :, cols(i)], ACT.Copy).then_inc(S["conv_done"], 1)
        for i in range(NT):
            act.wait_ge(S["ag_inv"], i + 1)
            if i >= 2:
                act.wait_ge(S["ag_tpe"], i - 1)
            act.activation(t1[i % 2][:, :], B[4 + i % 2][:, :], ACT.Copy, scale=inv_nat[:, i:i + 1]).then_inc(S["ag_scaled"], 1)
            act.activation(conv[i % 2][:, :, :], AT[:, :, cols((i + 2) % NT)], ACT.Copy).then_inc(S["conv_done"], 1)
        act.wait_ge(S["ag_tpe"], NT)
        act.sem_inc(S["h_done"], 2)
        act.wait_ge(S["small_in"], 16 * (GE + 3))
        with act.Fori(0, GE) as e:
            for n in range(12):
                (c, w), j = CHUNKS[n // KD], n % KD
                wait_first(act, "h_pe", e * 12 + n + 2)
                act.activation(HT[:, j, c:c + w], B[n % 2][:, 0:w], ACT.Relu,
                               bias=b1[:, bass.ds(e * KD + j, 1)]).then_inc(S["h_done"], 1)
            for i in range(NT):
                act.wait_ge(S["g_pe"], e * NT + i + 2)
                act.activation(GH[:, i, :], B[2 + i % 2][:, :], ACT.Copy).then_inc(S["g_h"], 1)
            for i in range(NT):
                act.wait_ge(S["e_pe"], e * NT + i + 2)
                act.wait_ge(S["e_done"], e * NT + i + 1)
                act.activation(t1[i % 2][:, :], B[4 + i % 2][:, :], ACT.Copy,
                               scale=inv_nat[:, i:i + 1]).then_inc(S["e_scaled"], 1)
                act.activation(conv[i % 2][:, :, :], AT[:, :, cols((i + 2) % NT)], ACT.Copy).then_inc(S["conv_done"], 1)
        act.wait_ge(S["f_var"], 1)
        act.activation(rstd[:, 1, :], rstd[:, 0, :], ACT.Sqrt).then_inc(S["f_std"], 1)
        act.preload_act_table(ACT.Sigmoid)
        for q in range(WB):
            act.wait_ge(S["prep_pe"], q + 1)
            dest = GUW[0][:, 0, :, cols(q)] if q < GU // P else DNW[0][:, 0, :, cols(q - GU // P)]
            act.activation(dest, bank4(PREP_BANKS[q % 3]), ACT.Copy).then_inc(S["prep_h"], 1)
            if 1 <= q <= NT:
                act.wait_ge(S["f_tpe"], q)
                act.activation(xft[(q - 1) % 2][:, :, :], bank4((q - 1) % 2), ACT.Copy).then_inc(S["f_tdone"], 1)
        act.wait_ge(S["xt_tpe"], 1)
        act.activation(xt[0][:, :, :], bank4(2), ACT.Copy).then_inc(S["xt_h"], 1)
        act.wait_ge(S["f_lg"], NT)
        act.activation(aff[:, :, :], B[3][:, 0:NT * NE].rearrange("p (t e) -> p t e", e=NE),
                       ACT.Sigmoid).then_inc(S["f_aff"], 1)

        def xt_high(n):
            act.wait_ge(S["xt_tpe"], n)
            act.activation(xt[0][:, :, :], bank4(2), ACT.Copy).then_inc(S["xt_h"], 1)

        act.sem_inc(S["y_done"], 1)
        tile_no = act.alloc_register("act_tile")
        act.reg_mov(tile_no, 0)

        def rows(g):
            act.wait_ge(S["dn_pe"], g + 1)
            act.wait_ge(S["meta_done"], g + 2)
            act.wait_ge(S["y_free"], g + 1)
            act.activation(y[:, :], B[5][:, :], ACT.Copy, scale=y_gate[:, 0:1]).then_inc(S["y_done"], 1)

        def tile(e, first):
            g = act.snap(tile_no, min_val=0, max_val=TILES - 1)
            par = None if e is None else (e + 1) & 1

            def blocks(*qs):
                for q in qs if first else ():
                    wait_first(act, "prep_pe", e * WB + (WB + q + 1))
                    if q < GU // P:
                        dest = GUW[0][:, bass.ds(par, 1), :, cols(q)]
                    else:
                        dest = DNW[0][:, bass.ds(par, 1), :, cols(q - GU // P)]
                    act.activation(dest.rearrange("p o k n -> p (o k) n"), bank4(PREP_BANKS[q % 3]),
                                   ACT.Copy).then_inc(S["prep_h"], 1)

            blocks(0, 1, 2)
            act.wait_ge(S["gate_pe"], g + 1)
            act.activation(sig[:, :], B[0][:, :], ACT.Sigmoid).then_inc(S["sig_done"], 1)
            blocks(3, 4, 5, 6, 7)
            xt_high(g + 2)
            rows(g)
            blocks(8)
            act.wait_ge(S["h_tpe"], g + 1)
            act.activation(ht[0][:, :, :], bank4(3), ACT.Copy).then_inc(S["ht_h"], 1)
            blocks(9, 10, 11)
            act.reg_add(tile_no, tile_no, 1)

        experts(act, tile)
        rows(act.snap(tile_no, min_val=NT + NE, max_val=TILES))

    @block.vector
    def _(dve):
        done = [0]

        def link(ins):
            done[0] += 1
            ins.then_inc(S["chain"], 1)
            dve.wait_ge(S["chain"], done[0])

        def normalise(dest, var_sem, std_sem, done_sem):
            for i in range(NT):
                last = dve.bn_stats(stats[:, i, :], X[:, i, :])
            link(last)
            for i in range(NT):
                last = dve.bn_aggr(mv[:, i, :], stats[:, i, :])
            link(last)
            link(dve.tensor_scalar(rstd[:, 0, :], mv[:, :, 1], EPS, None, ALU.add))
            dve.sem_inc(S[var_sem], 1)
            dve.wait_ge(S[std_sem], 1)
            link(dve.reciprocal(rstd[:, 2, :], rstd[:, 1, :]))
            link(dve.tensor_tensor(rstd[:, 3, :], rstd[:, 2, :], rstd[:, 2, :], ALU.mult))
            link(dve.tensor_tensor(rstd[:, 3, :], rstd[:, 3, :], rstd[:, 0, :], ALU.mult))
            link(dve.tensor_scalar(rstd[:, 3, :], rstd[:, 3, :], -0.5, 1.5, ALU.mult, ALU.add))
            link(dve.tensor_tensor(rstd[:, 3, :], rstd[:, 3, :], rstd[:, 2, :], ALU.mult))
            for i in range(NT):
                dve.tensor_scalar(dest[:, i, 0:D], X[:, i, :], mv[:, i, 0:1], rstd[:, 3, i:i + 1],
                                  ALU.subtract, ALU.mult).then_inc(S[done_sem], 1)

        dve.wait_ge(S["edge_in"], 6 * 16)
        link(dve.tensor_scalar(e_int[:, :, 0, :], e_raw[:, :, 1, :], 7, None, ALU.logical_shift_right))
        link(dve.tensor_scalar(e_int[:, :, 1, :], e_raw[:, :, 1, :], P - 1, None, ALU.bitwise_and))
        link(dve.tensor_copy(e_f[:, :, 0, :], e_raw[:, :, 0, :]))
        link(dve.tensor_copy(e_f[:, :, 1, :], e_int[:, :, 1, :]))
        link(dve.tensor_copy(e_f[:, :, 2, :], e_int[:, :, 0, :]))
        link(dve.scalar_tensor_tensor(e_f[:, :, 3, :], e_f[:, :, 2, :], float(KEY), e_f[:, :, 0, :],
                                      op0=ALU.mult, op1=ALU.add))
        link(dve.tensor_reduce(e_mm[:, :, 0], e_f[:, :, 0, :], AX.X, ALU.min))
        link(dve.tensor_reduce(e_mm[:, :, 1], e_f[:, :, 0, :], AX.X, ALU.max))
        dve.sem_inc(S["edge_keys"], 1)
        dve.wait_ge(S["x_in"], 33)
        normalise(XN, "var_done", "std_done", "xn_done")
        dve.wait_ge(S["consts"], 1)
        dve.wait_ge(S["edge_pe"], 1)
        T = B[2][:, :].rearrange("p (g k t) -> p g k t", g=2, k=2)
        dve.tensor_copy(keyT[:, 0:P], T[:, 0, 0, :])
        dve.tensor_copy(keyT[:, P:ET], T[:, 1, 0, 0:ET - P])
        dve.tensor_copy(lowT[:, 0:P], T[:, 0, 1, :])
        dve.tensor_copy(lowT[:, P:ET], T[:, 1, 1, 0:ET - P])
        link(dve.tensor_copy(ok[:, 0:2, :], B[3][0:NW, 0:2 * ET].rearrange("p (k t) -> p k t", k=2)))
        link(dve.tensor_scalar(ok[:, 2, :], ok[:, 1, :], win[:, 0:1], None, ALU.is_ge))
        link(dve.scalar_tensor_tensor(ok[:, 2, :], ok[:, 0, :], win[:, 1:2], ok[:, 2, :], op0=ALU.is_lt, op1=ALU.mult))
        link(dve.tensor_tensor(ok[:, 0, :], ok[:, 2, :], it_t[:, 0, :], ALU.mult))
        link(dve.tensor_tensor(ok[:, 1, :], ok[:, 2, :], it_t[:, 1, :], ALU.mult))
        link(dve.tensor_reduce(lohi[:, 0:2], ok[:, 0:2, :], AX.X, ALU.max))
        link(dve.tensor_scalar(lohi[:, 2:3], lohi[:, 1:2], -1.0, 256.0, ALU.mult, ALU.add))
        link(dve.tensor_scalar(lohi[:, 2:3], lohi[:, 2:3], float(ET - 1), None, ALU.min))
        link(dve.tensor_scalar(lohi[:, 3:4], lohi[:, 2:3], float(VISITS), None, ALU.add))
        link(dve.tensor_tensor(lohi[:, 4:5], lohi[:, 3:4], lohi[:, 0:1], ALU.max))
        dve.sem_inc(S["edge_bounds"], 1)
        dve.wait_ge(S["edge_pe"], 2)
        link(dve.tensor_copy(row_f[:, :], B[4][0:1, 0:3 * NW]))
        link(dve.tensor_tensor(row_d[:, :], row_f[:, 2 * NW:3 * NW], row_f[:, NW:2 * NW], ALU.subtract))
        link(dve.tensor_copy(bounds_i[:, 0:LONG], row_f[:, :]))
        link(dve.tensor_reduce(bounds_i[:, LONG:LONG + 1], row_d[:, :], AX.X, ALU.max))
        dve.sem_inc(S["bounds_out"], 1)

        dve.wait_ge(S["small_in"], 16 * (GE + 3))
        dve.wait_ge(S["lg_pe"], NT + 1)
        dve.wait_ge(S["mix_setup"], 1)
        link(dve.tensor_copy(b1[:, :], B[7][:, 0:GE * KD]))
        link(dve.tensor_tensor(lg[:, :, 0:GE], B[6][:, 0:NT * GE].rearrange("p (t e) -> p t e", e=GE),
                               gb[:, :].unsqueeze(1).to_broadcast([P, NT, GE]), ALU.add))
        link(dve.tensor_reduce(lt[:, 0, :], lg[:, :, 0:GE], AX.X, ALU.max))
        link(dve.tensor_tensor(lg[:, :, 0:GE], lg[:, :, 0:GE], lt[:, 0, :].unsqueeze(2).to_broadcast([P, NT, GE]),
                               ALU.subtract))
        dve.sem_inc(S["ex_max"], 1)
        dve.wait_ge(S["ex_exp"], 1)
        link(dve.tensor_reduce(lt[:, 1, :], lg[:, :, 0:GE], AX.X, ALU.add))
        link(dve.reciprocal(lt[:, 2, :], lt[:, 1, :]))
        link(dve.tensor_tensor(lg[:, :, 0:GE], lg[:, :, 0:GE], lt[:, 2, :].unsqueeze(2).to_broadcast([P, NT, GE]),
                               ALU.mult))
        for i in range(NT):
            last = dve.max(top8[:, i, :], lg[:, i, :])
        link(last)
        for i in range(NT):
            last = dve.max_index(idx8[:, i, :], top8[:, i, :], lg[:, i, :])
        link(last)
        link(dve.tensor_copy(idxf[:, :, :], idx8[:, :, :]))
        link(dve.tensor_tensor(eq[:, :, :, :], idxf[:, :, 0:2].unsqueeze(3).to_broadcast([P, NT, 2, GE]),
                               io8[:, 0:GE].unsqueeze(1).unsqueeze(1).to_broadcast([P, NT, 2, GE]), ALU.is_equal))
        link(dve.tensor_tensor(eq[:, :, 0, :], eq[:, :, 0, :], eq[:, :, 1, :], ALU.add))
        link(dve.tensor_tensor(coef[:, :, :], eq[:, :, 0, :], lg[:, :, 0:GE], ALU.mult))

        def feature(n, dest, e_tile, bank, exp_sem, done_sem):
            dve.wait_ge(S[exp_sem], n + 1)
            link(dve.tensor_scalar(e_tile, e_tile, 1.0, None, ALU.min))
            dve.scalar_tensor_tensor(dest, bank, 0.0, e_tile, op0=ALU.max, op1=ALU.add).then_inc(S[done_sem], 1)

        def one_hots(slot, v, tile_col, window):
            dve.tensor_scalar(low1[:, slot, v, :], iota_low[:, :], lowT[:, tile_col], None, ALU.is_equal)
            return dve.tensor_scalar(key1[:, slot, v, :], iota_key[:, :], keyT[:, tile_col],
                                     neg_win[:, window], ALU.subtract, ALU.is_equal)

        def hot_pair(p):
            for w in (2 * p, 2 * p + 1):
                lo = dve.value_load(bounds_i[0:1, w:w + 1], min_val=0, max_val=ET - 1)
                if w >= 2:
                    dve.wait_ge(S["win_pe"], w - 1)
                for v in range(VISITS):
                    one_hots(w % 2, v, bass.ds(lo + v, 1), slice(w, w + 1)).then_inc(S["hot_ready"], 1)

        hot_pair(0)
        for n in range(12):
            (c, w), j = CHUNKS[n // KD], n % KD
            feature(n, QT[:, j, c:c + w], expo[n % 2][:, 0:w], B[n % 2][:, 0:w], "q_exp", "q_done")
            if n in PAIR_AFTER_Q:
                hot_pair(PAIR_AFTER_Q[n] + 1)
        for i in range(NT):
            feature(i, K[:, i, :], expo[i % 2][:, :], B[2 + i % 2][:, :], "k_exp", "k_done")
            hot_pair(PAIR_AFTER_KV[i] + 1)
        for h in range(HP):
            dve.wait_ge(S["kv_pe"], h + 1)
            b = B[6 + h % 2]
            for r in (slice(0, 64), slice(64, P)):
                dve.tensor_copy(KVB[r, h, r], b[r, r])
                last = dve.tensor_copy(KSB[r, h, r], b[r, P:P + 1].to_broadcast([64, 64]))
            last.then_inc(S["kv_done"], 1)
        for n in range(12):
            (c, w), h = CHUNKS[n // HP], n % HP
            dve.wait_ge(S["den_done"], n + 1)
            r = expo[n % 2][:, 0:w]
            link(dve.reciprocal(r, r))
            dve.tensor_tensor(QT[:, h, c:c + w], B[n % 2][:, 0:w], r, ALU.mult).then_inc(S["at_done"], 1)
        for i in range(NT):
            dve.wait_ge(S["o_pe"], i + 1)
            dve.tensor_tensor(X[:, i, :], X[:, i, :], B[4 + i % 2][:, :], ALU.add).then_inc(S["o_done"], 1)
            if i in PAIR_AFTER_O and PAIR_AFTER_O[i] + 1 < NW // 2:
                hot_pair(PAIR_AFTER_O[i] + 1)

        dve.wait_ge(S["win_done"], NW)
        long = dve.value_load(bounds_i[0:1, LONG:LONG + 1], min_val=0, max_val=ETP)
        with dve.If(long > 0):
            more = dve.alloc_register("dve_more")
            dve.reg_mov(more, 1)
            with dve.Fori(0, NW) as w:
                at = dve.value_load(bounds_i[0:1, bass.ds(w + NW, 1)], min_val=VISITS, max_val=ETP - 1)
                end = dve.value_load(bounds_i[0:1, bass.ds(w + 2 * NW, 1)], min_val=VISITS, max_val=ETP - 1)
                with dve.If(end > at):
                    with dve.Fori(at, end) as t:
                        m = dve.snap(more, min_val=1, max_val=NW * ET)
                        one_hots(0, 0, bass.ds(t, 1), bass.ds(w, 1)).then_inc(S["lhot_ready"], 1)
                        dve.wait_ge(S["long_pe"], m)
                        part = AT[:, :, bass.ds(w * WIN, WIN)]
                        dve.tensor_tensor(part, part, B[6][:, 0:WC].rearrange("p (a w) -> p a w", a=NT), ALU.add)\
                            .then_inc(S["long_done"], 1)
                        dve.wait_ge(S["long_done"], m)
                        dve.reg_add(more, more, 1)
        dve.sem_inc(S["at_ready"], 1)

        def low_counts(n, i):
            with dve.If(long > 0):
                dve.wait_ge(S["conv_done"], n + 1)
                dve.wait_ge(S["ag_low_pe"], n + 1)
                dve.tensor_tensor(conv_low[:, :, :], AT[:, :, cols(i)], conv[i % 2][:, :, :].bitcast(F32), ALU.subtract)\
                    .then_inc(S["conv_l"], 1)

        for i in range(NT):
            low_counts(i, i)
            dve.wait_ge(S["ag_pe"], i + 1)
            link(dve.tensor_scalar(inv_nat[:, i:i + 1], B[2 + i % 2][:, 0:1], 1.0, None, ALU.max))
            dve.reciprocal(inv_nat[:, i:i + 1], inv_nat[:, i:i + 1]).then_inc(S["ag_inv"], 1)
            if i >= 1:
                dve.wait_ge(S["ag_tpe"], i)
                dve.tensor_copy(GT[:, :, cols(i - 1)], bank4((i - 1) % 2)).then_inc(S["ag_done"], 1)
        dve.wait_ge(S["ag_tpe"], NT)
        dve.tensor_copy(GT[:, :, cols(NT - 1)], bank4((NT - 1) % 2)).then_inc(S["ag_done"], 1)

        dve.sem_inc(S["g_done"], 2)
        dve.sem_inc(S["e_gated"], 2)
        with dve.Fori(0, GE) as e:
            for i in range(NT):
                dve.wait_ge(S["g_h"], e * NT + i + 1)
                dve.tensor_tensor(GL[:, i, :], B[2 + i % 2][:, :], GH[:, i, :].bitcast(F32), ALU.subtract).then_inc(S["g_done"], 1)
            for i in range(NT):
                low_counts(e * NT + (i + NT), i)
                dve.wait_ge(S["e_scaled"], e * NT + i + 1)
                dve.tensor_tensor(t1[i % 2][:, :], t1[i % 2][:, :], B[6 + i % 2][:, :], ALU.add).then_inc(S["e_chain"], 1)
                dve.wait_ge(S["e_chain"], e * NT + i + 1)
                dve.tensor_scalar(t1[i % 2][:, :], t1[i % 2][:, :], 0.0,
                                  coef[:, i, bass.ds(e, 1)], ALU.max, ALU.mult).then_inc(S["e_gated"], 1)

        dve.wait_ge(S["e_done"], GE * NT + 2)
        normalise(XR, "f_var", "f_std", "f_xn")
        def low_part(dest_l, dest_h, bank, done_sem):
            return dve.tensor_tensor(dest_l, bank, dest_h.bitcast(F32), ALU.subtract).then_inc(S[done_sem], 1)

        dve.wait_ge(S["fgt_pe"], 1)
        dve.tensor_copy(fgT[:, :, :], B[2][:, 0:KD * NE].rearrange("p (k e) -> p k e", e=NE)).then_inc(S["fgt_done"], 1)
        for q in range(WB):
            dve.wait_ge(S["prep_h"], q + 1)
            pair = [w[:, 0, :, cols(q)] for w in GUW] if q < GU // P else [w[:, 0, :, cols(q - GU // P)] for w in DNW]
            low_part(pair[1], pair[0], bank4(PREP_BANKS[q % 3]), "prep_l")
        STEPS = 8

        def gates(n, c):
            def step(k, ins):
                ins.then_inc(S["t_chain"], 1)
                dve.wait_ge(S["t_chain"], c + k)
            dve.wait_ge(S["xg_in"], n * 16)
            step(1, dve.tensor_copy(y_gate[:, :], meta[:, 1, 0:1]))
            step(2, dve.tensor_copy(y_tok[:, :], meta[:, 1, 1:2]))
            step(3, dve.tensor_copy(meta[:, 1, :], meta[:, 0, :]))
            step(4, dve.tensor_copy(meta[:, 0, 1:2], xg[:, TCOL:TCOL + 1]))
            step(5, dve.scalar_tensor_tensor(gprod[:, :], xg[:, SCOL:SCOL + 4], slot[:, 0:1], xg[:, GCOL:GCOL + 4],
                                             op0=ALU.is_equal, op1=ALU.mult))
            step(6, dve.tensor_scalar(slot[:, :], slot[:, :], float(P), None, ALU.add))
            step(7, dve.tensor_reduce(meta[:, 0, 0:1], gprod[:, :], AX.X, ALU.add))
            dve.sem_inc(S["xg_read"], 1)
            dve.sem_inc(S["meta_done"], 1)

        dve.wait_ge(S["f_consts"], 2)
        dve.wait_ge(S["xt_h"], 1)
        low_part(xt[1][:, :, :], xt[0][:, :, :], bank4(2), "xt_l")
        gates(1, 0)
        dve.wait_ge(S["f_small"], 32)
        dve.wait_ge(S["f_aff"], 1)
        link(dve.tensor_tensor(score[:, :, :], aff[:, :, :], fb[:, :].unsqueeze(1).to_broadcast([P, NT, NE]), ALU.add))
        for i in range(NT):
            last = dve.max(f8[:, i, :], score[:, i, :])
        link(last)
        for i in range(NT):
            last = dve.max_index(f8i[:, i, :], f8[:, i, :], score[:, i, :])
        link(last)
        link(dve.tensor_copy(f8f[:, :, :], f8i[:, :, :]))
        for k in range(TOPK):
            link(dve.tensor_tensor(pick[:, k, :, :], f8f[:, :, k:k + 1].to_broadcast([P, NT, NE]),
                                   io16[:, :].unsqueeze(1).to_broadcast([P, NT, NE]), ALU.is_equal))
            link(dve.tensor_tensor(tmp16[:, :, :], pick[:, k, :, :], aff[:, :, :], ALU.mult))
            link(dve.tensor_reduce(gsel[:, k, :], tmp16[:, :, :], AX.X, ALU.add))
        link(dve.tensor_tensor(gsum[:, 0, :], gsel[:, 0, :], gsel[:, 1, :], ALU.add))
        link(dve.tensor_tensor(gsum[:, 0, :], gsum[:, 0, :], gsel[:, 2, :], ALU.add))
        link(dve.tensor_scalar(gsum[:, 0, :], gsum[:, 0, :], 1e-9, None, ALU.add))
        link(dve.reciprocal(gsum[:, 1, :], gsum[:, 0, :]))
        dve.wait_ge(S["f_shared"], 16)
        for k in range(TOPK):
            link(dve.tensor_tensor(XR[:, :, GCOL + k], gsel[:, k, :], gsum[:, 1, :], ALU.mult))
        link(dve.tensor_tensor(tmp16[:, :, :], pick[:, 0, :, :], pick[:, 1, :, :], ALU.add))
        link(dve.tensor_tensor(tmp16[:, :, :], tmp16[:, :, :], pick[:, 2, :, :], ALU.add))
        link(dve.tensor_tensor(M[:, 0:NT, :], tmp16[:, :, :], valid[:, :].unsqueeze(2).to_broadcast([P, NT, NE]), ALU.mult))
        link(dve.memset(pref[:, 0, :], 0.0))
        for i in range(1, NT):
            link(dve.tensor_tensor(pref[:, i, :], pref[:, i - 1, :], M[:, i - 1, :], ALU.add))
        link(dve.tensor_tensor(M[:, NT, :], pref[:, NT - 1, :], M[:, NT - 1, :], ALU.add))
        dve.sem_inc(S["f_sel"], 1)
        dve.wait_ge(S["f_rank"], 1)
        counts = B[5][:, NT * NE:(NT + 1) * NE]
        link(dve.tensor_scalar(cnt[:, 0, :], counts, float(P - 1), None, ALU.add))
        link(dve.tensor_copy(cnt_i[:, :], cnt[:, 0, :]))
        link(dve.tensor_scalar(cnt_i[:, :], cnt_i[:, :], 7, None, ALU.logical_shift_right))
        link(dve.tensor_copy(cnt[:, 1, :], cnt_i[:, :]))
        link(dve.tensor_scalar(cnt[:, 1, :], cnt[:, 1, :], 1.0, None, ALU.max))
        link(dve.tensor_copy(nt_i[:, 1:NE + 1], cnt[:, 1, :]))
        dve.sem_inc(S["f_nt"], 1)
        link(dve.memset(cnt[:, 2, :], 1.0))
        link(dve.tensor_tensor_scan(cnt[:, 3, :], cnt[:, 2, :], cnt[:, 1, :], float(NT), ALU.mult, ALU.add))
        link(dve.tensor_tensor(cnt[:, 4, :], cnt[:, 3, :], cnt[:, 1, :], ALU.subtract))
        link(dve.tensor_scalar(cnt[:, 4, :], cnt[:, 4, :], float(P), None, ALU.mult))
        ranks = B[5][:, 0:NT * NE].rearrange("p (t e) -> p t e", e=NE)
        link(dve.tensor_tensor(score[:, :, :], ranks, cnt[:, 4, :].unsqueeze(1).to_broadcast([P, NT, NE]), ALU.add))
        for k in range(TOPK):
            link(dve.tensor_tensor(tmp16[:, :, :], score[:, :, :], pick[:, k, :, :], ALU.mult))
            link(dve.tensor_reduce(sl[:, k, :], tmp16[:, :, :], AX.X, ALU.add))
            link(dve.tensor_copy(XR[:, :, SCOL + k], sl[:, k, :]))
        link(dve.tensor_copy(sl_u[:, :, :], sl[:, :, :]))
        dve.sem_inc(S["f_slots"], 1)

        dve.sem_inc(S["ht_l"], 1)
        tile_no = dve.alloc_register("dve_tile")
        dve.reg_mov(tile_no, 0)

        def tile(e, first):
            g = dve.snap(tile_no, min_val=0, max_val=TILES - 1)
            par = None if e is None else (e + 1) & 1

            def blocks(*qs):
                for q in qs if first else ():
                    dve.wait_ge(S["prep_h"], e * WB + (WB + q + 1))
                    ws, qq = (GUW, q) if q < GU // P else (DNW, q - GU // P)
                    pair = [w[:, bass.ds(par, 1), :, cols(qq)].rearrange("p o k n -> p (o k) n") for w in ws]
                    low_part(pair[1], pair[0], bank4(PREP_BANKS[q % 3]), "prep_l")

            blocks(0, 1, 2)
            dve.wait_ge(S["sig_done"], g + 1)
            dve.tensor_tensor(ug[:, :], sig[:, :], B[0][:, :], ALU.mult).then_inc(S["t_chain"], 1)
            blocks(3, 4, 5, 6)
            dve.wait_ge(S["t_chain"], g * STEPS + STEPS)
            dve.wait_ge(S["up_pe"], g + 1)
            dve.tensor_tensor(hid[:, :], ug[:, :], B[1][:, :], ALU.mult).then_inc(S["hid_done"], 1)
            blocks(7)
            dve.wait_ge(S["xt_h"], g + 2)
            low_part(xt[1][:, :, :], xt[0][:, :, :], bank4(2), "xt_l")
            dve.wait_ge(S["y_free"], g + 1)
            dve.wait_ge(S["y_done"], g + 1)
            gates(g + 2, g * STEPS + STEPS)
            blocks(8)
            dve.wait_ge(S["ht_h"], g + 1)
            low_part(ht[1][:, :, :], ht[0][:, :, :], bank4(3), "ht_l")
            blocks(9, 10, 11)
            dve.reg_add(tile_no, tile_no, 1)

        experts(dve, tile)
        g = dve.snap(tile_no, min_val=NT + NE, max_val=TILES)
        dve.wait_ge(S["y_free"], g + 1)
        gates(g + 1, g * STEPS + STEPS - 1)

    @block.tensor
    def _(pe):
        def product(bank, pairs, start=True, stop=True):
            todo = []
            for a, b in pairs:
                if isinstance(a, tuple):
                    todo += [(a[0], b[0]), (a[0], b[1]), (a[1], b[0])]
                else:
                    todo.append((a, b))
            for n, (a, b) in enumerate(todo):
                last = pe.matmul(bank, a, b, start=start and n == 0, stop=stop and n == len(todo) - 1)
            return last

        pe.wait_ge(S["edge_keys"], 1)
        pe.wait_ge(S["consts"], 1)
        T = B[2][:, :].rearrange("p (g k t) -> p g k t", g=2, k=2)
        for g, n in ((0, P), (1, ET - P)):
            pe.transpose(T[:, g, 0, 0:n], e_f[0:n, g, 3, :], ident[0:n, 0:n])
            pe.transpose(T[:, g, 1, 0:n], e_f[0:n, g, 1, :], ident[0:n, 0:n])
            for k in range(2):
                c = k * ET + g * P
                last = pe.matmul(B[3][0:NW, c:c + n], e_mm[0:n, g, k:k + 1].to_broadcast([n, NW]), ident[0:n, 0:n],
                                 start=True, stop=True)
        last.then_inc(S["edge_pe"], 1)
        for i in range(NT):
            pe.wait_ge(S["xn_done"], i + 1)
            if i >= 2:
                pe.wait_ge(S["xt_done"], i - 1)
            for k in range(KD):
                last = pe.transpose(B[i % 2][:, cols(k)], XN[:, i, cols(k)], ident[:, :])
            last.then_inc(S["xt_pe"], 1)
        pe.wait_ge(S["edge_bounds"], 1)
        for k in range(3):
            last = pe.matmul(B[4][0:1, k * NW:(k + 1) * NW], lohi[:, 2 + k:3 + k], ident[0:NW, 0:NW], start=True, stop=True)
        last.then_inc(S["edge_pe"], 1)
        pe.wait_ge(S["xt_done"], NT)
        pe.wait_ge(S["small_in"], 16 * (GE + 3))
        for i in range(NT):
            product(B[6][:, i * GE:(i + 1) * GE], [(XT[:, k, cols(i)], gw[:, k, :]) for k in range(KD)])\
                .then_inc(S["lg_pe"], 1)
        pe.transpose(B[7][:, 0:GE * KD], b1_rows[:, :], ident[0:GE * KD, 0:GE * KD]).then_inc(S["lg_pe"], 1)
        def window_pair(p):
            for w in (2 * p, 2 * p + 1):
                lo_h, b = w % 2, B[6 + w % 2][:, 0:WC]
                if w >= 2:
                    pe.wait_ge(S["win_done"], w - 1)
                for v in range(VISITS):
                    pe.wait_ge(S["hot_ready"], w * VISITS + v + 1)
                    last = pe.matmul(b, low1[:, lo_h, v, :], key1[:, lo_h, v, :], start=v == 0, stop=v == VISITS - 1)
                last.then_inc(S["win_pe"], 1)

        pe.wait_ge(S["wqkv_in"], 16)
        for n in range(12):
            (c, w), j = CHUNKS[n // KD], n % KD
            if n >= 2:
                pe.wait_ge(S["q_done"], n - 1)
            product(B[n % 2][:, 0:w], [(WQKV[:, k, cols(j)], XT[:, k, c:c + w]) for k in range(KD)])\
                .then_inc(S["q_pe"], 1)
            if n == 0:
                pe.wait_ge(S["ex_max"], 1)
            if n in PAIR_AFTER_Q:
                window_pair(PAIR_AFTER_Q[n])
        pe.wait_ge(S["bounds_out"], 1)
        for i in range(NT):
            if i >= 2:
                pe.wait_ge(S["k_done"], i - 1)
            product(B[2 + i % 2][:, :], [(XT[:, k, cols(i)], WQKV[:, k, D:2 * D]) for k in range(KD)])\
                .then_inc(S["k_pe"], 1)
            if i >= 2:
                pe.wait_ge(S["v_done"], i - 1)
            product(B[4 + i % 2][:, :], [(XT[:, k, cols(i)], WQKV[:, k, 2 * D:3 * D]) for k in range(KD)])\
                .then_inc(S["v_pe"], 1)
            window_pair(PAIR_AFTER_KV[i])
        pe.wait_ge(S["k_done"], NT)
        pe.wait_ge(S["v_done"], NT)
        pe.wait_ge(S["mix_setup"], 1)
        pe.wait_ge(S["win_done"], 2 * (PAIR_AFTER_KV[NT - 1] + 1))
        for h in range(HP):
            if h >= 2:
                pe.wait_ge(S["kv_done"], h - 1)
            product(B[6 + h % 2][:, 0:P + 1], [(K[:, i, cols(h)], V[:, i, h, 0:P + 1]) for i in range(NT)])\
                .then_inc(S["kv_pe"], 1)
        pe.wait_ge(S["kv_done"], HP)
        for n in range(12):
            (c, w), h = CHUNKS[n // HP], n % HP
            if n >= 2:
                pe.wait_ge(S["at_done"], n - 1)
            product(B[n % 2][:, 0:w], [(KVB[:, h, :], QT[:, h, c:c + w])])
            product(B[2 + n % 2][:, 0:w], [(KSB[:, h, :], QT[:, h, c:c + w])]).then_inc(S["at_pe"], 1)
        pe.wait_ge(S["at_done"], 12)
        pe.wait_ge(S["wqkv_in"], 32)
        for i in range(NT):
            if i >= 2:
                pe.wait_ge(S["o_done"], i - 1)
            product(B[4 + i % 2][:, :], [(QT[:, h, cols(i)], WO[:, h, :]) for h in range(HP)]
                    + [(ones_row[:, :], bo[:, :])]).then_inc(S["o_pe"], 1)
            if i in PAIR_AFTER_O:
                window_pair(PAIR_AFTER_O[i])

        long = pe.value_load(bounds_i[0:1, LONG:LONG + 1], min_val=0, max_val=ETP)
        with pe.If(long > 0):
            more = pe.alloc_register("pe_more")
            pe.reg_mov(more, 1)
            with pe.Fori(0, NW) as w:
                at = pe.value_load(bounds_i[0:1, bass.ds(w + NW, 1)], min_val=VISITS, max_val=ETP - 1)
                end = pe.value_load(bounds_i[0:1, bass.ds(w + 2 * NW, 1)], min_val=VISITS, max_val=ETP - 1)
                with pe.If(end > at):
                    with pe.Fori(at, end):
                        pe.wait_ge(S["lhot_ready"], pe.snap(more, min_val=1, max_val=NW * ET))
                        pe.matmul(B[6][:, 0:WC], low1[:, 0, 0, :], key1[:, 0, 0, :], start=True, stop=True)\
                            .then_inc(S["long_pe"], 1)
                        pe.reg_add(more, more, 1)

        def aggregate(n, i, bank, high, low, ones=None):
            def products(counts, parts, a, stop):
                for part in parts:
                    last = pe.matmul(bank, counts[:, a, :], part[:, a, :], start=False if started else True,
                                     stop=stop and part is parts[-1], skip_group_check=True)
                    started.append(1)
                return last
            started = []
            pe.wait_ge(S["conv_done"], n + 1)
            for a in range(NT - 1):
                products(conv[i % 2], (high, low), a, False)
            with pe.If(long > 0):
                pe.wait_ge(S["conv_l"], n + 1)
                for a in range(NT):
                    last = products(conv_low, (high,), a, False)
                if ones is None:
                    last.then_inc(S["ag_low_pe"], 1)
            if ones is not None:
                for a in range(NT):
                    pe.matmul(ones, conv[i % 2][:, a, :], ones_r[:, :], start=a == 0, stop=False, skip_group_check=True)
                with pe.If(long > 0):
                    for a in range(NT):
                        last = pe.matmul(ones, conv_low[:, a, :], ones_r[:, :], start=False, stop=False,
                                         skip_group_check=True)
                    last.then_inc(S["ag_low_pe"], 1)
            return products(conv[i % 2], (high, low), NT - 1, True)

        def transpose_rows_out(i):
            pe.wait_ge(S["ag_scaled"], i + 1)
            if i >= 2:
                pe.wait_ge(S["ag_done"], i - 1)
            for k in range(KD):
                last = pe.transpose(B[i % 2][:, cols(k)], t1[i % 2][:, cols(k)], ident[:, :])
            last.then_inc(S["ag_tpe"], 1)

        pe.wait_ge(S["xn_l"], NT)
        pe.sem_inc(S["ag_low_pe"], 1)
        for i in range(NT):
            if i < 2:
                pe.wait_ge(S["o_done"], NT - 1 + i)
            else:
                pe.wait_ge(S["ag_scaled"], i - 1)
            aggregate(i, i, B[4 + i % 2][:, :], XN_H, XN_L, ones=B[2 + i % 2][:, 0:2]).then_inc(S["ag_pe"], 1)
            if i >= 1:
                transpose_rows_out(i - 1)
        transpose_rows_out(NT - 1)

        pe.wait_ge(S["ag_done"], NT)
        pe.sem_inc(S["h_pe"], 1)
        pe.sem_inc(S["g_pe"], 1)
        pe.sem_inc(S["e_pe"], 1)
        with pe.Fori(0, GE) as e:
            for m in range(2):
                pe.wait_ge(w_in[m], e * 16 + 16)
            for n in range(12):
                (c, w), j = CHUNKS[n // KD], n % KD
                pe.wait_ge(S["h_done"], e * 12 + n + 1)
                product(B[n % 2][:, 0:w], [(W4[0][:, k, cols(j)], GT[:, k, c:c + w]) for k in range(KD)]
                        + [(W4[1][:, k, cols(j)], XT[:, k, c:c + w]) for k in range(KD)]).then_inc(S["h_pe"], 1)
            pe.wait_ge(S["h_done"], e * 12 + 14)
            pe.wait_ge(w_in[2], e * 16 + 16)
            for i in range(NT):
                pe.wait_ge(S["g_done"], e * NT + i + 1)
                product(B[2 + i % 2][:, :], [(HT[:, k, cols(i)], W4[2][:, k, :]) for k in range(KD)])\
                    .then_inc(S["g_pe"], 1)
            pe.wait_ge(S["g_done"], e * NT + NT + 2)
            pe.wait_ge(w_in[3], e * 32 + 32)
            for i in range(NT):
                pe.wait_ge(S["e_gated"], e * NT + i + 1)
                product(B[6 + i % 2][:, :], [(HT[:, k, cols(i)], W4[3][:, k, :]) for k in range(KD)]
                        + [(ones_row[:, :], b2[:, :])])
                aggregate(e * NT + (i + NT), i, B[4 + i % 2][:, :], GH, GL).then_inc(S["e_pe"], 1)

        pe.wait_ge(S["e_gated"], GE * NT + 2)
        pe.wait_ge(S["f_small"], 32)
        for k in range(KD):
            last = pe.transpose(B[2][:, k * NE:(k + 1) * NE], fg_raw[:, cols(k)], ident[0:NE, 0:NE])
        last.then_inc(S["fgt_pe"], 1)
        pe.wait_ge(S["f_xn"], NT)
        pe.wait_ge(S["fgt_done"], 1)
        def weight_block(q):
            for k in range(KD):
                last = pe.transpose(B[PREP_BANKS[q % 3]][:, cols(k)], raw[:, q, cols(k)], ident[:, :])
            last.then_inc(S["prep_pe"], 1)

        def logits(i):
            pe.wait_ge(S["f_tdone"], i + 1)
            product(B[3][:, i * NE:(i + 1) * NE], [(xft[i % 2][:, k, :], fgT[:, k, :]) for k in range(KD)])\
                .then_inc(S["f_lg"], 1)

        for q in range(WB):
            if q % RB == 0:
                pe.wait_ge(raw_in[q // RB], 16)
            if q >= 3:
                pe.wait_ge(S["prep_l"], q - 2)
            weight_block(q)
            if q < NT:
                for k in range(KD):
                    last = pe.transpose(B[q % 2][:, cols(k)], XR[:, q, cols(k)], ident[:, :])
                last.then_inc(S["f_tpe"], 1)
            if 1 <= q <= NT:
                logits(q - 1)

        def transpose_rows(n):
            pe.wait_ge(S["xg_in"], n * 16)
            for k in range(KD):
                last = pe.transpose(B[2][:, cols(k)], xg[:, cols(k)], ident[:, :])
            last.then_inc(S["xt_tpe"], 1)

        transpose_rows(1)
        pe.wait_ge(S["f_sel"], 1)
        product(B[5][:, 0:NT * NE], [(upper[:, :], M[:, 0:NT, :].rearrange("p t e -> p (t e)")),
                                     (ones2[:, :], pref[:, :, :].rearrange("p t e -> p (t e)"))])
        product(B[5][:, NT * NE:(NT + 1) * NE], [(ones2[:, :], M[:, NT, :])]).then_inc(S["f_rank"], 1)
        tile_no = pe.alloc_register("pe_tile")
        pe.reg_mov(tile_no, 0)
        previous = pe.alloc_register("pe_previous")
        pe.reg_mov(previous, 1)

        def split_product(bank, rows, weights, after):
            for k in range(KD):
                for n, (a, b) in enumerate(((0, 0), (0, 1), (1, 0))):
                    last = pe.matmul(bank, rows[a][:, k, :], weights[b](k), start=k == 0 and n == 0,
                                     stop=k == KD - 1 and n == 2)
                if k < KD - 1:
                    after(k)
            return last

        def down(g, after=lambda k: None):
            pe.wait_ge(S["ht_l"], g + 1)
            pe.wait_ge(S["y_done"], g + 1)
            par = pe.snap(previous, min_val=0, max_val=1)
            split_product(B[5][:, :], ht, [lambda k, w=w: w[:, bass.ds(par, 1), k, :].rearrange("p o n -> p (o n)")
                                           for w in DNW], after).then_inc(S["dn_pe"], 1)
            after(KD - 1)

        def tile(e, first):
            g = pe.snap(tile_no, min_val=0, max_val=TILES - 1)
            ee = NE if e is None else e
            par = ee & 1

            def block(q):
                if first:
                    if q % RB == 0:
                        pe.wait_ge(raw_in[q // RB], e * 16 + 32)
                    pe.wait_ge(S["prep_l"], e * WB + (WB + q - 2))
                    weight_block(q)

            pe.wait_ge(S["xt_l"], g + 1)
            for half, done in ((0, "gate_pe"), (1, "up_pe")):
                split_product(B[half][:, :], xt,
                              [lambda k, w=w: w[:, bass.ds(par, 1), k, half * FF:(half + 1) * FF]
                               .rearrange("p o n -> p (o n)") for w in GUW],
                              lambda k: block(half * KD + k)).then_inc(S[done], 1)
                block(half * KD + KD - 1)
            transpose_rows(g + 2)
            down(g, lambda k: block(2 * KD + k) if k < KD - 1 else None)
            pe.reg_mov(previous, par)
            pe.wait_ge(S["hid_done"], g + 1)
            for k in range(KD):
                last = pe.transpose(B[3][:, cols(k)], hid[:, cols(k)], ident[:, :])
            last.then_inc(S["h_tpe"], 1)
            block(WB - 1)
            pe.reg_add(tile_no, tile_no, 1)

        pe.wait_ge(S["prep_l"], WB)
        experts(pe, tile)
        down(pe.snap(tile_no, min_val=NT + NE, max_val=TILES))

    ctx.close()


_INS = ["x", "src", "dst", "L0_gnn_gate_W", "L0_gnn_gate_b", "L0_gnn_Wl", "L0_gnn_bl", "L0_gnn_Wr",
        "L0_mix_w_qkv", "L0_mix_w_out", "L0_mix_b_out", "L0_ffn_gate_w", "L0_ffn_expert_bias",
        "L0_ffn_shared_gate_up", "L0_ffn_shared_down", "L0_ffn_expert_gate_up", "L0_ffn_expert_down"]


def kernel(**inputs):
    import numpy as np
    import concourse.bacc as bacc
    from concourse.bass_utils import run_bass_kernel_spmd

    nc = bacc.Bacc("TRN2", target_bir_lowering=False, num_devices=1)
    arrays, args = {}, []
    for name in _INS:
        a = np.ascontiguousarray(inputs[name])
        arrays[f"in_{name}"] = a
        args.append(nc.dram_tensor(f"in_{name}", a.shape, mybir.dt.from_np(a.dtype), kind="ExternalInput").ap())
    args.append(nc.dram_tensor("out_rows", (N + P, D), F32, kind="ExternalOutput").ap())
    program(nc, *args)
    r = run_bass_kernel_spmd(nc, [arrays], core_ids=[0])
    return r.results[0]["out_rows"][0:N]
```

```python
import math
from contextlib import ExitStack

import concourse.bass as bass
from concourse import mybir
from concourse.alu_op_type import AluOpType as ALU

F32, F32R, BF16 = mybir.dt.float32, mybir.dt.float32r, mybir.dt.bfloat16
I16, I32, U32 = mybir.dt.int16, mybir.dt.int32, mybir.dt.uint32
ACT = mybir.ActivationFunctionType
AX = mybir.AxisListType

P = 128
N, D, E = 1250, 512, 21250
NT = math.ceil(N / P)
NP = NT * P
LAST = N - (NT - 1) * P
KD = D // P
CHUNKS = [(0, 428), (428, 426), (854, 426)]
EPS = 1e-5
CW = CHUNKS[0][1]
STEPS1 = len(CHUNKS) * 2 * KD
RING = 4
GRING = 3
SLAB = (("WH", D), ("WL", D), ("XH", CW), ("XL", CW))

ET = math.ceil(E / P)
EFULL = E // P
ETAIL = E - EFULL * P
WIN = 32
NW = NP // WIN
VISITS = 6
LONG = 3 * NW
ETP = ET + VISITS
KEY = 1312
WC = NT * WIN

PAIR_AFTER_Q = {2 * p + 1: p for p in range(6)}
PAIR_AFTER_KV = {i: 6 + i for i in range(NT)}
PAIR_AFTER_O = {2 * q + 1: 16 + q for q in range(4)}

GE = 4
HP = 4
VW = 130

NE, TOPK, FF = 16, 3, 512
GU = 2 * FF
ROUTED = (TOPK * N + NE * P) // P
TILES = NT + ROUTED
ROW = 528
GCOL, SCOL, TCOL = D, D + 4, D + 8
WB = GU // P + D // P
RB = 4
PREP_BANKS = (4, 6, 7)
DUMP = N


def program(nc, x, src, dst, gate_w, gate_b, wl, bl, wr, w_qkv, w_out, b_out, ffn_gate, ffn_bias,
            sh_gu, sh_dn, ex_gu, ex_dn, out):
    ctx = ExitStack()
    base = (nc.sbuf_base + 63) // 64 * 64

    def at(name, shape, dtype, offset):
        return nc.alloc_sbuf_tensor_at(name, shape, dtype, offset=base + offset)

    size = {F32: 4, F32R: 4, BF16: 2, I16: 2, I32: 4, U32: 4}
    place = [0]

    def here(name, shape, dtype):
        n = size[dtype]
        for s in shape[1:]:
            n *= s
        t = at(name, shape, dtype, place[0])
        place[0] += (n + 31) // 32 * 32
        assert base + place[0] <= nc.sbuf_usable_end, (name, place[0])
        return t

    ident = here("ident", [P, P], F32)
    ones_row = here("ones_row", [1, P], F32)
    valid = here("valid", [P, NT], F32)
    coef = here("coef", [P, NT, GE], F32)
    inv_nat = here("inv_nat", [P, NT], F32)
    stats = here("stats", [P, NT, 6], F32)
    mv = here("mv", [P, NT, 2], F32)
    rstd = here("rstd", [P, 4, NT], F32)
    b1 = here("b1", [P, GE * KD], F32)
    bounds_i = here("bounds_i", [1, 3 * NW + 1], I32)
    ones_r = here("ones_r", [P, 2], F32R)
    ones_k = here("ones_k", [1, P], F32R)
    fill = here("fill", [P, ROW], F32)
    place[0] = X0 = (place[0] + 255) // 256 * 256
    X = here("X", [P, NT, D], F32)
    XN = here("XN", [P, NT, D], F32)
    XT = here("XT", [P, KD, NP], F32)
    AT = here("AT", [P, NT, NP], I16)
    R0 = place[0]
    XN_L = at("XN_L", [P, NT, D], F32R, X0 + NT * D * 4)

    K = here("K", [P, NT, D], F32)
    V = here("V", [P, NT, HP, VW], F32)
    QT = here("QT", [P, KD, NP], F32)
    W0 = place[0]
    WQKV = here("WQKV", [P, KD, 3 * D], F32)
    WO = at("WO", [P, KD, D], F32, W0)
    expo = [here(f"expo{i}", [P, 512], F32) for i in range(2)]
    KVB = here("KVB", [P, HP, P], F32)
    KSB = here("KSB", [P, HP, P], F32)
    bo = here("bo", [1, D], F32)
    gw = here("gw", [P, KD, GE], F32)
    b1_rows = here("b1_rows", [GE * KD, P], F32)
    gb = here("gb", [P, GE], F32)
    lg = here("lg", [P, NT, 8], F32)
    lt = here("lt", [P, 4, NT], F32)
    top8 = here("top8", [P, NT, 8], F32)
    idx8 = here("idx8", [P, NT, 8], U32)
    idxf = here("idxf", [P, NT, 8], F32)
    io8 = here("io8", [P, 8], F32)
    eq = here("eq", [P, NT, 2, GE], F32)
    keyT = here("keyT", [P, ETP], F32)
    lowT = here("lowT", [P, ETP], F32)
    iota_key = here("iota_key", [P, WC], I16)
    iota_low = here("iota_low", [P, P], I16)
    neg_win = here("neg_win", [P, NW], F32)
    low1 = here("low1", [P, 2, VISITS, P], BF16)
    key1 = here("key1", [P, 2, VISITS, WC], BF16)
    place[0] = R0
    e_raw = here("e_raw", [P, 2, 2, P], I32)
    e_int = here("e_int", [P, 2, 2, P], I32)
    e_f = here("e_f", [P, 2, 4, P], F32)
    e_mm = here("e_mm", [P, 2, 2], F32)
    win = here("win", [NW, 2], F32)
    ok = here("ok", [NW, 3, ET], F32)
    it_t = here("it_t", [NW, 2, ET], F32)
    lohi = here("lohi", [NW, 5], F32)
    row_f = here("row_f", [1, 3 * NW], F32)
    row_d = here("row_d", [1, NW], F32)

    place[0] = R0
    XN_H = at("XN_H", [P, NT, D], F32R, place[0])
    HT = here("HT", [P, KD, NP], F32)
    GH = here("GH", [P, NT, D], F32R)
    GL = at("GL", [P, NT, D], F32R, X0 + NT * D * 4)
    W = at("W", [P, 2, 2, KD, D], F32, place[0])
    WR = here("WR", [P, 2, 2, KD, D], F32R)
    b2 = [here(f"b2{s}", [1, D], t) for s, t in (("", F32), ("H", F32R), ("L", F32R))]
    t1 = [here(f"t1_{i}", [P, D], F32) for i in range(2)]
    conv0 = place[0]
    conv = [here(f"conv{i}", [P, NT, P], F32R) for i in range(2)]
    conv_low = here("conv_low", [P, NT, P], F32R)
    graw = [here(f"graw{i}", [P, CW], F32) for i in range(GRING)]
    slabs0 = place[0]
    place[0] = conv0
    slabs = [None, None] + [[here(f"slab{s}{i}", [P, n], F32R) for s, n in SLAB] for i in (2, 3)]
    assert place[0] <= slabs0 - GRING * CW * 4 and slabs0 + 2 * (2 * D + 2 * CW) * 4 <= nc.sbuf_usable_end - base
    place[0] = slabs0
    slabs[0:2] = [[here(f"slab{s}{i}", [P, n], F32R) for s, n in SLAB] for i in (0, 1)]
    place[0] = slabs0
    hs = [[here(f"hs{s}{i}", [P, KD, P], F32R) for s in "HL"] for i in range(2)]
    place[0] = slabs0
    g_out = [here(f"g_out{i}", [P, KD, P], F32) for i in range(2)]

    place[0] = X0 + NT * D * 4
    GUW = [here(f"GUW{s}", [P, 2, KD, GU], F32R) for s in "HL"]
    DNW = [here(f"DNW{s}", [P, 2, KD, D], F32R) for s in "HL"]
    raw = here("raw", [P, WB, D], F32)
    xg = here("xg", [P, ROW], F32)
    xt = [here(f"xt{s}", [P, KD, P], F32R) for s in "HL"]
    ht = [here(f"ht{s}", [P, KD, P], F32R) for s in "HL"]
    sig = here("sig", [P, FF], F32)
    ug = here("ug", [P, FF], F32)
    hid = here("hid", [P, FF], F32)
    y = here("y", [P, D], F32)
    meta = here("meta", [P, 2, 2], F32)
    y_gate = here("y_gate", [P, 1], F32)
    y_tok = here("y_tok", [P, 1], U32)
    slot = here("slot", [P, 1], F32)
    gprod = here("gprod", [P, 4], F32)
    nt_i = here("nt_i", [P, NE + 1], I32)
    F0 = place[0]
    XR = here("XR", [P, NT, ROW], F32)
    xft = [here(f"xft{i}", [P, KD, P], F32) for i in range(2)]
    fg_raw = here("fg_raw", [NE, D], F32)
    fgT = here("fgT", [P, KD, NE], F32)
    fb = here("fb", [P, NE], F32)
    aff = here("aff", [P, NT, NE], F32)
    score = here("score", [P, NT, NE], F32)
    f8 = here("f8", [P, NT, 8], F32)
    f8i = here("f8i", [P, NT, 8], U32)
    f8f = here("f8f", [P, NT, 8], F32)
    io16 = here("io16", [P, NE], F32)
    pick = here("pick", [P, TOPK, NT, NE], F32)
    M = here("M", [P, NT + 1, NE], F32)
    pref = here("pref", [P, NT, NE], F32)
    tmp16 = here("tmp16", [P, NT, NE], F32)
    gsel = here("gsel", [P, TOPK, NT], F32)
    gsum = here("gsum", [P, 2, NT], F32)
    sl = here("sl", [P, TOPK, NT], F32)
    sl_u = here("sl_u", [P, TOPK, NT], U32)
    cnt = here("cnt", [P, 6, NE], F32)
    cnt_i = here("cnt_i", [P, NE], I32)
    upper = here("upper", [P, P], F32)
    ones2 = here("ones2", [P, P], F32)

    B = [ctx.enter_context(nc.psum_tensor(f"B{i}", [P, 512], F32)) for i in range(8)]

    gt = nc.dram_tensor("gt", [KD, P, NP], F32, kind="Internal").ap()
    slots = nc.dram_tensor("slots", [(TILES + 1) * P, ROW], F32, kind="Internal").ap()

    def sem(name):
        return ctx.enter_context(nc.semaphore(name))

    ready = {n: sem(n) for n in (
        "x_in", "edge_fill", "edge_in", "wqkv_in", "small_in", "consts", "chain", "pool_chain",
        "edge_keys", "edge_pe", "edge_bounds", "bounds_out", "xn_done", "var_done", "std_done",
        "xt_pe", "xt_done", "lg_pe", "ex_max", "ex_exp",
        "q_pe", "q_exp", "q_done", "k_pe", "k_exp", "k_done", "v_pe", "v_done", "kv_pe", "kv_done",
        "at_pe", "den_done", "at_done", "o_pe", "o_done", "mix_setup",
        "hot_ready", "lhot_ready", "long_pe", "long_done", "at_ready", "win_pe", "win_done",
        "xn_h", "xn_l", "conv_done", "conv_l", "ag_low_pe", "ag_pe", "ag_inv", "ag_scaled", "ag_tpe", "ag_done",
        "w1_in", "wl2_in", "wr2_in", "b2_in", "b2_split", "slab_h", "slab_l", "l1_pe", "w2_h", "w2_l",
        "hs_h", "hs_l", "h_done", "g_pe", "g_h", "g_done", "e_pe", "e_scaled", "e_gated", "e_done", "e_chain",
        "f_var", "f_std", "f_xn", "f_tpe", "f_tdone", "f_lg", "f_aff", "f_sel", "f_rank", "f_slots",
        "fill_made", "f_consts", "f_filled", "f_small", "f_placed", "f_shared", "f_base", "fgt_pe", "fgt_done",
        "prep_pe", "prep_h", "prep_l", "xg_in", "xt_tpe", "xt_h", "xt_l", "gate_pe", "up_pe",
        "sig_done", "hid_done", "h_tpe", "ht_h", "ht_l", "dn_pe", "y_done", "y_added", "y_free", "meta_done",
        "t_chain", "xg_read", "f_nt", "waited",
    )}
    gt_out = [sem(f"gt_out{i}") for i in range(2)]
    g_in = [sem(f"g_in{i}") for i in range(GRING)]
    raw_in = [sem(f"raw_in{i}") for i in range(WB // RB)]
    S = ready

    block = ctx.enter_context(nc.Block())

    def cols(n):
        return slice(n * P, (n + 1) * P)

    def wait_first(eng, name, value):
        eng.wait_ge(S[name], value)
        eng.sem_inc(S["waited"], 1)

    def hs_free(e, u):
        if u < 2:
            return "l1_pe", e * STEPS1 + (RING + STEPS1)
        if u < NT + 2:
            return "g_pe", e * NT + (u + 1)
        return "e_pe", e * NT + (u - NT)

    def bank4(b):
        return B[b][:, :].rearrange("p (k n) -> p k n", k=KD)

    def experts(eng, tile):
        eng.wait_ge(S["f_nt"], 1)
        with eng.Fori(0, NE) as e:
            n = eng.value_load(nt_i[0:1, bass.ds(e, 1)], min_val=1, max_val=NT)
            tile(e, True)
            with eng.If(n > 1):
                with eng.Fori(1, n):
                    tile(e, False)
        n = eng.value_load(nt_i[0:1, NE:NE + 1], min_val=1, max_val=NT)
        with eng.Fori(0, n):
            tile(None, False)

    @block.sync
    def _(sp):
        sp.wait_ge(S["x_in"], 1)
        sp.dma_start(X[:, 0:NT - 1, :], x[0:(NT - 1) * P, :].rearrange("(t p) d -> p t d", p=P)).then_inc(S["x_in"], 16)
        sp.dma_start(X[0:LAST, NT - 1, :], x[(NT - 1) * P:N, :]).then_inc(S["x_in"], 16)
        sp.wait_ge(S["edge_fill"], 1)
        for k, t in enumerate((dst, src)):
            sp.dma_start(e_raw[:, 0, k, :], t[0:P * P].rearrange("(t p) -> t p", p=P)).then_inc(S["edge_in"], 16)
            sp.dma_start(e_raw[0:EFULL - P, 1, k, :],
                         t[P * P:EFULL * P].rearrange("(t p) -> t p", p=P)).then_inc(S["edge_in"], 16)
            sp.dma_start(e_raw[EFULL - P:EFULL - P + 1, 1, k, 0:ETAIL],
                         t[EFULL * P:E].rearrange("(t p) -> t p", t=1)).then_inc(S["edge_in"], 16)
        sp.dma_start(WQKV[:, :, :], w_qkv.rearrange("(k p) n -> p k n", p=P)).then_inc(S["wqkv_in"], 16)
        sp.wait_ge(S["fill_made"], 1)
        sp.dma_start(out[DUMP:DUMP + P, :], fill[:, 0:D]).then_inc(S["f_filled"], 16)
        per = 8
        for t in range(NT, TILES + 1, per):
            n = min(per, TILES + 1 - t)
            sp.dma_start(slots[t * P:(t + n) * P, :].rearrange("(t p) c -> p t c", p=P),
                         fill[:, :].unsqueeze(1).to_broadcast([P, n, ROW])).then_inc(S["f_filled"], 16)
        sp.wait_ge(S["k_pe"], NT)
        sp.wait_ge(S["v_pe"], NT)
        sp.dma_start(WO[:, :, :], w_out.rearrange("(k p) n -> p k n", p=P)).then_inc(S["wqkv_in"], 16)
        def first_weights(e, half):
            for m, t in enumerate((wl, wr)):
                sp.dma_start(W[:, bass.ds(half, 1), m].rearrange("p o k n -> p (o k) n"),
                             t[bass.ds(e, 1), 0].rearrange("o (k p) n -> p (o k) n", p=P)).then_inc(S["w1_in"], 16)

        def second_weights(t, e, half, name):
            sp.dma_start(W[:, bass.ds(half, 1), 1].rearrange("p o k n -> p (o k) n"),
                         t[bass.ds(e, 1), 1].rearrange("o (k p) n -> p (o k) n", p=P)).then_inc(S[name], 16)

        sp.wait_ge(S["o_pe"], NT)
        first_weights(0, 0)
        for i in range(NT):
            sp.wait_ge(S["ag_done"], i + 1)
            sp.dma_start(gt[:, :, cols(i)].rearrange("k p n -> p k n"), g_out[i % 2][:, :, :]).then_inc(gt_out[i % 2], 16)
        for t in gt_out:
            sp.wait_ge(t, 16 * NT // 2)

        def expert_loads(e, last):
            half = e & 1
            for n in range(KD * len(CHUNKS)):
                (c, w), k = CHUNKS[n // KD], n % KD
                if n == GRING:
                    wait_first(sp, "e_pe", e * NT + 1)
                    second_weights(wl, e, (e + 1) & 1, "wl2_in")
                    sp.dma_start(b2[0][:, :], bl[bass.ds(e, 1), 1, :]).then_inc(S["b2_in"], 16)
                before = (n - GRING) // KD * 2 * KD + (n - GRING) % KD
                wait_first(sp, "slab_l", e * STEPS1 + (STEPS1 + before + 1))
                sp.dma_start(graw[n % GRING][:, 0:w], gt[k, :, c:c + w]).then_inc(g_in[n % GRING], 16)
            wait_first(sp, "slab_l", e * STEPS1 + 2 * STEPS1)
            second_weights(wr, e, half, "wr2_in")
            if not last:
                wait_first(sp, "g_pe", e * NT + (NT + 2))
                first_weights(e + 1, (e + 1) & 1)

        with sp.Fori(0, GE - 1) as e:
            expert_loads(e, False)
        expert_loads(GE - 1, True)
        sp.wait_ge(S["e_done"], GE * NT + 2)
        sp.wait_ge(S["conv_done"], (GE + 1) * NT)
        for r in range(WB // RB):
            w = sh_gu[r * RB * P:(r + 1) * RB * P, :] if r < 2 else sh_dn
            sp.dma_start(raw[:, r * RB:(r + 1) * RB, :], w.rearrange("(q p) d -> p q d", p=P)).then_inc(raw_in[r], 16)
        sp.dma_start(fg_raw[:, :], ffn_gate).then_inc(S["f_small"], 16)
        sp.dma_start(fb[:, :], ffn_bias.partition_broadcast(P)).then_inc(S["f_small"], 16)
        sp.dma_start(out[0:(NT - 1) * P, :].rearrange("(t p) d -> p t d", p=P), X[:, 0:NT - 1, :]).then_inc(S["f_filled"], 16)
        sp.dma_start(out[(NT - 1) * P:N, :], X[0:LAST, NT - 1, :]).then_inc(S["f_filled"], 16)
        sp.wait_ge(S["f_xn"], NT)
        sp.wait_ge(S["f_consts"], 1)
        sp.dma_start(slots[0:NP, :].rearrange("(t p) c -> p t c", p=P), XR[:, :, :]).then_inc(S["f_shared"], 16)

        def raw_blocks(e, r):
            w = ex_gu[bass.ds(e, 1), r * RB * P:(r + 1) * RB * P, :] if r < 2 else ex_dn[bass.ds(e, 1)]
            sp.dma_start(raw[:, r * RB:(r + 1) * RB, :], w.rearrange("o (q p) d -> p (o q) d", p=P)).then_inc(raw_in[r], 16)

        sp.wait_ge(S["f_shared"], 16)
        sp.dma_start(xg[:, :], slots[0:P, :]).then_inc(S["xg_in"], 16)
        for r in range(WB // RB):
            sp.wait_ge(S["prep_pe"], (r + 1) * RB)
            raw_blocks(0, r)
        tile_no = sp.alloc_register("sp_tile")
        sp.reg_mov(tile_no, 0)

        def next_rows():
            g = sp.snap(tile_no, min_val=0, max_val=TILES - 1)
            sp.wait_ge(S["xt_tpe"], g + 1)
            sp.wait_ge(S["xg_read"], g + 1)
            sp.dma_start(xg[:, :], slots[bass.ds(g * P + P, P), :]).then_inc(S["xg_in"], 16)
            sp.reg_add(tile_no, tile_no, 1)

        sp.wait_ge(S["f_nt"], 1)
        for i in range(NT):
            if i == NT - 1:
                sp.wait_ge(S["f_placed"], 16 * NT * TOPK)
            next_rows()
            if i == 0:
                for r in range(WB // RB):
                    sp.wait_ge(S["prep_pe"], WB + (r + 1) * RB)
                    raw_blocks(1, r)
        with sp.Fori(1, NE - 1) as e:
            n = sp.value_load(nt_i[0:1, bass.ds(e, 1)], min_val=1, max_val=NT)
            next_rows()
            for r in range(WB // RB):
                sp.wait_ge(S["prep_pe"], e * WB + (WB + (r + 1) * RB))
                raw_blocks(e + 1, r)
            with sp.If(n > 1):
                with sp.Fori(1, n):
                    next_rows()
        with sp.Fori(NE - 1, NE + 1) as e:
            n = sp.value_load(nt_i[0:1, bass.ds(e, 1)], min_val=1, max_val=NT)
            with sp.Fori(0, n):
                next_rows()

    @block.gpsimd
    def _(pool):
        done = [0]

        def link(ins):
            done[0] += 1
            ins.then_inc(S["pool_chain"], 1)
            pool.wait_ge(S["pool_chain"], done[0])

        imprecise = dict(allow_small_or_imprecise_dtypes=True)
        link(pool.memset(X[96:P, NT - 1, :], 0.0))
        pool.sem_inc(S["x_in"], 1)
        pool.memset(e_raw[:, :, 0, :], N - 1)
        link(pool.memset(e_raw[:, :, 1, :], 8191))
        pool.sem_inc(S["edge_fill"], 1)
        link(pool.memset(ones_r[:, :].bitcast(F32), 1.0))
        link(pool.memset(ones_k[:, :].bitcast(F32), 1.0))
        link(pool.memset(ident[:, :], 0.0))
        link(pool.affine_select(out=ident[:, :], in_=ident[:, :], compare_op=ALU.not_equal, fill=1.0,
                                base=0, pattern=[[-1, P]], channel_multiplier=1))
        link(pool.memset(valid[:, :], 1.0))
        link(pool.affine_select(out=valid[:, :], in_=valid[:, :], compare_op=ALU.is_ge, fill=0.0,
                                base=N - 1, pattern=[[-P, NT]], channel_multiplier=-1))
        pool.iota(iota_key[:, :].rearrange("p (a w) -> p a w", a=NT), pattern=[[KEY, NT], [1, WIN]], base=0,
                  channel_multiplier=0, **imprecise)
        pool.iota(iota_low[:, :], pattern=[[1, P]], base=0, channel_multiplier=0, **imprecise)
        pool.iota(neg_win[:, :], pattern=[[-WIN, NW]], base=0, channel_multiplier=0, **imprecise)
        pool.iota(win[:, 0:1], pattern=[[0, 1]], base=0, channel_multiplier=WIN, **imprecise)
        pool.iota(win[:, 1:2], pattern=[[0, 1]], base=WIN, channel_multiplier=WIN, **imprecise)
        pool.iota(it_t[:, 0, :], pattern=[[1, ET]], base=1, channel_multiplier=0, **imprecise)
        pool.iota(it_t[:, 1, :], pattern=[[-1, ET]], base=256, channel_multiplier=0, **imprecise)
        pool.iota(io8[:, :], pattern=[[1, 8]], base=0, channel_multiplier=0, **imprecise)
        pool.memset(keyT[:, :], -10000.0)
        pool.memset(lowT[:, :], 0.0)
        link(pool.memset(ones_row[:, :], 1.0))
        pool.sem_inc(S["consts"], 1)
        for e in range(GE):
            pool.dma_start(b1_rows[e * KD:(e + 1) * KD, :],
                           bl[e, 0].rearrange("(k p) -> k p", p=P)).then_inc(S["small_in"], 16)
        pool.dma_start(gw[:, :, :], gate_w.rearrange("(k p) n -> p k n", p=P)).then_inc(S["small_in"], 16)
        pool.dma_start(gb[:, :], gate_b.partition_broadcast(P)).then_inc(S["small_in"], 16)
        pool.dma_start(bo[:, :], b_out.rearrange("(o d) -> o d", o=1)).then_inc(S["small_in"], 16)
        link(pool.memset(fill[:, :], 0.0))
        link(pool.iota(fill[:, TCOL:TCOL + 1], pattern=[[0, 1]], base=DUMP, channel_multiplier=1, **imprecise))
        pool.sem_inc(S["fill_made"], 1)
        pool.memset(lg[:, :, :], -1.0)
        pool.memset(KVB[:, :, :], 0.0)
        link(pool.memset(KSB[:, :, :], 0.0))
        pool.wait_ge(S["bounds_out"], 1)
        for h in range(HP):
            last = pool.tensor_copy(V[:, :, h, P:P + 1], valid[:, :].unsqueeze(2))
        link(last)
        pool.sem_inc(S["mix_setup"], 1)
        for i in range(NT):
            pool.wait_ge(S["xn_h"], i + 1)
            pool.tensor_tensor(XN_L[:, i, :], XN[:, i, :], XN_H[:, i, :].bitcast(F32), ALU.subtract).then_inc(S["xn_l"], 1)
        pool.sem_inc(S["e_done"], 2)
        with pool.Fori(0, GE) as e:
            for i in range(NT):
                pool.wait_ge(S["e_gated"], e * NT + i + 3)
                pool.tensor_tensor(X[:, i, :], X[:, i, :], t1[i % 2][:, :], ALU.add).then_inc(S["e_done"], 1)
        pool.wait_ge(S["e_done"], GE * NT + 2)
        pool.wait_ge(S["conv_done"], (GE + 1) * NT)
        link(pool.memset(XR[:, :, D:ROW], 0.0))
        pool.memset(XR[:, :, GCOL + TOPK:GCOL + TOPK + 1], 1.0)
        pool.iota(XR[:, :, SCOL + TOPK], pattern=[[P, NT]], base=0, channel_multiplier=1, **imprecise)
        link(pool.iota(XR[:, :, TCOL], pattern=[[P, NT]], base=0, channel_multiplier=1, **imprecise))
        pool.sem_inc(S["f_consts"], 1)
        pool.iota(io16[:, :], pattern=[[1, NE]], base=0, channel_multiplier=0, **imprecise)
        pool.iota(slot[:, :], pattern=[[0, 1]], base=0, channel_multiplier=1, **imprecise)
        pool.memset(ones2[:, :], 1.0)
        link(pool.memset(upper[:, :], 1.0))
        link(pool.affine_select(out=upper[:, :], in_=upper[:, :], compare_op=ALU.is_gt, fill=0.0,
                                base=0, pattern=[[1, P]], channel_multiplier=-1))
        for z in [w[:, 1, :, :] for w in DNW] + [h[:, :, :] for h in ht]:
            pool.memset(z.bitcast(F32), 0.0)
        pool.iota(meta[:, :, 1], pattern=[[0, 2]], base=DUMP, channel_multiplier=1, **imprecise)
        pool.memset(nt_i[:, 0:1], NT)
        link(pool.memset(meta[:, :, 0], 0.0))
        pool.sem_inc(S["f_consts"], 1)
        fills = 3 + math.ceil((TILES + 1 - NT) / 8)
        pool.wait_ge(S["f_filled"], 16 * fills)
        pool.wait_ge(S["f_shared"], 16)
        tile_no = pool.alloc_register("pool_tile")
        pool.reg_mov(tile_no, 0)

        def tile(scatter=None):
            g = pool.snap(tile_no, min_val=0, max_val=TILES - 1)
            if scatter is not None:
                r = P if scatter < NT - 1 else LAST
                for k in range(TOPK):
                    pool.indirect_dma_start(
                        out=slots, out_offset=bass.IndirectOffsetOnAxis(ap=sl_u[0:r, k, scatter:scatter + 1], axis=0),
                        in_=XR[0:r, scatter, :], in_offset=None).then_inc(S["f_placed"], 16)
            add_rows(g)
            pool.reg_add(tile_no, tile_no, 1)

        def add_rows(g):
            wait_first(pool, "y_done", g + 2)
            pool.indirect_dma_start(
                out=out, out_offset=bass.IndirectOffsetOnAxis(ap=y_tok[:, 0:1], axis=0),
                in_=y[:, :], in_offset=None, compute_op=ALU.add).then_inc(S["y_added"], 16)
            pool.wait_ge(S["y_added"], g * 16 + 16)
            pool.sem_inc(S["y_free"], 1)

        pool.sem_inc(S["y_free"], 1)
        pool.wait_ge(S["f_slots"], 1)
        for i in range(NT):
            tile(i)
        with pool.Fori(1, NE + 1) as e:
            n = pool.value_load(nt_i[0:1, bass.ds(e, 1)], min_val=1, max_val=NT)
            with pool.Fori(0, n):
                tile()
        add_rows(pool.snap(tile_no, min_val=NT + NE, max_val=TILES))

    @block.scalar
    def _(act):
        act.wait_ge(S["var_done"], 1)
        act.activation(rstd[:, 1, :], rstd[:, 0, :], ACT.Sqrt).then_inc(S["std_done"], 1)
        act.preload_act_table(ACT.Exp)
        for i in range(NT):
            act.wait_ge(S["xt_pe"], i + 1)
            act.activation(XT[:, :, cols(i)], B[i % 2][:, :].rearrange("p (k n) -> p k n", k=KD),
                           ACT.Copy).then_inc(S["xt_done"], 1)
        act.wait_ge(S["ex_max"], 1)
        act.activation(lg[:, :, 0:GE], lg[:, :, 0:GE], ACT.Exp).then_inc(S["ex_exp"], 1)
        def window_pair(p):
            for w in (2 * p, 2 * p + 1):
                act.wait_ge(S["win_pe"], w + 1)
                act.activation(AT[:, :, w * WIN:(w + 1) * WIN],
                               B[6 + w % 2][:, 0:WC].rearrange("p (a w) -> p a w", a=NT), ACT.Copy).then_inc(S["win_done"], 1)

        for n in range(12):
            c, w = CHUNKS[n // KD]
            act.wait_ge(S["q_pe"], n + 1)
            if n >= 2:
                act.wait_ge(S["q_done"], n - 1)
            act.activation(expo[n % 2][:, 0:w], B[n % 2][:, 0:w], ACT.Exp).then_inc(S["q_exp"], 1)
            if n in PAIR_AFTER_Q:
                window_pair(PAIR_AFTER_Q[n])
        for i in range(NT):
            act.wait_ge(S["k_pe"], i + 1)
            if i < 2:
                act.wait_ge(S["q_done"], 11 + i)
            else:
                act.wait_ge(S["k_done"], i - 1)
            act.activation(expo[i % 2][:, :], B[2 + i % 2][:, :], ACT.Exp).then_inc(S["k_exp"], 1)
            act.wait_ge(S["v_pe"], i + 1)
            act.activation(V[:, i, :, 0:P], B[4 + i % 2][:, :].rearrange("p (h m) -> p h m", h=HP),
                           ACT.Copy).then_inc(S["v_done"], 1)
            window_pair(PAIR_AFTER_KV[i])
        act.wait_ge(S["kv_pe"], HP)
        for n in range(12):
            c, w = CHUNKS[n // HP]
            act.wait_ge(S["at_pe"], n + 1)
            if n < 2:
                act.wait_ge(S["k_done"], NT - 1 + n)
            else:
                act.wait_ge(S["at_done"], n - 1)
            act.activation(expo[n % 2][:, 0:w], B[2 + n % 2][:, 0:w], ACT.Copy, bias=1e-6).then_inc(S["den_done"], 1)
            if n < NT:
                act.activation(XN_H[:, n, :], XN[:, n, :], ACT.Copy).then_inc(S["xn_h"], 1)
        for i in sorted(PAIR_AFTER_O):
            window_pair(PAIR_AFTER_O[i])

        act.wait_ge(S["at_ready"], 1)
        for i in range(2):
            act.activation(conv[i][:, :, :], AT[:, :, cols(i)], ACT.Copy).then_inc(S["conv_done"], 1)
        for i in range(NT):
            act.wait_ge(S["ag_inv"], i + 1)
            if i >= 2:
                act.wait_ge(S["ag_tpe"], i - 1)
            act.activation(t1[i % 2][:, :], B[4 + i % 2][:, :], ACT.Copy, scale=inv_nat[:, i:i + 1]).then_inc(S["ag_scaled"], 1)
            if i + 2 < NT:
                act.activation(conv[i % 2][:, :, :], AT[:, :, cols(i + 2)], ACT.Copy).then_inc(S["conv_done"], 1)
        act.wait_ge(S["ag_tpe"], NT)
        for t in gt_out:
            act.wait_ge(t, 16 * NT // 2)
        act.wait_ge(S["small_in"], 16 * (GE + 3))

        def h_tile(e, u):
            wait_first(act, *hs_free(e, u))
            act.activation(hs[u % 2][0][:, :, :], HT[:, :, cols(u % NT)], ACT.Copy).then_inc(S["hs_h"], 1)

        with act.Fori(0, GE) as e:
            half = act.snap(e & 1, min_val=0, max_val=1)
            other = act.snap((e + 1) & 1, min_val=0, max_val=1)

            def relu(c):
                wait_first(act, "l1_pe", e * STEPS1 + (RING + (c + 1) * 2 * KD))
                at0, w = CHUNKS[c]
                for j in range(KD):
                    act.activation(HT[:, j, at0:at0 + w], B[4 * (c % 2) + j][:, 0:w], ACT.Relu,
                                   bias=b1[:, bass.ds(e * KD + j, 1)]).then_inc(S["h_done"], 1)

            act.wait_ge(S["w1_in"], e * 32 + 32)
            act.wait_ge(S["e_pe"], e * NT + 1)
            for n in range(STEPS1):
                (c, w), k = CHUNKS[n // (2 * KD)], n % (2 * KD)
                wh, _, xh, _ = slabs[n % RING]
                wait_first(act, "l1_pe", e * STEPS1 + (n + 1))
                act.activation(wh[:, :], W[:, bass.ds(half, 1), k // KD, k % KD, :].rearrange("p o n -> p (o n)"), ACT.Copy)
                if k < KD:
                    g = n // (2 * KD) * KD + k
                    act.wait_ge(g_in[g % GRING], e * (16 * KD * len(CHUNKS) // GRING) + 16 * (g // GRING + 1))
                    source = graw[g % GRING][:, 0:w]
                else:
                    source = XT[:, k - KD, c:c + w]
                act.activation(xh[:, 0:w], source, ACT.Copy).then_inc(S["slab_h"], 1)
                if n // (2 * KD) > 0 and k == 2:
                    relu(n // (2 * KD) - 1)
                if n == STEPS1 // 2 + KD:
                    wait_first(act, "wl2_in", e * 16 + 16)
                    act.activation(WR[:, bass.ds(other, 1), 0].rearrange("p o k n -> p (o k) n"),
                                   W[:, bass.ds(other, 1), 1].rearrange("p o k n -> p (o k) n"), ACT.Copy).then_inc(S["w2_h"], 1)
                    act.wait_ge(S["b2_in"], e * 16 + 16)
                    act.activation(b2[1][:, :], b2[0][:, :], ACT.Copy).then_inc(S["w2_h"], 1)
            relu(2)
            act.wait_ge(S["h_done"], e * 12 + 12)
            h_tile(e, 0)
            for i in range(NT):
                h_tile(e, i + 1)
                act.wait_ge(S["g_pe"], e * NT + (i + 3))
                act.activation(GH[:, i, :], B[4 + i % 2][:, :], ACT.Copy).then_inc(S["g_h"], 1)
                if i < 2:
                    act.activation(conv[i][:, :, :], AT[:, :, cols(i)], ACT.Copy).then_inc(S["conv_done"], 1)
                if i == 4:
                    wait_first(act, "wr2_in", e * 16 + 16)
                    act.activation(WR[:, bass.ds(half, 1), 0].rearrange("p o k n -> p (o k) n"),
                                   W[:, bass.ds(half, 1), 1].rearrange("p o k n -> p (o k) n"), ACT.Copy).then_inc(S["w2_h"], 1)
            for i in range(NT):
                if i + 1 < NT:
                    h_tile(e, NT + i + 1)
                act.wait_ge(S["e_pe"], e * NT + i + 2)
                act.wait_ge(S["e_done"], e * NT + i + 1)
                act.activation(t1[i % 2][:, :], B[2 + i % 2][:, :], ACT.Copy,
                               scale=inv_nat[:, i:i + 1]).then_inc(S["e_scaled"], 1)
                if i + 2 < NT:
                    act.activation(conv[i % 2][:, :, :], AT[:, :, cols(i + 2)], ACT.Copy).then_inc(S["conv_done"], 1)
        act.wait_ge(S["f_var"], 1)
        act.activation(rstd[:, 1, :], rstd[:, 0, :], ACT.Sqrt).then_inc(S["f_std"], 1)
        act.preload_act_table(ACT.Sigmoid)
        for q in range(WB):
            act.wait_ge(S["prep_pe"], q + 1)
            dest = GUW[0][:, 0, :, cols(q)] if q < GU // P else DNW[0][:, 0, :, cols(q - GU // P)]
            act.activation(dest, bank4(PREP_BANKS[q % 3]), ACT.Copy).then_inc(S["prep_h"], 1)
            if 1 <= q <= NT:
                act.wait_ge(S["f_tpe"], q)
                act.activation(xft[(q - 1) % 2][:, :, :], bank4((q - 1) % 2), ACT.Copy).then_inc(S["f_tdone"], 1)
        act.wait_ge(S["xt_tpe"], 1)
        act.activation(xt[0][:, :, :], bank4(2), ACT.Copy).then_inc(S["xt_h"], 1)
        act.wait_ge(S["f_lg"], NT)
        act.activation(aff[:, :, :], B[3][:, 0:NT * NE].rearrange("p (t e) -> p t e", e=NE),
                       ACT.Sigmoid).then_inc(S["f_aff"], 1)

        def xt_high(n):
            act.wait_ge(S["xt_tpe"], n)
            act.activation(xt[0][:, :, :], bank4(2), ACT.Copy).then_inc(S["xt_h"], 1)

        act.sem_inc(S["y_done"], 1)
        tile_no = act.alloc_register("act_tile")
        act.reg_mov(tile_no, 0)

        def rows(g):
            act.wait_ge(S["dn_pe"], g + 1)
            act.wait_ge(S["meta_done"], g + 2)
            act.wait_ge(S["y_free"], g + 1)
            act.activation(y[:, :], B[5][:, :], ACT.Copy, scale=y_gate[:, 0:1]).then_inc(S["y_done"], 1)

        def tile(e, first):
            g = act.snap(tile_no, min_val=0, max_val=TILES - 1)
            par = None if e is None else (e + 1) & 1

            def blocks(*qs):
                for q in qs if first else ():
                    wait_first(act, "prep_pe", e * WB + (WB + q + 1))
                    if q < GU // P:
                        dest = GUW[0][:, bass.ds(par, 1), :, cols(q)]
                    else:
                        dest = DNW[0][:, bass.ds(par, 1), :, cols(q - GU // P)]
                    act.activation(dest.rearrange("p o k n -> p (o k) n"), bank4(PREP_BANKS[q % 3]),
                                   ACT.Copy).then_inc(S["prep_h"], 1)

            blocks(0, 1, 2)
            act.wait_ge(S["gate_pe"], g + 1)
            act.activation(sig[:, :], B[0][:, :], ACT.Sigmoid).then_inc(S["sig_done"], 1)
            blocks(3, 4, 5, 6, 7)
            xt_high(g + 2)
            rows(g)
            blocks(8)
            act.wait_ge(S["h_tpe"], g + 1)
            act.activation(ht[0][:, :, :], bank4(3), ACT.Copy).then_inc(S["ht_h"], 1)
            blocks(9, 10, 11)
            act.reg_add(tile_no, tile_no, 1)

        experts(act, tile)
        rows(act.snap(tile_no, min_val=NT + NE, max_val=TILES))

    @block.vector
    def _(dve):
        done = [0]

        def link(ins):
            done[0] += 1
            ins.then_inc(S["chain"], 1)
            dve.wait_ge(S["chain"], done[0])

        def normalise(dest, var_sem, std_sem, done_sem):
            for i in range(NT):
                last = dve.bn_stats(stats[:, i, :], X[:, i, :])
            link(last)
            for i in range(NT):
                last = dve.bn_aggr(mv[:, i, :], stats[:, i, :])
            link(last)
            link(dve.tensor_scalar(rstd[:, 0, :], mv[:, :, 1], EPS, None, ALU.add))
            dve.sem_inc(S[var_sem], 1)
            dve.wait_ge(S[std_sem], 1)
            link(dve.reciprocal(rstd[:, 2, :], rstd[:, 1, :]))
            link(dve.tensor_tensor(rstd[:, 3, :], rstd[:, 2, :], rstd[:, 2, :], ALU.mult))
            link(dve.tensor_tensor(rstd[:, 3, :], rstd[:, 3, :], rstd[:, 0, :], ALU.mult))
            link(dve.tensor_scalar(rstd[:, 3, :], rstd[:, 3, :], -0.5, 1.5, ALU.mult, ALU.add))
            link(dve.tensor_tensor(rstd[:, 3, :], rstd[:, 3, :], rstd[:, 2, :], ALU.mult))
            for i in range(NT):
                dve.tensor_scalar(dest[:, i, 0:D], X[:, i, :], mv[:, i, 0:1], rstd[:, 3, i:i + 1],
                                  ALU.subtract, ALU.mult).then_inc(S[done_sem], 1)

        dve.wait_ge(S["edge_in"], 6 * 16)
        link(dve.tensor_scalar(e_int[:, :, 0, :], e_raw[:, :, 1, :], 7, None, ALU.logical_shift_right))
        link(dve.tensor_scalar(e_int[:, :, 1, :], e_raw[:, :, 1, :], P - 1, None, ALU.bitwise_and))
        link(dve.tensor_copy(e_f[:, :, 0, :], e_raw[:, :, 0, :]))
        link(dve.tensor_copy(e_f[:, :, 1, :], e_int[:, :, 1, :]))
        link(dve.tensor_copy(e_f[:, :, 2, :], e_int[:, :, 0, :]))
        link(dve.scalar_tensor_tensor(e_f[:, :, 3, :], e_f[:, :, 2, :], float(KEY), e_f[:, :, 0, :],
                                      op0=ALU.mult, op1=ALU.add))
        link(dve.tensor_reduce(e_mm[:, :, 0], e_f[:, :, 0, :], AX.X, ALU.min))
        link(dve.tensor_reduce(e_mm[:, :, 1], e_f[:, :, 0, :], AX.X, ALU.max))
        dve.sem_inc(S["edge_keys"], 1)
        dve.wait_ge(S["x_in"], 33)
        normalise(XN, "var_done", "std_done", "xn_done")
        dve.wait_ge(S["consts"], 1)
        dve.wait_ge(S["edge_pe"], 1)
        T = B[2][:, :].rearrange("p (g k t) -> p g k t", g=2, k=2)
        dve.tensor_copy(keyT[:, 0:P], T[:, 0, 0, :])
        dve.tensor_copy(keyT[:, P:ET], T[:, 1, 0, 0:ET - P])
        dve.tensor_copy(lowT[:, 0:P], T[:, 0, 1, :])
        dve.tensor_copy(lowT[:, P:ET], T[:, 1, 1, 0:ET - P])
        link(dve.tensor_copy(ok[:, 0:2, :], B[3][0:NW, 0:2 * ET].rearrange("p (k t) -> p k t", k=2)))
        link(dve.tensor_scalar(ok[:, 2, :], ok[:, 1, :], win[:, 0:1], None, ALU.is_ge))
        link(dve.scalar_tensor_tensor(ok[:, 2, :], ok[:, 0, :], win[:, 1:2], ok[:, 2, :], op0=ALU.is_lt, op1=ALU.mult))
        link(dve.tensor_tensor(ok[:, 0, :], ok[:, 2, :], it_t[:, 0, :], ALU.mult))
        link(dve.tensor_tensor(ok[:, 1, :], ok[:, 2, :], it_t[:, 1, :], ALU.mult))
        link(dve.tensor_reduce(lohi[:, 0:2], ok[:, 0:2, :], AX.X, ALU.max))
        link(dve.tensor_scalar(lohi[:, 2:3], lohi[:, 1:2], -1.0, 256.0, ALU.mult, ALU.add))
        link(dve.tensor_scalar(lohi[:, 2:3], lohi[:, 2:3], float(ET - 1), None, ALU.min))
        link(dve.tensor_scalar(lohi[:, 3:4], lohi[:, 2:3], float(VISITS), None, ALU.add))
        link(dve.tensor_tensor(lohi[:, 4:5], lohi[:, 3:4], lohi[:, 0:1], ALU.max))
        dve.sem_inc(S["edge_bounds"], 1)
        dve.wait_ge(S["edge_pe"], 2)
        link(dve.tensor_copy(row_f[:, :], B[4][0:1, 0:3 * NW]))
        link(dve.tensor_tensor(row_d[:, :], row_f[:, 2 * NW:3 * NW], row_f[:, NW:2 * NW], ALU.subtract))
        link(dve.tensor_copy(bounds_i[:, 0:LONG], row_f[:, :]))
        link(dve.tensor_reduce(bounds_i[:, LONG:LONG + 1], row_d[:, :], AX.X, ALU.max))
        dve.sem_inc(S["bounds_out"], 1)

        dve.wait_ge(S["small_in"], 16 * (GE + 3))
        dve.wait_ge(S["lg_pe"], NT + 1)
        dve.wait_ge(S["mix_setup"], 1)
        link(dve.tensor_copy(b1[:, :], B[7][:, 0:GE * KD]))
        link(dve.tensor_tensor(lg[:, :, 0:GE], B[6][:, 0:NT * GE].rearrange("p (t e) -> p t e", e=GE),
                               gb[:, :].unsqueeze(1).to_broadcast([P, NT, GE]), ALU.add))
        link(dve.tensor_reduce(lt[:, 0, :], lg[:, :, 0:GE], AX.X, ALU.max))
        link(dve.tensor_tensor(lg[:, :, 0:GE], lg[:, :, 0:GE], lt[:, 0, :].unsqueeze(2).to_broadcast([P, NT, GE]),
                               ALU.subtract))
        dve.sem_inc(S["ex_max"], 1)
        dve.wait_ge(S["ex_exp"], 1)
        link(dve.tensor_reduce(lt[:, 1, :], lg[:, :, 0:GE], AX.X, ALU.add))
        link(dve.reciprocal(lt[:, 2, :], lt[:, 1, :]))
        link(dve.tensor_tensor(lg[:, :, 0:GE], lg[:, :, 0:GE], lt[:, 2, :].unsqueeze(2).to_broadcast([P, NT, GE]),
                               ALU.mult))
        for i in range(NT):
            last = dve.max(top8[:, i, :], lg[:, i, :])
        link(last)
        for i in range(NT):
            last = dve.max_index(idx8[:, i, :], top8[:, i, :], lg[:, i, :])
        link(last)
        link(dve.tensor_copy(idxf[:, :, :], idx8[:, :, :]))
        link(dve.tensor_tensor(eq[:, :, :, :], idxf[:, :, 0:2].unsqueeze(3).to_broadcast([P, NT, 2, GE]),
                               io8[:, 0:GE].unsqueeze(1).unsqueeze(1).to_broadcast([P, NT, 2, GE]), ALU.is_equal))
        link(dve.tensor_tensor(eq[:, :, 0, :], eq[:, :, 0, :], eq[:, :, 1, :], ALU.add))
        link(dve.tensor_tensor(coef[:, :, :], eq[:, :, 0, :], lg[:, :, 0:GE], ALU.mult))

        def feature(n, dest, e_tile, bank, exp_sem, done_sem):
            dve.wait_ge(S[exp_sem], n + 1)
            link(dve.tensor_scalar(e_tile, e_tile, 1.0, None, ALU.min))
            dve.scalar_tensor_tensor(dest, bank, 0.0, e_tile, op0=ALU.max, op1=ALU.add).then_inc(S[done_sem], 1)

        def one_hots(slot, v, tile_col, window):
            dve.tensor_scalar(low1[:, slot, v, :], iota_low[:, :], lowT[:, tile_col], None, ALU.is_equal)
            return dve.tensor_scalar(key1[:, slot, v, :], iota_key[:, :], keyT[:, tile_col],
                                     neg_win[:, window], ALU.subtract, ALU.is_equal)

        def hot_pair(p):
            for w in (2 * p, 2 * p + 1):
                lo = dve.value_load(bounds_i[0:1, w:w + 1], min_val=0, max_val=ET - 1)
                if w >= 2:
                    dve.wait_ge(S["win_pe"], w - 1)
                for v in range(VISITS):
                    one_hots(w % 2, v, bass.ds(lo + v, 1), slice(w, w + 1)).then_inc(S["hot_ready"], 1)

        hot_pair(0)
        for n in range(12):
            (c, w), j = CHUNKS[n // KD], n % KD
            feature(n, QT[:, j, c:c + w], expo[n % 2][:, 0:w], B[n % 2][:, 0:w], "q_exp", "q_done")
            if n in PAIR_AFTER_Q:
                hot_pair(PAIR_AFTER_Q[n] + 1)
        for i in range(NT):
            feature(i, K[:, i, :], expo[i % 2][:, :], B[2 + i % 2][:, :], "k_exp", "k_done")
            hot_pair(PAIR_AFTER_KV[i] + 1)
        for h in range(HP):
            dve.wait_ge(S["kv_pe"], h + 1)
            b = B[6 + h % 2]
            for r in (slice(0, 64), slice(64, P)):
                dve.tensor_copy(KVB[r, h, r], b[r, r])
                last = dve.tensor_copy(KSB[r, h, r], b[r, P:P + 1].to_broadcast([64, 64]))
            last.then_inc(S["kv_done"], 1)
        for n in range(12):
            (c, w), h = CHUNKS[n // HP], n % HP
            dve.wait_ge(S["den_done"], n + 1)
            r = expo[n % 2][:, 0:w]
            link(dve.reciprocal(r, r))
            dve.tensor_tensor(QT[:, h, c:c + w], B[n % 2][:, 0:w], r, ALU.mult).then_inc(S["at_done"], 1)
        for i in range(NT):
            dve.wait_ge(S["o_pe"], i + 1)
            dve.tensor_tensor(X[:, i, :], X[:, i, :], B[4 + i % 2][:, :], ALU.add).then_inc(S["o_done"], 1)
            if i in PAIR_AFTER_O and PAIR_AFTER_O[i] + 1 < NW // 2:
                hot_pair(PAIR_AFTER_O[i] + 1)

        dve.wait_ge(S["win_done"], NW)
        long = dve.value_load(bounds_i[0:1, LONG:LONG + 1], min_val=0, max_val=ETP)
        with dve.If(long > 0):
            more = dve.alloc_register("dve_more")
            dve.reg_mov(more, 1)
            with dve.Fori(0, NW) as w:
                at = dve.value_load(bounds_i[0:1, bass.ds(w + NW, 1)], min_val=VISITS, max_val=ETP - 1)
                end = dve.value_load(bounds_i[0:1, bass.ds(w + 2 * NW, 1)], min_val=VISITS, max_val=ETP - 1)
                with dve.If(end > at):
                    with dve.Fori(at, end) as t:
                        m = dve.snap(more, min_val=1, max_val=NW * ET)
                        one_hots(0, 0, bass.ds(t, 1), bass.ds(w, 1)).then_inc(S["lhot_ready"], 1)
                        dve.wait_ge(S["long_pe"], m)
                        part = AT[:, :, bass.ds(w * WIN, WIN)]
                        dve.tensor_tensor(part, part, B[6][:, 0:WC].rearrange("p (a w) -> p a w", a=NT), ALU.add)\
                            .then_inc(S["long_done"], 1)
                        dve.wait_ge(S["long_done"], m)
                        dve.reg_add(more, more, 1)
        dve.sem_inc(S["at_ready"], 1)

        def low_counts(n, i):
            with dve.If(long > 0):
                dve.wait_ge(S["conv_done"], n + 1)
                dve.wait_ge(S["ag_low_pe"], n + 1)
                dve.tensor_tensor(conv_low[:, :, :], AT[:, :, cols(i)], conv[i % 2][:, :, :].bitcast(F32), ALU.subtract)\
                    .then_inc(S["conv_l"], 1)

        def rows_out(i):
            dve.wait_ge(S["ag_tpe"], i + 1)
            if i >= 2:
                dve.wait_ge(gt_out[i % 2], 16 * (i // 2))
            dve.tensor_copy(g_out[i % 2][:, :, :], bank4(i % 2)).then_inc(S["ag_done"], 1)

        for i in range(NT):
            low_counts(i, i)
            dve.wait_ge(S["ag_pe"], i + 1)
            link(dve.tensor_scalar(inv_nat[:, i:i + 1], B[2 + i % 2][:, 0:1], 1.0, None, ALU.max))
            dve.reciprocal(inv_nat[:, i:i + 1], inv_nat[:, i:i + 1]).then_inc(S["ag_inv"], 1)
            if i >= 1:
                rows_out(i - 1)
        rows_out(NT - 1)

        dve.sem_inc(S["g_done"], 2)
        dve.sem_inc(S["e_gated"], 2)
        dve.sem_inc(S["slab_l"], STEPS1)

        def rest(dest, source, high):
            return dve.tensor_tensor(dest, source, high.bitcast(F32), ALU.subtract)

        def second_rest(half, n):
            dve.wait_ge(S["w2_h"], n)
            place = [t[:, bass.ds(half, 1), m].rearrange("p o k n -> p (o k) n") for t, m in ((WR, 1), (W, 1), (WR, 0))]
            rest(*place).then_inc(S["w2_l"], 1)

        def h_tile(e, u):
            dve.wait_ge(S["hs_h"], e * (2 * NT) + (u + 1))
            rest(hs[u % 2][1][:, :, :], HT[:, :, cols(u % NT)], hs[u % 2][0][:, :, :]).then_inc(S["hs_l"], 1)

        with dve.Fori(0, GE) as e:
            half = dve.snap(e & 1, min_val=0, max_val=1)
            other = dve.snap((e + 1) & 1, min_val=0, max_val=1)
            for n in range(STEPS1):
                (c, w), k = CHUNKS[n // (2 * KD)], n % (2 * KD)
                wh, wlo, xh, xlo = slabs[n % RING]
                dve.wait_ge(S["slab_h"], e * STEPS1 + (n + 1))
                rest(wlo[:, :], W[:, bass.ds(half, 1), k // KD, k % KD, :].rearrange("p o n -> p (o n)"), wh[:, :])
                source = graw[(n // (2 * KD) * KD + k) % GRING][:, 0:w] if k < KD else XT[:, k - KD, c:c + w]
                rest(xlo[:, 0:w], source, xh[:, 0:w]).then_inc(S["slab_l"], 1)
                if n == STEPS1 // 2 + KD:
                    second_rest(other, e * 3 + 1)
                    dve.wait_ge(S["w2_h"], e * 3 + 2)
                    rest(b2[2][:, :], b2[0][:, :], b2[1][:, :]).then_inc(S["w2_l"], 1)
            h_tile(e, 0)
            for i in range(NT):
                h_tile(e, i + 1)
                dve.wait_ge(S["g_h"], e * NT + i + 1)
                rest(GL[:, i, :], B[4 + i % 2][:, :], GH[:, i, :]).then_inc(S["g_done"], 1)
                if i == 4:
                    second_rest(half, e * 3 + 3)
            for i in range(NT):
                if i + 1 < NT:
                    h_tile(e, NT + i + 1)
                low_counts(e * NT + (i + NT), i)
                dve.wait_ge(S["e_scaled"], e * NT + i + 1)
                dve.tensor_tensor(t1[i % 2][:, :], t1[i % 2][:, :], B[6 + i % 2][:, :], ALU.add).then_inc(S["e_chain"], 1)
                dve.wait_ge(S["e_chain"], e * NT + i + 1)
                dve.tensor_scalar(t1[i % 2][:, :], t1[i % 2][:, :], 0.0,
                                  coef[:, i, bass.ds(e, 1)], ALU.max, ALU.mult).then_inc(S["e_gated"], 1)

        dve.wait_ge(S["e_done"], GE * NT + 2)
        normalise(XR, "f_var", "f_std", "f_xn")
        def low_part(dest_l, dest_h, bank, done_sem):
            return dve.tensor_tensor(dest_l, bank, dest_h.bitcast(F32), ALU.subtract).then_inc(S[done_sem], 1)

        dve.wait_ge(S["fgt_pe"], 1)
        dve.tensor_copy(fgT[:, :, :], B[2][:, 0:KD * NE].rearrange("p (k e) -> p k e", e=NE)).then_inc(S["fgt_done"], 1)
        for q in range(WB):
            dve.wait_ge(S["prep_h"], q + 1)
            pair = [w[:, 0, :, cols(q)] for w in GUW] if q < GU // P else [w[:, 0, :, cols(q - GU // P)] for w in DNW]
            low_part(pair[1], pair[0], bank4(PREP_BANKS[q % 3]), "prep_l")
        STEPS = 8

        def gates(n, c):
            def step(k, ins):
                ins.then_inc(S["t_chain"], 1)
                dve.wait_ge(S["t_chain"], c + k)
            dve.wait_ge(S["xg_in"], n * 16)
            step(1, dve.tensor_copy(y_gate[:, :], meta[:, 1, 0:1]))
            step(2, dve.tensor_copy(y_tok[:, :], meta[:, 1, 1:2]))
            step(3, dve.tensor_copy(meta[:, 1, :], meta[:, 0, :]))
            step(4, dve.tensor_copy(meta[:, 0, 1:2], xg[:, TCOL:TCOL + 1]))
            step(5, dve.scalar_tensor_tensor(gprod[:, :], xg[:, SCOL:SCOL + 4], slot[:, 0:1], xg[:, GCOL:GCOL + 4],
                                             op0=ALU.is_equal, op1=ALU.mult))
            step(6, dve.tensor_scalar(slot[:, :], slot[:, :], float(P), None, ALU.add))
            step(7, dve.tensor_reduce(meta[:, 0, 0:1], gprod[:, :], AX.X, ALU.add))
            dve.sem_inc(S["xg_read"], 1)
            dve.sem_inc(S["meta_done"], 1)

        dve.wait_ge(S["f_consts"], 2)
        dve.wait_ge(S["xt_h"], 1)
        low_part(xt[1][:, :, :], xt[0][:, :, :], bank4(2), "xt_l")
        gates(1, 0)
        dve.wait_ge(S["f_small"], 32)
        dve.wait_ge(S["f_aff"], 1)
        link(dve.tensor_tensor(score[:, :, :], aff[:, :, :], fb[:, :].unsqueeze(1).to_broadcast([P, NT, NE]), ALU.add))
        for i in range(NT):
            last = dve.max(f8[:, i, :], score[:, i, :])
        link(last)
        for i in range(NT):
            last = dve.max_index(f8i[:, i, :], f8[:, i, :], score[:, i, :])
        link(last)
        link(dve.tensor_copy(f8f[:, :, :], f8i[:, :, :]))
        for k in range(TOPK):
            link(dve.tensor_tensor(pick[:, k, :, :], f8f[:, :, k:k + 1].to_broadcast([P, NT, NE]),
                                   io16[:, :].unsqueeze(1).to_broadcast([P, NT, NE]), ALU.is_equal))
            link(dve.tensor_tensor(tmp16[:, :, :], pick[:, k, :, :], aff[:, :, :], ALU.mult))
            link(dve.tensor_reduce(gsel[:, k, :], tmp16[:, :, :], AX.X, ALU.add))
        link(dve.tensor_tensor(gsum[:, 0, :], gsel[:, 0, :], gsel[:, 1, :], ALU.add))
        link(dve.tensor_tensor(gsum[:, 0, :], gsum[:, 0, :], gsel[:, 2, :], ALU.add))
        link(dve.tensor_scalar(gsum[:, 0, :], gsum[:, 0, :], 1e-9, None, ALU.add))
        link(dve.reciprocal(gsum[:, 1, :], gsum[:, 0, :]))
        dve.wait_ge(S["f_shared"], 16)
        for k in range(TOPK):
            link(dve.tensor_tensor(XR[:, :, GCOL + k], gsel[:, k, :], gsum[:, 1, :], ALU.mult))
        link(dve.tensor_tensor(tmp16[:, :, :], pick[:, 0, :, :], pick[:, 1, :, :], ALU.add))
        link(dve.tensor_tensor(tmp16[:, :, :], tmp16[:, :, :], pick[:, 2, :, :], ALU.add))
        link(dve.tensor_tensor(M[:, 0:NT, :], tmp16[:, :, :], valid[:, :].unsqueeze(2).to_broadcast([P, NT, NE]), ALU.mult))
        link(dve.memset(pref[:, 0, :], 0.0))
        for i in range(1, NT):
            link(dve.tensor_tensor(pref[:, i, :], pref[:, i - 1, :], M[:, i - 1, :], ALU.add))
        link(dve.tensor_tensor(M[:, NT, :], pref[:, NT - 1, :], M[:, NT - 1, :], ALU.add))
        dve.sem_inc(S["f_sel"], 1)
        dve.wait_ge(S["f_rank"], 1)
        counts = B[5][:, NT * NE:(NT + 1) * NE]
        link(dve.tensor_scalar(cnt[:, 0, :], counts, float(P - 1), None, ALU.add))
        link(dve.tensor_copy(cnt_i[:, :], cnt[:, 0, :]))
        link(dve.tensor_scalar(cnt_i[:, :], cnt_i[:, :], 7, None, ALU.logical_shift_right))
        link(dve.tensor_copy(cnt[:, 1, :], cnt_i[:, :]))
        link(dve.tensor_scalar(cnt[:, 1, :], cnt[:, 1, :], 1.0, None, ALU.max))
        link(dve.tensor_copy(nt_i[:, 1:NE + 1], cnt[:, 1, :]))
        dve.sem_inc(S["f_nt"], 1)
        link(dve.memset(cnt[:, 2, :], 1.0))
        link(dve.tensor_tensor_scan(cnt[:, 3, :], cnt[:, 2, :], cnt[:, 1, :], float(NT), ALU.mult, ALU.add))
        link(dve.tensor_tensor(cnt[:, 4, :], cnt[:, 3, :], cnt[:, 1, :], ALU.subtract))
        link(dve.tensor_scalar(cnt[:, 4, :], cnt[:, 4, :], float(P), None, ALU.mult))
        ranks = B[5][:, 0:NT * NE].rearrange("p (t e) -> p t e", e=NE)
        link(dve.tensor_tensor(score[:, :, :], ranks, cnt[:, 4, :].unsqueeze(1).to_broadcast([P, NT, NE]), ALU.add))
        for k in range(TOPK):
            link(dve.tensor_tensor(tmp16[:, :, :], score[:, :, :], pick[:, k, :, :], ALU.mult))
            link(dve.tensor_reduce(sl[:, k, :], tmp16[:, :, :], AX.X, ALU.add))
            link(dve.tensor_copy(XR[:, :, SCOL + k], sl[:, k, :]))
        link(dve.tensor_copy(sl_u[:, :, :], sl[:, :, :]))
        dve.sem_inc(S["f_slots"], 1)

        dve.sem_inc(S["ht_l"], 1)
        tile_no = dve.alloc_register("dve_tile")
        dve.reg_mov(tile_no, 0)

        def tile(e, first):
            g = dve.snap(tile_no, min_val=0, max_val=TILES - 1)
            par = None if e is None else (e + 1) & 1

            def blocks(*qs):
                for q in qs if first else ():
                    dve.wait_ge(S["prep_h"], e * WB + (WB + q + 1))
                    ws, qq = (GUW, q) if q < GU // P else (DNW, q - GU // P)
                    pair = [w[:, bass.ds(par, 1), :, cols(qq)].rearrange("p o k n -> p (o k) n") for w in ws]
                    low_part(pair[1], pair[0], bank4(PREP_BANKS[q % 3]), "prep_l")

            blocks(0, 1, 2)
            dve.wait_ge(S["sig_done"], g + 1)
            dve.tensor_tensor(ug[:, :], sig[:, :], B[0][:, :], ALU.mult).then_inc(S["t_chain"], 1)
            blocks(3, 4, 5, 6)
            dve.wait_ge(S["t_chain"], g * STEPS + STEPS)
            dve.wait_ge(S["up_pe"], g + 1)
            dve.tensor_tensor(hid[:, :], ug[:, :], B[1][:, :], ALU.mult).then_inc(S["hid_done"], 1)
            blocks(7)
            dve.wait_ge(S["xt_h"], g + 2)
            low_part(xt[1][:, :, :], xt[0][:, :, :], bank4(2), "xt_l")
            dve.wait_ge(S["y_free"], g + 1)
            dve.wait_ge(S["y_done"], g + 1)
            gates(g + 2, g * STEPS + STEPS)
            blocks(8)
            dve.wait_ge(S["ht_h"], g + 1)
            low_part(ht[1][:, :, :], ht[0][:, :, :], bank4(3), "ht_l")
            blocks(9, 10, 11)
            dve.reg_add(tile_no, tile_no, 1)

        experts(dve, tile)
        g = dve.snap(tile_no, min_val=NT + NE, max_val=TILES)
        dve.wait_ge(S["y_free"], g + 1)
        gates(g + 1, g * STEPS + STEPS - 1)

    @block.tensor
    def _(pe):
        def product(bank, pairs, start=True, stop=True):
            todo = []
            for a, b in pairs:
                if isinstance(a, tuple):
                    todo += [(a[0], b[0]), (a[0], b[1]), (a[1], b[0])]
                else:
                    todo.append((a, b))
            for n, (a, b) in enumerate(todo):
                last = pe.matmul(bank, a, b, start=start and n == 0, stop=stop and n == len(todo) - 1)
            return last

        pe.wait_ge(S["edge_keys"], 1)
        pe.wait_ge(S["consts"], 1)
        T = B[2][:, :].rearrange("p (g k t) -> p g k t", g=2, k=2)
        for g, n in ((0, P), (1, ET - P)):
            pe.transpose(T[:, g, 0, 0:n], e_f[0:n, g, 3, :], ident[0:n, 0:n])
            pe.transpose(T[:, g, 1, 0:n], e_f[0:n, g, 1, :], ident[0:n, 0:n])
            for k in range(2):
                c = k * ET + g * P
                last = pe.matmul(B[3][0:NW, c:c + n], e_mm[0:n, g, k:k + 1].to_broadcast([n, NW]), ident[0:n, 0:n],
                                 start=True, stop=True)
        last.then_inc(S["edge_pe"], 1)
        for i in range(NT):
            pe.wait_ge(S["xn_done"], i + 1)
            if i >= 2:
                pe.wait_ge(S["xt_done"], i - 1)
            for k in range(KD):
                last = pe.transpose(B[i % 2][:, cols(k)], XN[:, i, cols(k)], ident[:, :])
            last.then_inc(S["xt_pe"], 1)
        pe.wait_ge(S["edge_bounds"], 1)
        for k in range(3):
            last = pe.matmul(B[4][0:1, k * NW:(k + 1) * NW], lohi[:, 2 + k:3 + k], ident[0:NW, 0:NW], start=True, stop=True)
        last.then_inc(S["edge_pe"], 1)
        pe.wait_ge(S["xt_done"], NT)
        pe.wait_ge(S["small_in"], 16 * (GE + 3))
        for i in range(NT):
            product(B[6][:, i * GE:(i + 1) * GE], [(XT[:, k, cols(i)], gw[:, k, :]) for k in range(KD)])\
                .then_inc(S["lg_pe"], 1)
        pe.transpose(B[7][:, 0:GE * KD], b1_rows[:, :], ident[0:GE * KD, 0:GE * KD]).then_inc(S["lg_pe"], 1)
        def window_pair(p):
            for w in (2 * p, 2 * p + 1):
                lo_h, b = w % 2, B[6 + w % 2][:, 0:WC]
                if w >= 2:
                    pe.wait_ge(S["win_done"], w - 1)
                for v in range(VISITS):
                    pe.wait_ge(S["hot_ready"], w * VISITS + v + 1)
                    last = pe.matmul(b, low1[:, lo_h, v, :], key1[:, lo_h, v, :], start=v == 0, stop=v == VISITS - 1)
                last.then_inc(S["win_pe"], 1)

        pe.wait_ge(S["wqkv_in"], 16)
        for n in range(12):
            (c, w), j = CHUNKS[n // KD], n % KD
            if n >= 2:
                pe.wait_ge(S["q_done"], n - 1)
            product(B[n % 2][:, 0:w], [(WQKV[:, k, cols(j)], XT[:, k, c:c + w]) for k in range(KD)])\
                .then_inc(S["q_pe"], 1)
            if n == 0:
                pe.wait_ge(S["ex_max"], 1)
            if n in PAIR_AFTER_Q:
                window_pair(PAIR_AFTER_Q[n])
        pe.wait_ge(S["bounds_out"], 1)
        for i in range(NT):
            if i >= 2:
                pe.wait_ge(S["k_done"], i - 1)
            product(B[2 + i % 2][:, :], [(XT[:, k, cols(i)], WQKV[:, k, D:2 * D]) for k in range(KD)])\
                .then_inc(S["k_pe"], 1)
            if i >= 2:
                pe.wait_ge(S["v_done"], i - 1)
            product(B[4 + i % 2][:, :], [(XT[:, k, cols(i)], WQKV[:, k, 2 * D:3 * D]) for k in range(KD)])\
                .then_inc(S["v_pe"], 1)
            window_pair(PAIR_AFTER_KV[i])
        pe.wait_ge(S["k_done"], NT)
        pe.wait_ge(S["v_done"], NT)
        pe.wait_ge(S["mix_setup"], 1)
        pe.wait_ge(S["win_done"], 2 * (PAIR_AFTER_KV[NT - 1] + 1))
        for h in range(HP):
            if h >= 2:
                pe.wait_ge(S["kv_done"], h - 1)
            product(B[6 + h % 2][:, 0:P + 1], [(K[:, i, cols(h)], V[:, i, h, 0:P + 1]) for i in range(NT)])\
                .then_inc(S["kv_pe"], 1)
        pe.wait_ge(S["kv_done"], HP)
        for n in range(12):
            (c, w), h = CHUNKS[n // HP], n % HP
            if n >= 2:
                pe.wait_ge(S["at_done"], n - 1)
            product(B[n % 2][:, 0:w], [(KVB[:, h, :], QT[:, h, c:c + w])])
            product(B[2 + n % 2][:, 0:w], [(KSB[:, h, :], QT[:, h, c:c + w])]).then_inc(S["at_pe"], 1)
        pe.wait_ge(S["at_done"], 12)
        pe.wait_ge(S["wqkv_in"], 32)
        for i in range(NT):
            if i >= 2:
                pe.wait_ge(S["o_done"], i - 1)
            product(B[4 + i % 2][:, :], [(QT[:, h, cols(i)], WO[:, h, :]) for h in range(HP)]
                    + [(ones_row[:, :], bo[:, :])]).then_inc(S["o_pe"], 1)
            if i in PAIR_AFTER_O:
                window_pair(PAIR_AFTER_O[i])

        long = pe.value_load(bounds_i[0:1, LONG:LONG + 1], min_val=0, max_val=ETP)
        with pe.If(long > 0):
            more = pe.alloc_register("pe_more")
            pe.reg_mov(more, 1)
            with pe.Fori(0, NW) as w:
                at = pe.value_load(bounds_i[0:1, bass.ds(w + NW, 1)], min_val=VISITS, max_val=ETP - 1)
                end = pe.value_load(bounds_i[0:1, bass.ds(w + 2 * NW, 1)], min_val=VISITS, max_val=ETP - 1)
                with pe.If(end > at):
                    with pe.Fori(at, end):
                        pe.wait_ge(S["lhot_ready"], pe.snap(more, min_val=1, max_val=NW * ET))
                        pe.matmul(B[6][:, 0:WC], low1[:, 0, 0, :], key1[:, 0, 0, :], start=True, stop=True)\
                            .then_inc(S["long_pe"], 1)
                        pe.reg_add(more, more, 1)

        def aggregate(n, i, bank, high, low, ones=None):
            def products(counts, parts, a, stop):
                for part in parts:
                    last = pe.matmul(bank, counts[:, a, :], part[:, a, :], start=False if started else True,
                                     stop=stop and part is parts[-1], skip_group_check=True)
                    started.append(1)
                return last
            started = []
            pe.wait_ge(S["conv_done"], n + 1)
            for a in range(NT - 1):
                products(conv[i % 2], (high, low), a, False)
            with pe.If(long > 0):
                pe.wait_ge(S["conv_l"], n + 1)
                for a in range(NT):
                    last = products(conv_low, (high,), a, False)
                if ones is None:
                    last.then_inc(S["ag_low_pe"], 1)
            if ones is not None:
                for a in range(NT):
                    pe.matmul(ones, conv[i % 2][:, a, :], ones_r[:, :], start=a == 0, stop=False, skip_group_check=True)
                with pe.If(long > 0):
                    for a in range(NT):
                        last = pe.matmul(ones, conv_low[:, a, :], ones_r[:, :], start=False, stop=False,
                                         skip_group_check=True)
                    last.then_inc(S["ag_low_pe"], 1)
            return products(conv[i % 2], (high, low), NT - 1, True)

        def transpose_rows_out(i):
            pe.wait_ge(S["ag_scaled"], i + 1)
            if i >= 2:
                pe.wait_ge(S["ag_done"], i - 1)
            for k in range(KD):
                last = pe.transpose(B[i % 2][:, cols(k)], t1[i % 2][:, cols(k)], ident[:, :])
            last.then_inc(S["ag_tpe"], 1)

        pe.wait_ge(S["xn_l"], NT)
        pe.sem_inc(S["ag_low_pe"], 1)
        for i in range(NT):
            if i < 2:
                pe.wait_ge(S["o_done"], NT - 1 + i)
            else:
                pe.wait_ge(S["ag_scaled"], i - 1)
            aggregate(i, i, B[4 + i % 2][:, :], XN_H, XN_L, ones=B[2 + i % 2][:, 0:2]).then_inc(S["ag_pe"], 1)
            if i >= 1:
                transpose_rows_out(i - 1)
        transpose_rows_out(NT - 1)

        def parts(a, b):
            return (a[0], b[0]), (a[0], b[1]), (a[1], b[0])

        pe.wait_ge(S["ag_done"], NT)
        pe.sem_inc(S["l1_pe"], RING)
        pe.sem_inc(S["g_pe"], 2)
        pe.sem_inc(S["e_pe"], 1)
        with pe.Fori(0, GE) as e:
            half = pe.snap(e & 1, min_val=0, max_val=1)
            other = pe.snap((e + 1) & 1, min_val=0, max_val=1)
            pe.wait_ge(S["e_gated"], e * NT + 2)
            for n in range(STEPS1):
                chunk, k = n // (2 * KD), n % (2 * KD)
                c, w = CHUNKS[chunk]
                whi, wlo, xhi, xlo = slabs[n % RING]
                if chunk == 2 and k == 0:
                    pe.wait_ge(S["h_done"], e * 12 + 4)
                pe.wait_ge(S["slab_l"], e * STEPS1 + (STEPS1 + n + 1))
                for j in range(KD):
                    for m, (a, b) in enumerate(parts((whi[:, cols(j)], wlo[:, cols(j)]), (xhi[:, 0:w], xlo[:, 0:w]))):
                        last = pe.matmul(B[4 * (chunk % 2) + j][:, 0:w], a, b, start=k == 0 and m == 0,
                                         stop=k == 2 * KD - 1 and m == 2)
                last.then_inc(S["l1_pe"], 1)

            def with_weights(bank, u, which, stop):
                pe.wait_ge(S["hs_l"], e * (2 * NT) + (u + 1))
                for k in range(KD):
                    rows = [t[:, k, :] for t in hs[u % 2]]
                    weights = [WR[:, bass.ds(which, 1), m, k, :].rearrange("p o n -> p (o n)") for m in range(2)]
                    for m, (a, b) in enumerate(parts(rows, weights)):
                        last = pe.matmul(bank, a, b, start=k == 0 and m == 0, stop=stop and k == KD - 1 and m == 2)
                return last

            pe.wait_ge(S["h_done"], e * 12 + 8)
            pe.wait_ge(S["w2_l"], e * 3 + 1)
            for i in range(NT):
                pe.wait_ge(S["g_done"], e * NT + i + 1)
                with_weights(B[4 + i % 2][:, :], i, other, True).then_inc(S["g_pe"], 1)
            pe.wait_ge(S["g_done"], e * NT + NT + 2)
            pe.wait_ge(S["w2_l"], e * 3 + 3)
            for i in range(NT):
                pe.wait_ge(S["e_gated"], e * NT + i + 1)
                with_weights(B[6 + i % 2][:, :], NT + i, half, False)
                for m in range(2):
                    pe.matmul(B[6 + i % 2][:, :], ones_k[:, :], b2[1 + m][:, :], start=False, stop=m == 1)
                aggregate(e * NT + (i + NT), i, B[2 + i % 2][:, :], GH, GL).then_inc(S["e_pe"], 1)

        pe.wait_ge(S["e_gated"], GE * NT + 2)
        pe.wait_ge(S["f_small"], 32)
        for k in range(KD):
            last = pe.transpose(B[2][:, k * NE:(k + 1) * NE], fg_raw[:, cols(k)], ident[0:NE, 0:NE])
        last.then_inc(S["fgt_pe"], 1)
        pe.wait_ge(S["f_xn"], NT)
        pe.wait_ge(S["fgt_done"], 1)
        def weight_block(q):
            for k in range(KD):
                last = pe.transpose(B[PREP_BANKS[q % 3]][:, cols(k)], raw[:, q, cols(k)], ident[:, :])
            last.then_inc(S["prep_pe"], 1)

        def logits(i):
            pe.wait_ge(S["f_tdone"], i + 1)
            product(B[3][:, i * NE:(i + 1) * NE], [(xft[i % 2][:, k, :], fgT[:, k, :]) for k in range(KD)])\
                .then_inc(S["f_lg"], 1)

        for q in range(WB):
            if q % RB == 0:
                pe.wait_ge(raw_in[q // RB], 16)
            if q >= 3:
                pe.wait_ge(S["prep_l"], q - 2)
            weight_block(q)
            if q < NT:
                for k in range(KD):
                    last = pe.transpose(B[q % 2][:, cols(k)], XR[:, q, cols(k)], ident[:, :])
                last.then_inc(S["f_tpe"], 1)
            if 1 <= q <= NT:
                logits(q - 1)

        def transpose_rows(n):
            pe.wait_ge(S["xg_in"], n * 16)
            for k in range(KD):
                last = pe.transpose(B[2][:, cols(k)], xg[:, cols(k)], ident[:, :])
            last.then_inc(S["xt_tpe"], 1)

        transpose_rows(1)
        pe.wait_ge(S["f_sel"], 1)
        product(B[5][:, 0:NT * NE], [(upper[:, :], M[:, 0:NT, :].rearrange("p t e -> p (t e)")),
                                     (ones2[:, :], pref[:, :, :].rearrange("p t e -> p (t e)"))])
        product(B[5][:, NT * NE:(NT + 1) * NE], [(ones2[:, :], M[:, NT, :])]).then_inc(S["f_rank"], 1)
        tile_no = pe.alloc_register("pe_tile")
        pe.reg_mov(tile_no, 0)
        previous = pe.alloc_register("pe_previous")
        pe.reg_mov(previous, 1)

        def split_product(bank, rows, weights, after):
            for k in range(KD):
                for n, (a, b) in enumerate(((0, 0), (0, 1), (1, 0))):
                    last = pe.matmul(bank, rows[a][:, k, :], weights[b](k), start=k == 0 and n == 0,
                                     stop=k == KD - 1 and n == 2)
                if k < KD - 1:
                    after(k)
            return last

        def down(g, after=lambda k: None):
            pe.wait_ge(S["ht_l"], g + 1)
            pe.wait_ge(S["y_done"], g + 1)
            par = pe.snap(previous, min_val=0, max_val=1)
            split_product(B[5][:, :], ht, [lambda k, w=w: w[:, bass.ds(par, 1), k, :].rearrange("p o n -> p (o n)")
                                           for w in DNW], after).then_inc(S["dn_pe"], 1)
            after(KD - 1)

        def tile(e, first):
            g = pe.snap(tile_no, min_val=0, max_val=TILES - 1)
            ee = NE if e is None else e
            par = ee & 1

            def block(q):
                if first:
                    if q % RB == 0:
                        pe.wait_ge(raw_in[q // RB], e * 16 + 32)
                    pe.wait_ge(S["prep_l"], e * WB + (WB + q - 2))
                    weight_block(q)

            pe.wait_ge(S["xt_l"], g + 1)
            for half, done in ((0, "gate_pe"), (1, "up_pe")):
                split_product(B[half][:, :], xt,
                              [lambda k, w=w: w[:, bass.ds(par, 1), k, half * FF:(half + 1) * FF]
                               .rearrange("p o n -> p (o n)") for w in GUW],
                              lambda k: block(half * KD + k)).then_inc(S[done], 1)
                block(half * KD + KD - 1)
            transpose_rows(g + 2)
            down(g, lambda k: block(2 * KD + k) if k < KD - 1 else None)
            pe.reg_mov(previous, par)
            pe.wait_ge(S["hid_done"], g + 1)
            for k in range(KD):
                last = pe.transpose(B[3][:, cols(k)], hid[:, cols(k)], ident[:, :])
            last.then_inc(S["h_tpe"], 1)
            block(WB - 1)
            pe.reg_add(tile_no, tile_no, 1)

        pe.wait_ge(S["prep_l"], WB)
        experts(pe, tile)
        down(pe.snap(tile_no, min_val=NT + NE, max_val=TILES))

    ctx.close()


_INS = ["x", "src", "dst", "L0_gnn_gate_W", "L0_gnn_gate_b", "L0_gnn_Wl", "L0_gnn_bl", "L0_gnn_Wr",
        "L0_mix_w_qkv", "L0_mix_w_out", "L0_mix_b_out", "L0_ffn_gate_w", "L0_ffn_expert_bias",
        "L0_ffn_shared_gate_up", "L0_ffn_shared_down", "L0_ffn_expert_gate_up", "L0_ffn_expert_down"]


def kernel(**inputs):
    import numpy as np
    import concourse.bacc as bacc
    from concourse.bass_utils import run_bass_kernel_spmd

    nc = bacc.Bacc("TRN2", target_bir_lowering=False, num_devices=1)
    arrays, args = {}, []
    for name in _INS:
        a = np.ascontiguousarray(inputs[name])
        arrays[f"in_{name}"] = a
        args.append(nc.dram_tensor(f"in_{name}", a.shape, mybir.dt.from_np(a.dtype), kind="ExternalInput").ap())
    args.append(nc.dram_tensor("out_rows", (N + P, D), F32, kind="ExternalOutput").ap())
    program(nc, *args)
    r = run_bass_kernel_spmd(nc, [arrays], core_ids=[0])
    return r.results[0]["out_rows"][0:N]
```

```python
import math
from contextlib import ExitStack

import concourse.bass as bass
from concourse import mybir
from concourse.alu_op_type import AluOpType as ALU

F32, F32R, BF16 = mybir.dt.float32, mybir.dt.float32r, mybir.dt.bfloat16
I16, I32, U32 = mybir.dt.int16, mybir.dt.int32, mybir.dt.uint32
ACT = mybir.ActivationFunctionType
AX = mybir.AxisListType

P = 128
N, D, E = 1250, 512, 21250
NT = math.ceil(N / P)
NP = NT * P
LAST = N - (NT - 1) * P
KD = D // P
CHUNKS = [(0, 428), (428, 426), (854, 426)]
HCHUNKS = [(0, 418), (418, 416), (834, 416)]
EPS = 1e-5
X_TILES = 3
CW = CHUNKS[0][1]
STEPS1 = len(CHUNKS) * 2 * KD
RING = 4
GRING = 3
SLAB = (("WH", D), ("WL", D), ("XH", CW), ("XL", CW))

ET = math.ceil(E / P)
EFULL = E // P
ETAIL = E - EFULL * P
WIN = 32
NW = NP // WIN
VISITS = 6
LONG = 3 * NW
ETP = ET + VISITS
KEY = NP + WIN
WC = NT * WIN

PAIR_AFTER_Q = {2 * p + 1: p for p in range(6)}
PAIR_AFTER_KV = {i: 6 + i for i in range(NT)}
PAIR_AFTER_O = {2 * q + 1: 16 + q for q in range(4)}

GE = 4
HP = 4
VW = 130

NE, TOPK, FF = 16, 3, 512
GU = 2 * FF
ROUTED = (TOPK * N + NE * P) // P
TILES = NT + ROUTED
ROW = 528
GCOL, SCOL, TCOL = D, D + 4, D + 8
WB = GU // P + D // P
RB = 4
PREP_BANKS = (3, 4, 6, 7)
PRING = len(PREP_BANKS)
SHARED_APART = 3
DUMP = N


def program(nc, x, src, dst, gate_w, gate_b, wl, bl, wr, w_qkv, w_out, b_out, ffn_gate, ffn_bias,
            sh_gu, sh_dn, ex_gu, ex_dn, out):
    ctx = ExitStack()
    base = (nc.sbuf_base + 63) // 64 * 64

    def at(name, shape, dtype, offset):
        return nc.alloc_sbuf_tensor_at(name, shape, dtype, offset=base + offset)

    size = {F32: 4, F32R: 4, BF16: 2, I16: 2, I32: 4, U32: 4}
    place = [0]

    def here(name, shape, dtype):
        n = size[dtype]
        for s in shape[1:]:
            n *= s
        t = at(name, shape, dtype, place[0])
        place[0] += (n + 31) // 32 * 32
        assert base + place[0] <= nc.sbuf_usable_end, (name, place[0])
        return t

    ident = here("ident", [P, P], F32)
    valid = here("valid", [P, NT], F32)
    coef = here("coef", [P, NT, GE], F32)
    inv_nat = here("inv_nat", [P, NT], F32)
    stats = here("stats", [P, NT, 6], F32)
    mv = here("mv", [P, NT, 2], F32)
    rstd = here("rstd", [P, 4, NT], F32)
    b1 = here("b1", [P, GE * KD], F32)
    bounds_i = here("bounds_i", [1, 3 * NW + 1], I32)
    ones_r = here("ones_r", [P, 2], F32R)
    fill = here("fill", [P, ROW], F32)
    place[0] = X0 = (place[0] + 255) // 256 * 256
    X = here("X", [P, NT, D], F32)
    XN = here("XN", [P, NT, D], F32)
    XT = here("XT", [P, KD, NP], F32)
    AT = here("AT", [P, NT, NP], I16)
    R0 = place[0]
    XN_L = at("XN_L", [P, NT, D], F32R, X0 + NT * D * 4)

    K = here("K", [P, NT, D], F32)
    V0 = place[0]
    V = here("V", [P, NT, HP, VW], F32)
    QT = here("QT", [P, KD, NP], F32)
    W0 = place[0]
    WQKV = here("WQKV", [P, KD, 3 * D], F32)
    WO = [at(f"WO{s}", [P, KD, D], t, W0 + m * KD * D * 4)
          for s, t, m in (("", F32, 1), ("H", F32R, 0), ("L", F32R, 1))]
    QH = at("QH", [P, KD, NP], F32R, V0)
    QL = at("QL", [P, KD, NP], F32R, W0 - KD * NP * 4)
    expo = [here(f"expo{i}", [P, 512], F32) for i in range(3)]
    KVB = here("KVB", [P, HP, P], F32)
    KS = here("KS", [P, HP, 2 * HP], F32)
    heads = here("heads", [2 * HP, HP, P], F32)
    den = here("den", [2 * HP, NP], F32)
    bo = here("bo", [P, D], F32)
    gw = here("gw", [P, KD, GE], F32)
    b1_rows = here("b1_rows", [GE * KD, P], F32)
    gb = here("gb", [P, GE], F32)
    lg = here("lg", [P, NT, 8], F32)
    lt = here("lt", [P, 4, NT], F32)
    top8 = here("top8", [P, NT, 8], F32)
    idx8 = here("idx8", [P, NT, 8], U32)
    idxf = here("idxf", [P, NT, 8], F32)
    io8 = here("io8", [P, 8], F32)
    eq = here("eq", [P, NT, 2, GE], F32)
    keyT = here("keyT", [P, ETP], F32)
    lowT = here("lowT", [P, ETP], F32)
    iota_key = here("iota_key", [P, WC], I16)
    iota_low = here("iota_low", [P, P], I16)
    neg_win = here("neg_win", [P, NW], F32)
    low1 = here("low1", [P, 2, VISITS, P], BF16)
    key1 = here("key1", [P, 2, VISITS, WC], BF16)
    place[0] = R0
    e_raw = here("e_raw", [P, 2, 2, P], I32)
    e_int = here("e_int", [P, 2, 2, P], I32)
    e_f = here("e_f", [P, 2, 4, P], F32)
    e_mm = here("e_mm", [P, 2, 2], F32)
    win = here("win", [NW, 2], F32)
    ok = here("ok", [NW, 3, ET], F32)
    it_t = here("it_t", [NW, 2, ET], F32)
    lohi = here("lohi", [NW, 5], F32)
    row_f = here("row_f", [1, 3 * NW], F32)
    row_d = here("row_d", [1, NW], F32)

    place[0] = R0
    XN_H = at("XN_H", [P, NT, D], F32R, place[0])
    HT = here("HT", [P, KD, NP], F32)
    GH = here("GH", [P, NT, D], F32R)
    GL = at("GL", [P, NT, D], F32R, X0 + NT * D * 4)
    W = at("W", [P, 2, 2, KD, D], F32, place[0])
    WR = here("WR", [P, 2, 2, KD, D], F32R)
    b2 = here("b2", [P, D], F32)
    t1 = [here(f"t1_{i}", [P, D], F32) for i in range(2)]
    conv0 = place[0]
    conv = [here(f"conv{i}", [P, NT, P], F32R) for i in range(2)]
    conv_low = here("conv_low", [P, NT, P], F32R)
    graw0 = place[0]
    graw = [here(f"graw{i}", [P, CW], F32) for i in range(GRING)]
    slabs0 = place[0]
    place[0] = conv0
    slabs = [None, None] + [[here(f"slab{s}{i}", [P, n], F32R) for s, n in SLAB] for i in (2, 3)]
    assert place[0] <= slabs0 - GRING * CW * 4 and slabs0 + 2 * (2 * D + 2 * CW) * 4 <= nc.sbuf_usable_end - base
    place[0] = slabs0
    slabs[0:2] = [[here(f"slab{s}{i}", [P, n], F32R) for s, n in SLAB] for i in (0, 1)]
    place[0] = slabs0
    hs = [[here(f"hs{s}{i}", [P, KD, P], F32R) for s in "HL"] for i in range(2)]
    place[0] = graw0
    g_out = [here(f"g_out{i}", [P, KD, P], F32) for i in range(2)]

    place[0] = X0 + NT * D * 4
    GUW = [here(f"GUW{s}", [P, 2, KD, GU], F32R) for s in "HL"]
    DNW = [here(f"DNW{s}", [P, 2, KD, D], F32R) for s in "HL"]
    raw = here("raw", [P, WB, D], F32)
    xg = here("xg", [P, ROW], F32)
    xt = [here(f"xt{s}", [P, KD, P], F32R) for s in "HL"]
    ht = [here(f"ht{s}", [P, KD, P], F32R) for s in "HL"]
    sig = here("sig", [P, FF], F32)
    ug = here("ug", [P, FF], F32)
    hid = here("hid", [P, FF], F32)
    y = here("y", [P, D], F32)
    meta = here("meta", [P, 2, 2], F32)
    y_gate = here("y_gate", [P, 1], F32)
    y_tok = here("y_tok", [P, 1], U32)
    slot = here("slot", [P, 1], F32)
    gprod = here("gprod", [P, 4], F32)
    nt_i = here("nt_i", [P, NE + 1], I32)
    F0 = place[0]
    XR = here("XR", [P, NT, ROW], F32)
    xft = [here(f"xft{i}", [P, KD, P], F32) for i in range(2)]
    fg_raw = here("fg_raw", [NE, D], F32)
    fgT = here("fgT", [P, KD, NE], F32)
    lgT = here("lgT", [NE, NP], F32)
    fb = here("fb", [P, NE], F32)
    aff = here("aff", [P, NT, NE], F32)
    score = here("score", [P, NT, NE], F32)
    f8 = here("f8", [P, NT, 8], F32)
    f8i = here("f8i", [P, NT, 8], U32)
    f8f = here("f8f", [P, NT, 8], F32)
    io16 = here("io16", [P, NE], F32)
    pick = here("pick", [P, TOPK, NT, NE], F32)
    M = here("M", [P, NT + 1, NE], F32)
    pref = here("pref", [P, NT, NE], F32)
    tmp16 = here("tmp16", [P, NT, NE], F32)
    gsel = here("gsel", [P, TOPK, NT], F32)
    gsum = here("gsum", [P, 2, NT], F32)
    sl = here("sl", [P, TOPK, NT], F32)
    sl_u = here("sl_u", [P, TOPK, NT], U32)
    cnt = here("cnt", [P, 6, NE], F32)
    cnt_i = here("cnt_i", [P, NE], I32)
    upper = here("upper", [P, P], F32)
    ones2 = here("ones2", [P, P], F32)

    B = [ctx.enter_context(nc.psum_tensor(f"B{i}", [P, 512], F32)) for i in range(8)]

    gt = nc.dram_tensor("gt", [KD, P, NP], F32, kind="Internal").ap()
    slots = nc.dram_tensor("slots", [(TILES + 1) * P, ROW], F32, kind="Internal").ap()

    def sem(name):
        return ctx.enter_context(nc.semaphore(name))

    ready = {n: sem(n) for n in (
        "x_zero", "edge_fill", "edge_in", "wqkv_in", "small_in", "consts", "chain", "pool_chain",
        "edge_keys", "edge_pe", "edge_bounds", "bounds_out", "xn_done", "var_done", "std_done",
        "xt_pe", "xt_done", "lg_pe", "ex_max", "ex_exp",
        "q_pe", "q_exp", "q_done", "k_pe", "k_exp", "k_done", "v_pe", "v_done", "kv_pe", "kv_done",
        "at_pe", "den_pe", "den_done", "at_factor", "at_whole", "at_h", "at_done", "wo_h", "wo_l", "o_pe", "o_done", "mix_setup",
        "hot_ready", "lhot_ready", "long_pe", "long_done", "at_ready", "win_pe", "win_done",
        "bias_added", "xn_h", "xn_l", "conv_done", "conv_l", "ag_low_pe", "ag_pe", "ag_inv", "ag_scaled", "ag_tpe", "ag_done",
        "w1_in", "wl2_in", "wr2_in", "b2_in", "slab_h", "slab_l", "l1_pe", "w2_h", "w2_l",
        "hs_h", "hs_l", "h_zero", "h_done", "g_pe", "own_pe", "g_h", "g_done", "e_pe", "e_scaled", "e_gated", "e_done", "e_chain", "stats_done",
        "f_var", "f_std", "f_xn", "f_tpe", "f_tdone", "f_lg", "f_lgdone", "f_lgt", "f_aff", "f_sel", "f_rank", "f_slots",
        "fill_made", "f_consts", "f_filled", "f_small", "f_placed", "f_shared", "fgt_pe", "fgt_done",
        "prep_pe", "prep_h", "prep_l", "xg_in", "xt_tpe", "xt_h", "xt_l", "gate_pe", "up_pe",
        "sig_done", "hid_done", "h_tpe", "ht_h", "ht_l", "dn_pe", "y_done", "y_added", "y_free", "meta_done",
        "t_chain", "xg_read", "waited",
    )}
    x_in = [sem(f"x_in{i}") for i in range(NT // X_TILES + 1)]
    gt_out = [sem(f"gt_out{i}") for i in range(2)]
    g_in = [sem(f"g_in{i}") for i in range(GRING)]
    raw_in = [sem(f"raw_in{i}") for i in range(WB // RB)]
    S = ready

    block = ctx.enter_context(nc.Block())

    def cols(n):
        return slice(n * P, (n + 1) * P)

    def wait_first(eng, name, value):
        eng.wait_ge(S[name], value)
        eng.sem_inc(S["waited"], 1)

    def hs_free(e, u):
        if u < 2:
            return "l1_pe", e * STEPS1 + (RING + STEPS1 - 2)
        if u < NT + 2:
            return "g_pe", e * NT + (u + 1)
        return "e_pe", e * NT + (u - NT)

    def bank4(b):
        return B[b][:, :].rearrange("p (k n) -> p k n", k=KD)

    def experts(eng, tile, between=lambda i: None):
        for i in range(SHARED_APART):
            tile(0, i == 0)
            between(i)
        with eng.Fori(SHARED_APART, NT):
            tile(0, False)
        eng.wait_ge(S["f_slots"], 1)
        with eng.Fori(1, NE) as e:
            n = eng.value_load(nt_i[0:1, bass.ds(e, 1)], min_val=1, max_val=NT)
            tile(e, True)
            with eng.If(n > 1):
                with eng.Fori(1, n):
                    tile(e, False)
        n = eng.value_load(nt_i[0:1, NE:NE + 1], min_val=1, max_val=NT)
        with eng.Fori(0, n):
            tile(None, False)

    @block.sync
    def _(sp):
        for t0 in range(0, NT - 1, X_TILES):
            sp.dma_start(X[:, t0:t0 + X_TILES, :],
                         x[t0 * P:(t0 + X_TILES) * P, :].rearrange("(t p) d -> p t d", p=P)).then_inc(x_in[t0 // X_TILES], 16)
        sp.wait_ge(S["x_zero"], 1)
        sp.dma_start(X[0:LAST, NT - 1, :], x[(NT - 1) * P:N, :]).then_inc(x_in[-1], 16)
        sp.wait_ge(S["edge_fill"], 1)
        for k, t in enumerate((dst, src)):
            sp.dma_start(e_raw[:, 0, k, :], t[0:P * P].rearrange("(t p) -> t p", p=P)).then_inc(S["edge_in"], 16)
            sp.dma_start(e_raw[0:EFULL - P, 1, k, :],
                         t[P * P:EFULL * P].rearrange("(t p) -> t p", p=P)).then_inc(S["edge_in"], 16)
            sp.dma_start(e_raw[EFULL - P:EFULL - P + 1, 1, k, 0:ETAIL],
                         t[EFULL * P:E].rearrange("(t p) -> t p", t=1)).then_inc(S["edge_in"], 16)
        sp.dma_start(WQKV[:, :, :], w_qkv.rearrange("(k p) n -> p k n", p=P)).then_inc(S["wqkv_in"], 16)
        sp.wait_ge(S["fill_made"], 1)
        sp.dma_start(out[DUMP:DUMP + P, :], fill[:, 0:D]).then_inc(S["f_filled"], 16)
        per = 8
        for t in range(NT, TILES + 1, per):
            n = min(per, TILES + 1 - t)
            sp.dma_start(slots[t * P:(t + n) * P, :].rearrange("(t p) c -> p t c", p=P),
                         fill[:, :].unsqueeze(1).to_broadcast([P, n, ROW])).then_inc(S["f_filled"], 16)
        sp.wait_ge(S["k_pe"], NT)
        sp.wait_ge(S["v_pe"], NT)
        sp.dma_start(WO[0][:, :, :], w_out.rearrange("(k p) n -> p k n", p=P)).then_inc(S["wqkv_in"], 16)

        def first_weights(e, half):
            for m, t in enumerate((wl, wr)):
                sp.dma_start(W[:, bass.ds(half, 1), m].rearrange("p o k n -> p (o k) n"),
                             t[bass.ds(e, 1), 0].rearrange("o (k p) n -> p (o k) n", p=P)).then_inc(S["w1_in"], 16)

        def second_weights(t, e, half, name):
            sp.dma_start(W[:, bass.ds(half, 1), 1].rearrange("p o k n -> p (o k) n"),
                         t[bass.ds(e, 1), 1].rearrange("o (k p) n -> p (o k) n", p=P)).then_inc(S[name], 16)

        sp.wait_ge(S["o_pe"], NT)
        first_weights(0, 0)
        for i in range(NT):
            sp.wait_ge(S["ag_done"], i + 1)
            sp.dma_start(gt[:, :, cols(i)].rearrange("k p n -> p k n"), g_out[i % 2][:, :, :]).then_inc(gt_out[i % 2], 16)
        for t in gt_out:
            sp.wait_ge(t, 16 * NT // 2)

        def expert_loads(e, last):
            half = e & 1
            for n in range(KD * len(CHUNKS)):
                (c, w), k = HCHUNKS[n // KD], n % KD
                if n == GRING:
                    wait_first(sp, "e_pe", e * NT + 1)
                    second_weights(wl, e, (e + 1) & 1, "wl2_in")
                    wait_first(sp, "e_done", e * NT + 2)
                    sp.dma_start(b2[:, :], bl[bass.ds(e, 1), 1, :].rearrange("o d -> (o d)").partition_broadcast(P))\
                        .then_inc(S["b2_in"], 16)
                before = (n - GRING) // KD * 2 * KD + KD + (n - GRING) % KD
                wait_first(sp, "slab_l", e * STEPS1 + (STEPS1 + before + 1))
                sp.dma_start(graw[n % GRING][:, 0:w], gt[k, :, c:c + w]).then_inc(g_in[n % GRING], 16)
            wait_first(sp, "slab_l", e * STEPS1 + 2 * STEPS1)
            second_weights(wr, e, half, "wr2_in")
            if not last:
                wait_first(sp, "g_pe", e * NT + (NT + 2))
                first_weights(e + 1, (e + 1) & 1)

        with sp.Fori(0, GE - 1) as e:
            expert_loads(e, False)
        expert_loads(GE - 1, True)
        sp.wait_ge(S["e_done"], GE * NT + 2)
        sp.wait_ge(S["conv_done"], (GE + 1) * NT)
        sp.dma_start(fg_raw[:, :], ffn_gate).then_inc(S["f_small"], 16)
        sp.dma_start(fb[:, :], ffn_bias.partition_broadcast(P)).then_inc(S["f_small"], 16)
        for r in range(WB // RB):
            w = sh_gu[r * RB * P:(r + 1) * RB * P, :] if r < 2 else sh_dn
            sp.dma_start(raw[:, r * RB:(r + 1) * RB, :], w.rearrange("(q p) d -> p q d", p=P)).then_inc(raw_in[r], 16)
        sp.dma_start(out[0:(NT - 1) * P, :].rearrange("(t p) d -> p t d", p=P), X[:, 0:NT - 1, :]).then_inc(S["f_filled"], 16)
        sp.dma_start(out[(NT - 1) * P:N, :], X[0:LAST, NT - 1, :]).then_inc(S["f_filled"], 16)
        sp.wait_ge(S["f_xn"], NT)
        sp.wait_ge(S["f_consts"], 1)
        sp.dma_start(slots[0:NP, :].rearrange("(t p) c -> p t c", p=P), XR[:, :, :]).then_inc(S["f_shared"], 16)

        def raw_blocks(e, r):
            w = ex_gu[bass.ds(e, 1), r * RB * P:(r + 1) * RB * P, :] if r < 2 else ex_dn[bass.ds(e, 1)]
            sp.dma_start(raw[:, r * RB:(r + 1) * RB, :], w.rearrange("o (q p) d -> p (o q) d", p=P)).then_inc(raw_in[r], 16)

        sp.wait_ge(S["f_shared"], 16)
        sp.dma_start(xg[:, :], slots[0:P, :]).then_inc(S["xg_in"], 16)
        for r in range(WB // RB):
            sp.wait_ge(S["prep_pe"], (r + 1) * RB)
            raw_blocks(0, r)
        tile_no = sp.alloc_register("sp_tile")
        sp.reg_mov(tile_no, 0)

        def next_rows():
            g = sp.snap(tile_no, min_val=0, max_val=TILES - 1)
            sp.wait_ge(S["xt_tpe"], g + 1)
            sp.wait_ge(S["xg_read"], g + 1)
            sp.dma_start(xg[:, :], slots[bass.ds(g * P + P, P), :]).then_inc(S["xg_in"], 16)
            sp.reg_add(tile_no, tile_no, 1)

        for i in range(NT):
            if i == NT - 1:
                sp.wait_ge(S["f_placed"], 16 * NT * TOPK)
            next_rows()
            if i == 0:
                for r in range(WB // RB):
                    sp.wait_ge(S["prep_pe"], WB + (r + 1) * RB)
                    raw_blocks(1, r)
        with sp.Fori(1, NE - 1) as e:
            n = sp.value_load(nt_i[0:1, bass.ds(e, 1)], min_val=1, max_val=NT)
            next_rows()
            for r in range(WB // RB):
                sp.wait_ge(S["prep_pe"], e * WB + (WB + (r + 1) * RB))
                raw_blocks(e + 1, r)
            with sp.If(n > 1):
                with sp.Fori(1, n):
                    next_rows()
        with sp.Fori(NE - 1, NE + 1) as e:
            n = sp.value_load(nt_i[0:1, bass.ds(e, 1)], min_val=1, max_val=NT)
            with sp.Fori(0, n):
                next_rows()

    @block.gpsimd
    def _(pool):
        done = [0]

        def link(ins):
            done[0] += 1
            ins.then_inc(S["pool_chain"], 1)
            pool.wait_ge(S["pool_chain"], done[0])

        imprecise = dict(allow_small_or_imprecise_dtypes=True)
        link(pool.memset(X[96:P, NT - 1, :], 0.0))
        pool.sem_inc(S["x_zero"], 1)
        pool.memset(e_raw[:, :, 0, :], N - 1)
        link(pool.memset(e_raw[:, :, 1, :], 8191))
        pool.sem_inc(S["edge_fill"], 1)
        link(pool.memset(ones_r[:, :].bitcast(F32), 1.0))
        link(pool.memset(ident[:, :], 0.0))
        link(pool.affine_select(out=ident[:, :], in_=ident[:, :], compare_op=ALU.not_equal, fill=1.0,
                                base=0, pattern=[[-1, P]], channel_multiplier=1))
        link(pool.memset(valid[:, :], 1.0))
        link(pool.affine_select(out=valid[:, :], in_=valid[:, :], compare_op=ALU.is_ge, fill=0.0,
                                base=N - 1, pattern=[[-P, NT]], channel_multiplier=-1))
        pool.iota(iota_key[:, :].rearrange("p (a w) -> p a w", a=NT), pattern=[[KEY, NT], [1, WIN]], base=0,
                  channel_multiplier=0, **imprecise)
        pool.iota(iota_low[:, :], pattern=[[1, P]], base=0, channel_multiplier=0, **imprecise)
        pool.iota(neg_win[:, :], pattern=[[-WIN, NW]], base=0, channel_multiplier=0, **imprecise)
        pool.iota(win[:, 0:1], pattern=[[0, 1]], base=0, channel_multiplier=WIN, **imprecise)
        pool.iota(win[:, 1:2], pattern=[[0, 1]], base=WIN, channel_multiplier=WIN, **imprecise)
        pool.iota(it_t[:, 0, :], pattern=[[1, ET]], base=1, channel_multiplier=0, **imprecise)
        pool.iota(it_t[:, 1, :], pattern=[[-1, ET]], base=256, channel_multiplier=0, **imprecise)
        pool.iota(io8[:, :], pattern=[[1, 8]], base=0, channel_multiplier=0, **imprecise)
        pool.memset(keyT[:, :], -10000.0)
        link(pool.memset(lowT[:, :], 0.0))
        pool.sem_inc(S["consts"], 1)
        for e in range(GE):
            pool.dma_start(b1_rows[e * KD:(e + 1) * KD, :],
                           bl[e, 0].rearrange("(k p) -> k p", p=P)).then_inc(S["small_in"], 16)
        pool.dma_start(gw[:, :, :], gate_w.rearrange("(k p) n -> p k n", p=P)).then_inc(S["small_in"], 16)
        pool.dma_start(gb[:, :], gate_b.partition_broadcast(P)).then_inc(S["small_in"], 16)
        pool.dma_start(bo[:, :], b_out.partition_broadcast(P)).then_inc(S["small_in"], 16)
        link(pool.memset(fill[:, :], 0.0))
        link(pool.iota(fill[:, TCOL:TCOL + 1], pattern=[[0, 1]], base=DUMP, channel_multiplier=1, **imprecise))
        pool.sem_inc(S["fill_made"], 1)
        pool.memset(lg[:, :, :], -1.0)
        pool.memset(KVB[:, :, :], 0.0)
        link(pool.memset(KS[:, :, :], 0.0))
        link(pool.memset(heads[:, :, :], 1.0))
        link(pool.affine_select(out=heads[:, :, :], in_=heads[:, :, :], compare_op=ALU.is_ge, fill=0.0,
                                base=0, pattern=[[P, HP], [1, P]], channel_multiplier=-P // 2))
        link(pool.affine_select(out=heads[:, :, :], in_=heads[:, :, :], compare_op=ALU.is_ge, fill=0.0,
                                base=P // 2 - 1, pattern=[[-P, HP], [-1, P]], channel_multiplier=P // 2))
        pool.wait_ge(S["bounds_out"], 1)
        for h in range(HP):
            last = pool.tensor_copy(V[:, :, h, P:P + 1], valid[:, :].unsqueeze(2))
        link(last)
        pool.sem_inc(S["mix_setup"], 1)
        pool.wait_ge(S["small_in"], 16 * (GE + 3))
        pool.wait_ge(S["xn_done"], NT)
        pool.tensor_tensor(X[:, :, :], X[:, :, :], bo[:, :].unsqueeze(1).to_broadcast([P, NT, D]), ALU.add)\
            .then_inc(S["bias_added"], 1)
        for i in range(NT):
            pool.wait_ge(S["xn_h"], i + 1)
            pool.tensor_tensor(XN_L[:, i, :], XN[:, i, :], XN_H[:, i, :].bitcast(F32), ALU.subtract).then_inc(S["xn_l"], 1)
        pool.wait_ge(S["ag_pe"], NT)
        link(pool.memset(HT[:, :, N:NP], 0.0))
        pool.sem_inc(S["h_zero"], 1)
        pool.sem_inc(S["e_done"], 2)
        with pool.Fori(0, GE) as e:
            for i in range(NT):
                pool.wait_ge(S["e_gated"], e * NT + i + 3)
                pool.tensor_tensor(X[:, i, :], X[:, i, :], t1[i % 2][:, :], ALU.add).then_inc(S["e_done"], 1)
        pool.wait_ge(S["e_done"], GE * NT + 2)
        pool.wait_ge(S["conv_done"], (GE + 1) * NT)
        link(pool.memset(XR[:, :, D:ROW], 0.0))
        pool.memset(XR[:, :, GCOL + TOPK:GCOL + TOPK + 1], 1.0)
        pool.iota(XR[:, :, SCOL + TOPK], pattern=[[P, NT]], base=0, channel_multiplier=1, **imprecise)
        link(pool.iota(XR[:, :, TCOL], pattern=[[P, NT]], base=0, channel_multiplier=1, **imprecise))
        pool.sem_inc(S["f_consts"], 1)
        pool.iota(io16[:, :], pattern=[[1, NE]], base=0, channel_multiplier=0, **imprecise)
        pool.iota(slot[:, :], pattern=[[0, 1]], base=0, channel_multiplier=1, **imprecise)
        pool.memset(ones2[:, :], 1.0)
        link(pool.memset(upper[:, :], 1.0))
        link(pool.affine_select(out=upper[:, :], in_=upper[:, :], compare_op=ALU.is_gt, fill=0.0,
                                base=0, pattern=[[1, P]], channel_multiplier=-1))
        for z in [w[:, 1, :, :] for w in DNW] + [h[:, :, :] for h in ht]:
            pool.memset(z.bitcast(F32), 0.0)
        pool.iota(meta[:, :, 1], pattern=[[0, 2]], base=DUMP, channel_multiplier=1, **imprecise)
        pool.memset(nt_i[:, 0:1], NT)
        link(pool.memset(meta[:, :, 0], 0.0))
        pool.sem_inc(S["f_consts"], 1)
        fills = 3 + math.ceil((TILES + 1 - NT) / 8)
        pool.wait_ge(S["f_filled"], 16 * fills)
        pool.wait_ge(S["f_shared"], 16)
        tile_no = pool.alloc_register("pool_tile")
        pool.reg_mov(tile_no, 0)

        def add_rows(g, scatter=()):
            wait_first(pool, "y_done", g + 2)
            pool.indirect_dma_start(
                out=out, out_offset=bass.IndirectOffsetOnAxis(ap=y_tok[:, 0:1], axis=0),
                in_=y[:, :], in_offset=None, compute_op=ALU.add).then_inc(S["y_added"], 16)
            for i in scatter:
                if i == 0:
                    pool.wait_ge(S["f_slots"], 1)
                r = P if i < NT - 1 else LAST
                for k in range(TOPK):
                    pool.indirect_dma_start(
                        out=slots, out_offset=bass.IndirectOffsetOnAxis(ap=sl_u[0:r, k, i:i + 1], axis=0),
                        in_=XR[0:r, i, :], in_offset=None).then_inc(S["f_placed"], 16)
                if i == scatter[0]:
                    free(g)
            if not scatter:
                free(g)

        def free(g):
            pool.wait_ge(S["y_added"], g * 16 + 16)
            pool.sem_inc(S["y_free"], 1)

        def tile(scatter=()):
            g = pool.snap(tile_no, min_val=0, max_val=TILES - 1)
            add_rows(g, scatter)
            pool.reg_add(tile_no, tile_no, 1)

        pool.sem_inc(S["y_free"], 1)
        scattered = 0
        for i in range(NT):
            todo = min(2 * max(0, i - SHARED_APART + 1), NT)
            tile(range(scattered, todo))
            scattered = todo
        with pool.Fori(1, NE + 1) as e:
            n = pool.value_load(nt_i[0:1, bass.ds(e, 1)], min_val=1, max_val=NT)
            with pool.Fori(0, n):
                tile()
        add_rows(pool.snap(tile_no, min_val=NT + NE, max_val=TILES))

    @block.scalar
    def _(act):
        act.wait_ge(S["var_done"], 1)
        act.activation(rstd[:, 1, :], rstd[:, 0, :], ACT.Sqrt).then_inc(S["std_done"], 1)
        act.preload_act_table(ACT.Exp)
        for i in range(NT):
            act.wait_ge(S["xt_pe"], i + 1)
            act.activation(XT[:, :, cols(i)], B[i % 2][:, :].rearrange("p (k n) -> p k n", k=KD),
                           ACT.Copy).then_inc(S["xt_done"], 1)
        act.wait_ge(S["ex_max"], 1)
        act.activation(lg[:, :, 0:GE], lg[:, :, 0:GE], ACT.Exp).then_inc(S["ex_exp"], 1)
        def window_pair(p):
            for w in (2 * p, 2 * p + 1):
                act.wait_ge(S["win_pe"], w + 1)
                act.activation(AT[:, :, w * WIN:(w + 1) * WIN],
                               B[6 + w % 2][:, 0:WC].rearrange("p (a w) -> p a w", a=NT), ACT.Copy).then_inc(S["win_done"], 1)

        for n in range(12):
            c, w = CHUNKS[n // KD]
            act.wait_ge(S["q_pe"], n + 1)
            if n >= 2:
                act.wait_ge(S["q_done"], n - 1)
            act.activation(expo[n % 2][:, 0:w], B[n % 2][:, 0:w], ACT.Exp).then_inc(S["q_exp"], 1)
            if n in PAIR_AFTER_Q:
                window_pair(PAIR_AFTER_Q[n])
        for i in range(NT):
            act.wait_ge(S["k_pe"], i + 1)
            if i < 2:
                act.wait_ge(S["q_done"], 11 + i)
            else:
                act.wait_ge(S["k_done"], i - 1)
            act.activation(expo[i % 2][:, :], B[2 + i % 2][:, :], ACT.Exp).then_inc(S["k_exp"], 1)
            act.wait_ge(S["v_pe"], i + 1)
            act.activation(V[:, i, :, 0:P], B[4 + i % 2][:, :].rearrange("p (h m) -> p h m", h=HP),
                           ACT.Copy).then_inc(S["v_done"], 1)
            window_pair(PAIR_AFTER_KV[i])

        def at_high(n):
            (c, w), h = CHUNKS[n // HP], n % HP
            act.wait_ge(S["at_whole"], n + 1)
            act.activation(QH[:, h, c:c + w], expo[n % 3][:, 0:w], ACT.Copy).then_inc(S["at_h"], 1)

        act.wait_ge(S["kv_pe"], HP)
        act.wait_ge(S["wqkv_in"], 32)
        act.activation(WO[1][:, :, :], WO[0][:, :, :], ACT.Copy).then_inc(S["wo_h"], 1)
        for n in range(12):
            c, w = CHUNKS[n // HP]
            act.wait_ge(S["at_pe"], n + 1)
            if n >= 3:
                act.wait_ge(S["at_done"], n - 2)
            act.activation(expo[n % 3][:, 0:w], B[2 + n % 2][:, 0:w], ACT.Copy).then_inc(S["at_factor"], 1)
            if n >= 1:
                at_high(n - 1)
        at_high(11)
        for n in range(NT):
            act.activation(XN_H[:, n, :], XN[:, n, :], ACT.Copy).then_inc(S["xn_h"], 1)
        for i in sorted(PAIR_AFTER_O):
            window_pair(PAIR_AFTER_O[i])

        def slab(e, half, n):
            (c, w), k = HCHUNKS[n // (2 * KD)], n % (2 * KD)
            wh, _, xh, _ = slabs[n % RING]
            wait_first(act, "l1_pe", e * STEPS1 + (n + 1))
            act.activation(wh[:, :], W[:, bass.ds(half, 1), 1 - k // KD, k % KD, :].rearrange("p o n -> p (o n)"), ACT.Copy)
            if k >= KD:
                g = n // (2 * KD) * KD + k - KD
                act.wait_ge(g_in[g % GRING], e * (16 * KD * len(CHUNKS) // GRING) + 16 * (g // GRING + 1))
                source = graw[g % GRING][:, 0:w]
            else:
                source = XT[:, k, c:c + w]
            act.activation(xh[:, 0:w], source, ACT.Copy).then_inc(S["slab_h"], 1)

        act.wait_ge(S["at_ready"], 1)
        for i in range(2):
            act.activation(conv[i][:, :, :], AT[:, :, cols(i)], ACT.Copy).then_inc(S["conv_done"], 1)
        act.sem_inc(S["e_scaled"], 1)
        for i in range(NT):
            if i == NT - 1:
                act.wait_ge(S["w1_in"], 32)
                for n in range(2):
                    slab(0, 0, n)
            act.wait_ge(S["ag_inv"], i + 1)
            if i >= 2:
                act.wait_ge(S["ag_tpe"], i - 1)
            act.activation(t1[i % 2][:, :], B[4 + i % 2][:, :], ACT.Copy, scale=inv_nat[:, i:i + 1]).then_inc(S["ag_scaled"], 1)
            if i + 2 < NT:
                act.activation(conv[i % 2][:, :, :], AT[:, :, cols(i + 2)], ACT.Copy).then_inc(S["conv_done"], 1)
        act.wait_ge(S["ag_tpe"], NT)
        act.wait_ge(S["h_zero"], 1)
        act.wait_ge(S["small_in"], 16 * (GE + 3))

        def h_tile(e, u):
            wait_first(act, *hs_free(e, u))
            act.activation(hs[u % 2][0][:, :, :], HT[:, :, cols(u % NT)], ACT.Copy).then_inc(S["hs_h"], 1)

        with act.Fori(0, GE) as e:
            half = act.snap(e & 1, min_val=0, max_val=1)
            other = act.snap((e + 1) & 1, min_val=0, max_val=1)

            def relu(c):
                wait_first(act, "l1_pe", e * STEPS1 + (RING + (c + 1) * 2 * KD))
                at0, w = HCHUNKS[c]
                for j in range(KD):
                    act.activation(HT[:, j, at0:at0 + w], B[4 * (c % 2) + j][:, 0:w], ACT.Relu,
                                   bias=b1[:, bass.ds(e * KD + j, 1)]).then_inc(S["h_done"], 1)

            act.wait_ge(S["e_pe"], e * NT + 1)
            for n in range(2, STEPS1):
                k = n % (2 * KD)
                slab(e, half, n)
                if n // (2 * KD) > 0 and k == 2:
                    relu(n // (2 * KD) - 1)
                if n == STEPS1 // 2 + KD:
                    wait_first(act, "wl2_in", e * 16 + 16)
                    act.activation(WR[:, bass.ds(other, 1), 0].rearrange("p o k n -> p (o k) n"),
                                   W[:, bass.ds(other, 1), 1].rearrange("p o k n -> p (o k) n"), ACT.Copy).then_inc(S["w2_h"], 1)
            act.wait_ge(S["h_done"], e * 12 + 8)
            h_tile(e, 0)
            h_tile(e, 1)
            relu(2)
            act.wait_ge(S["h_done"], e * 12 + 12)
            for i in range(NT):
                if i >= 1:
                    h_tile(e, i + 1)
                act.wait_ge(S["g_pe"], e * NT + (i + 3))
                act.activation(GH[:, i, :], B[4 + i % 2][:, :], ACT.Copy).then_inc(S["g_h"], 1)
                if i < 2:
                    act.activation(conv[i][:, :, :], AT[:, :, cols(i)], ACT.Copy).then_inc(S["conv_done"], 1)
                if 4 <= i < 4 + KD:
                    if i == 4:
                        wait_first(act, "wr2_in", e * 16 + 16)
                    act.activation(WR[:, bass.ds(half, 1), 0, i - 4].rearrange("p o n -> p (o n)"),
                                   W[:, bass.ds(half, 1), 1, i - 4].rearrange("p o n -> p (o n)"), ACT.Copy).then_inc(S["w2_h"], 1)
            for i in range(NT):
                if i + 1 < NT:
                    h_tile(e, NT + i + 1)
                else:
                    with act.If(e < GE - 1):
                        act.wait_ge(S["w1_in"], e * 32 + 64)
                        wait_first(act, "own_pe", e * NT + NT)
                        for n in range(2):
                            slab(e + 1, other, n)
                act.wait_ge(S["e_pe"], e * NT + i + 2)
                act.wait_ge(S["e_done"], e * NT + i + 1)
                act.activation(t1[i % 2][:, :], B[2 + i % 2][:, :], ACT.Copy,
                               scale=inv_nat[:, i:i + 1]).then_inc(S["e_scaled"], 1)
                if i + 2 < NT:
                    act.activation(conv[i % 2][:, :, :], AT[:, :, cols(i + 2)], ACT.Copy).then_inc(S["conv_done"], 1)
        act.wait_ge(S["f_var"], 1)
        act.activation(rstd[:, 1, :], rstd[:, 0, :], ACT.Sqrt).then_inc(S["f_std"], 1)
        act.preload_act_table(ACT.Sigmoid)

        def logits_out(i):
            act.wait_ge(S["f_lg"], i + 1)
            act.activation(lgT[:, cols(i)], B[5][0:NE, 0:P], ACT.Copy).then_inc(S["f_lgdone"], 1)

        for q in range(WB):
            if q >= 2:
                logits_out(q - 2)
            if 1 <= q <= NT:
                act.wait_ge(S["f_tpe"], q)
                act.activation(xft[(q - 1) % 2][:, :, :], bank4((q - 1) % 2), ACT.Copy).then_inc(S["f_tdone"], 1)
            act.wait_ge(S["prep_pe"], q + 1)
            dest = GUW[0][:, 0, :, cols(q)] if q < GU // P else DNW[0][:, 0, :, cols(q - GU // P)]
            act.activation(dest, bank4(PREP_BANKS[q % PRING]), ACT.Copy).then_inc(S["prep_h"], 1)
        act.wait_ge(S["xt_tpe"], 1)
        act.activation(xt[0][:, :, :], bank4(2), ACT.Copy).then_inc(S["xt_h"], 1)
        act.wait_ge(S["f_lgt"], 1)
        act.activation(aff[:, :, :], B[5][:, 0:NT * NE].rearrange("p (t e) -> p t e", e=NE),
                       ACT.Sigmoid).then_inc(S["f_aff"], 1)

        def xt_high(n):
            act.wait_ge(S["xt_tpe"], n)
            act.activation(xt[0][:, :, :], bank4(2), ACT.Copy).then_inc(S["xt_h"], 1)

        act.sem_inc(S["y_done"], 1)
        tile_no = act.alloc_register("act_tile")
        act.reg_mov(tile_no, 0)

        def rows(g):
            act.wait_ge(S["dn_pe"], g + 1)
            act.wait_ge(S["meta_done"], g + 2)
            act.wait_ge(S["y_free"], g + 1)
            act.activation(y[:, :], B[5][:, :], ACT.Copy, scale=y_gate[:, 0:1]).then_inc(S["y_done"], 1)

        def tile(e, first):
            g = act.snap(tile_no, min_val=0, max_val=TILES - 1)
            par = None if e is None else (e + 1) & 1

            def blocks(*qs):
                for q in qs if first else ():
                    wait_first(act, "prep_pe", e * WB + (WB + q + 1))
                    if q < GU // P:
                        dest = GUW[0][:, bass.ds(par, 1), :, cols(q)]
                    else:
                        dest = DNW[0][:, bass.ds(par, 1), :, cols(q - GU // P)]
                    act.activation(dest.rearrange("p o k n -> p (o k) n"), bank4(PREP_BANKS[q % PRING]),
                                   ACT.Copy).then_inc(S["prep_h"], 1)

            blocks(0, 1, 2)
            act.wait_ge(S["gate_pe"], g + 1)
            act.activation(sig[:, :], B[0][:, :], ACT.Sigmoid).then_inc(S["sig_done"], 1)
            blocks(3, 4, 5, 6, 7)
            xt_high(g + 2)
            rows(g)
            blocks(8)
            act.wait_ge(S["h_tpe"], g + 1)
            act.activation(ht[0][:, :, :], bank4(2), ACT.Copy).then_inc(S["ht_h"], 1)
            blocks(9, 10, 11)
            act.reg_add(tile_no, tile_no, 1)

        experts(act, tile)
        rows(act.snap(tile_no, min_val=NT + NE, max_val=TILES))

    @block.vector
    def _(dve):
        done = [0]

        def link(ins):
            done[0] += 1
            ins.then_inc(S["chain"], 1)
            dve.wait_ge(S["chain"], done[0])

        def normalise(dest, var_sem, std_sem, done_sem, first=0):
            if first:
                dve.wait_ge(S["stats_done"], GE * first)
            for i in range(first, NT):
                if not first and i % X_TILES == 0:
                    dve.wait_ge(x_in[i // X_TILES], 16)
                last = dve.bn_stats(stats[:, i, :], X[:, i, :])
            link(last)
            for i in range(NT):
                last = dve.bn_aggr(mv[:, i, :], stats[:, i, :])
            link(last)
            link(dve.tensor_scalar(rstd[:, 0, :], mv[:, :, 1], EPS, None, ALU.add))
            dve.sem_inc(S[var_sem], 1)
            dve.wait_ge(S[std_sem], 1)
            link(dve.reciprocal(rstd[:, 2, :], rstd[:, 1, :]))
            link(dve.tensor_tensor(rstd[:, 3, :], rstd[:, 2, :], rstd[:, 2, :], ALU.mult))
            link(dve.tensor_tensor(rstd[:, 3, :], rstd[:, 3, :], rstd[:, 0, :], ALU.mult))
            link(dve.tensor_scalar(rstd[:, 3, :], rstd[:, 3, :], -0.5, 1.5, ALU.mult, ALU.add))
            link(dve.tensor_tensor(rstd[:, 3, :], rstd[:, 3, :], rstd[:, 2, :], ALU.mult))
            for i in range(NT):
                dve.tensor_scalar(dest[:, i, 0:D], X[:, i, :], mv[:, i, 0:1], rstd[:, 3, i:i + 1],
                                  ALU.subtract, ALU.mult).then_inc(S[done_sem], 1)

        normalise(XN, "var_done", "std_done", "xn_done")

        dve.wait_ge(S["edge_in"], 6 * 16)
        link(dve.tensor_scalar(e_int[:, :, 0, :], e_raw[:, :, 1, :], 7, None, ALU.logical_shift_right))
        link(dve.tensor_scalar(e_int[:, :, 1, :], e_raw[:, :, 1, :], P - 1, None, ALU.bitwise_and))
        link(dve.tensor_copy(e_f[:, :, 0, :], e_raw[:, :, 0, :]))
        link(dve.tensor_copy(e_f[:, :, 1, :], e_int[:, :, 1, :]))
        link(dve.tensor_copy(e_f[:, :, 2, :], e_int[:, :, 0, :]))
        link(dve.scalar_tensor_tensor(e_f[:, :, 3, :], e_f[:, :, 2, :], float(KEY), e_f[:, :, 0, :],
                                      op0=ALU.mult, op1=ALU.add))
        link(dve.tensor_reduce(e_mm[:, :, 0], e_f[:, :, 0, :], AX.X, ALU.min))
        link(dve.tensor_reduce(e_mm[:, :, 1], e_f[:, :, 0, :], AX.X, ALU.max))
        dve.sem_inc(S["edge_keys"], 1)
        dve.wait_ge(S["consts"], 1)
        dve.wait_ge(S["edge_pe"], 1)
        T = B[2][:, :].rearrange("p (g k t) -> p g k t", g=2, k=2)
        dve.tensor_copy(keyT[:, 0:P], T[:, 0, 0, :])
        dve.tensor_copy(keyT[:, P:ET], T[:, 1, 0, 0:ET - P])
        dve.tensor_copy(lowT[:, 0:P], T[:, 0, 1, :])
        dve.tensor_copy(lowT[:, P:ET], T[:, 1, 1, 0:ET - P])
        link(dve.tensor_copy(ok[:, 0:2, :], B[3][0:NW, 0:2 * ET].rearrange("p (k t) -> p k t", k=2)))
        link(dve.tensor_scalar(ok[:, 2, :], ok[:, 1, :], win[:, 0:1], None, ALU.is_ge))
        link(dve.scalar_tensor_tensor(ok[:, 2, :], ok[:, 0, :], win[:, 1:2], ok[:, 2, :], op0=ALU.is_lt, op1=ALU.mult))
        link(dve.tensor_tensor(ok[:, 0, :], ok[:, 2, :], it_t[:, 0, :], ALU.mult))
        link(dve.tensor_tensor(ok[:, 1, :], ok[:, 2, :], it_t[:, 1, :], ALU.mult))
        link(dve.tensor_reduce(lohi[:, 0:2], ok[:, 0:2, :], AX.X, ALU.max))
        link(dve.tensor_scalar(lohi[:, 2:3], lohi[:, 1:2], -1.0, 256.0, ALU.mult, ALU.add))
        link(dve.tensor_scalar(lohi[:, 2:3], lohi[:, 2:3], float(ET - 1), None, ALU.min))
        link(dve.tensor_scalar(lohi[:, 3:4], lohi[:, 2:3], float(VISITS), None, ALU.add))
        link(dve.tensor_tensor(lohi[:, 4:5], lohi[:, 3:4], lohi[:, 0:1], ALU.max))
        dve.sem_inc(S["edge_bounds"], 1)
        dve.wait_ge(S["edge_pe"], 2)
        link(dve.tensor_copy(row_f[:, :], B[4][0:1, 0:3 * NW]))
        link(dve.tensor_tensor(row_d[:, :], row_f[:, 2 * NW:3 * NW], row_f[:, NW:2 * NW], ALU.subtract))
        link(dve.tensor_copy(bounds_i[:, 0:LONG], row_f[:, :]))
        link(dve.tensor_reduce(bounds_i[:, LONG:LONG + 1], row_d[:, :], AX.X, ALU.max))
        dve.sem_inc(S["bounds_out"], 1)

        dve.wait_ge(S["small_in"], 16 * (GE + 3))
        dve.wait_ge(S["lg_pe"], NT + 1)
        dve.wait_ge(S["mix_setup"], 1)
        link(dve.tensor_copy(b1[:, :], B[7][:, 0:GE * KD]))
        link(dve.tensor_tensor(lg[:, :, 0:GE], B[6][:, 0:NT * GE].rearrange("p (t e) -> p t e", e=GE),
                               gb[:, :].unsqueeze(1).to_broadcast([P, NT, GE]), ALU.add))
        link(dve.tensor_reduce(lt[:, 0, :], lg[:, :, 0:GE], AX.X, ALU.max))
        link(dve.tensor_tensor(lg[:, :, 0:GE], lg[:, :, 0:GE], lt[:, 0, :].unsqueeze(2).to_broadcast([P, NT, GE]),
                               ALU.subtract))
        dve.sem_inc(S["ex_max"], 1)
        dve.wait_ge(S["ex_exp"], 1)
        link(dve.tensor_reduce(lt[:, 1, :], lg[:, :, 0:GE], AX.X, ALU.add))
        link(dve.reciprocal(lt[:, 2, :], lt[:, 1, :]))
        link(dve.tensor_tensor(lg[:, :, 0:GE], lg[:, :, 0:GE], lt[:, 2, :].unsqueeze(2).to_broadcast([P, NT, GE]),
                               ALU.mult))
        for i in range(NT):
            last = dve.max(top8[:, i, :], lg[:, i, :])
        link(last)
        for i in range(NT):
            last = dve.max_index(idx8[:, i, :], top8[:, i, :], lg[:, i, :])
        link(last)
        link(dve.tensor_copy(idxf[:, :, :], idx8[:, :, :]))
        link(dve.tensor_tensor(eq[:, :, :, :], idxf[:, :, 0:2].unsqueeze(3).to_broadcast([P, NT, 2, GE]),
                               io8[:, 0:GE].unsqueeze(1).unsqueeze(1).to_broadcast([P, NT, 2, GE]), ALU.is_equal))
        link(dve.tensor_tensor(eq[:, :, 0, :], eq[:, :, 0, :], eq[:, :, 1, :], ALU.add))
        link(dve.tensor_tensor(coef[:, :, :], eq[:, :, 0, :], lg[:, :, 0:GE], ALU.mult))

        def feature(n, dest, e_tile, bank, exp_sem, done_sem):
            dve.wait_ge(S[exp_sem], n + 1)
            link(dve.tensor_scalar(e_tile, e_tile, 1.0, None, ALU.min))
            dve.scalar_tensor_tensor(dest, bank, 0.0, e_tile, op0=ALU.max, op1=ALU.add).then_inc(S[done_sem], 1)

        def one_hots(slot, v, tile_col, window):
            dve.tensor_scalar(low1[:, slot, v, :], iota_low[:, :], lowT[:, tile_col], None, ALU.is_equal)
            return dve.tensor_scalar(key1[:, slot, v, :], iota_key[:, :], keyT[:, tile_col],
                                     neg_win[:, window], ALU.subtract, ALU.is_equal)

        def hot_pair(p):
            for w in (2 * p, 2 * p + 1):
                lo = dve.value_load(bounds_i[0:1, w:w + 1], min_val=0, max_val=ET - 1)
                if w >= 2:
                    dve.wait_ge(S["win_pe"], w - 1)
                for v in range(VISITS):
                    one_hots(w % 2, v, bass.ds(lo + v, 1), slice(w, w + 1)).then_inc(S["hot_ready"], 1)

        hot_pair(0)
        for n in range(12):
            (c, w), j = CHUNKS[n // KD], n % KD
            feature(n, QT[:, j, c:c + w], expo[n % 2][:, 0:w], B[n % 2][:, 0:w], "q_exp", "q_done")
            if n in PAIR_AFTER_Q:
                hot_pair(PAIR_AFTER_Q[n] + 1)
        for i in range(NT):
            feature(i, K[:, i, :], expo[i % 2][:, :], B[2 + i % 2][:, :], "k_exp", "k_done")
            hot_pair(PAIR_AFTER_KV[i] + 1)
        for h in range(HP):
            dve.wait_ge(S["kv_pe"], h + 1)
            b = B[6 + h % 2]
            for m, r in enumerate((slice(0, 64), slice(64, P))):
                dve.tensor_copy(KVB[r, h, r], b[r, r])
                last = dve.tensor_copy(KS[r, h, 2 * h + m:2 * h + m + 1], b[r, P:P + 1])
            last.then_inc(S["kv_done"], 1)
        def denominators(chunk):
            c, w = CHUNKS[chunk]
            dve.wait_ge(S["den_pe"], chunk + 1)
            link(dve.tensor_scalar(den[:, c:c + w], B[4 + chunk % 2][0:2 * HP, 0:w], 1e-6, None, ALU.add))
            dve.reciprocal(den[:, c:c + w], den[:, c:c + w]).then_inc(S["den_done"], 1)

        def at_low(n):
            (c, w), h = CHUNKS[n // HP], n % HP
            dve.wait_ge(S["at_h"], n + 1)
            dve.tensor_tensor(QL[:, h, c:c + w], expo[n % 3][:, 0:w], QH[:, h, c:c + w].bitcast(F32), ALU.subtract)\
                .then_inc(S["at_done"], 1)

        denominators(0)
        denominators(1)
        dve.wait_ge(S["wo_h"], 1)
        dve.tensor_tensor(WO[2][:, :, :], WO[0][:, :, :], WO[1][:, :, :].bitcast(F32), ALU.subtract).then_inc(S["wo_l"], 1)
        for n in range(12):
            (c, w), h = CHUNKS[n // HP], n % HP
            if n == HP:
                denominators(2)
            dve.wait_ge(S["at_pe"], n + 1)
            r = expo[n % 3][:, 0:w]
            dve.wait_ge(S["at_factor"], n + 1)
            dve.tensor_tensor(r, B[n % 2][:, 0:w], r, ALU.mult).then_inc(S["at_whole"], 1)
            if n >= 1:
                at_low(n - 1)
        at_low(11)
        for i in range(NT):
            dve.wait_ge(S["o_pe"], i + 1)
            if i == 0:
                dve.wait_ge(S["bias_added"], 1)
            dve.tensor_tensor(X[:, i, :], X[:, i, :], B[4 + i % 2][:, :], ALU.add).then_inc(S["o_done"], 1)
            if i in PAIR_AFTER_O and PAIR_AFTER_O[i] + 1 < NW // 2:
                hot_pair(PAIR_AFTER_O[i] + 1)

        dve.wait_ge(S["win_done"], NW)
        long = dve.value_load(bounds_i[0:1, LONG:LONG + 1], min_val=0, max_val=ETP)
        with dve.If(long > 0):
            more = dve.alloc_register("dve_more")
            dve.reg_mov(more, 1)
            with dve.Fori(0, NW) as w:
                at = dve.value_load(bounds_i[0:1, bass.ds(w + NW, 1)], min_val=VISITS, max_val=ETP - 1)
                end = dve.value_load(bounds_i[0:1, bass.ds(w + 2 * NW, 1)], min_val=VISITS, max_val=ETP - 1)
                with dve.If(end > at):
                    with dve.Fori(at, end) as t:
                        m = dve.snap(more, min_val=1, max_val=NW * ET)
                        one_hots(0, 0, bass.ds(t, 1), bass.ds(w, 1)).then_inc(S["lhot_ready"], 1)
                        dve.wait_ge(S["long_pe"], m)
                        part = AT[:, :, bass.ds(w * WIN, WIN)]
                        dve.tensor_tensor(part, part, B[6][:, 0:WC].rearrange("p (a w) -> p a w", a=NT), ALU.add)\
                            .then_inc(S["long_done"], 1)
                        dve.wait_ge(S["long_done"], m)
                        dve.reg_add(more, more, 1)
        dve.sem_inc(S["at_ready"], 1)

        def low_counts(n, i):
            with dve.If(long > 0):
                dve.wait_ge(S["conv_done"], n + 1)
                dve.wait_ge(S["ag_low_pe"], n + 1)
                dve.tensor_tensor(conv_low[:, :, :], AT[:, :, cols(i)], conv[i % 2][:, :, :].bitcast(F32), ALU.subtract)\
                    .then_inc(S["conv_l"], 1)

        def rest(dest, source, high):
            return dve.tensor_tensor(dest, source, high.bitcast(F32), ALU.subtract)

        def slab(e, half, n):
            (c, w), k = HCHUNKS[n // (2 * KD)], n % (2 * KD)
            wh, wlo, xh, xlo = slabs[n % RING]
            dve.wait_ge(S["slab_h"], e * STEPS1 + (n + 1))
            rest(wlo[:, :], W[:, bass.ds(half, 1), 1 - k // KD, k % KD, :].rearrange("p o n -> p (o n)"), wh[:, :])
            source = XT[:, k, c:c + w] if k < KD else graw[(n // (2 * KD) * KD + k - KD) % GRING][:, 0:w]
            rest(xlo[:, 0:w], source, xh[:, 0:w]).then_inc(S["slab_l"], 1)

        dve.sem_inc(S["slab_l"], STEPS1)

        def rows_out(i):
            dve.wait_ge(S["ag_tpe"], i + 1)
            if i >= 2:
                dve.wait_ge(gt_out[i % 2], 16 * (i // 2))
            dve.tensor_copy(g_out[i % 2][:, :, :], bank4(i % 2)).then_inc(S["ag_done"], 1)

        for i in range(NT):
            if i == NT - 1:
                for n in range(2):
                    slab(0, 0, n)
            low_counts(i, i)
            dve.wait_ge(S["ag_pe"], i + 1)
            link(dve.tensor_scalar(inv_nat[:, i:i + 1], B[2 + i % 2][:, 0:1], 1.0, None, ALU.max))
            dve.reciprocal(inv_nat[:, i:i + 1], inv_nat[:, i:i + 1]).then_inc(S["ag_inv"], 1)
            if i >= 1:
                rows_out(i - 1)
        rows_out(NT - 1)

        dve.sem_inc(S["g_done"], 2)
        dve.sem_inc(S["e_gated"], 2)

        def second_rest(half, n):
            dve.wait_ge(S["w2_h"], n)
            place = [t[:, bass.ds(half, 1), m].rearrange("p o k n -> p (o k) n") for t, m in ((WR, 1), (W, 1), (WR, 0))]
            rest(*place).then_inc(S["w2_l"], 1)

        def h_tile(e, u):
            dve.wait_ge(S["hs_h"], e * (2 * NT) + (u + 1))
            rest(hs[u % 2][1][:, :, :], HT[:, :, cols(u % NT)], hs[u % 2][0][:, :, :]).then_inc(S["hs_l"], 1)

        with dve.Fori(0, GE) as e:
            half = dve.snap(e & 1, min_val=0, max_val=1)
            other = dve.snap((e + 1) & 1, min_val=0, max_val=1)
            for n in range(2, STEPS1):
                slab(e, half, n)
                if n == STEPS1 // 2 + KD:
                    second_rest(other, e * (1 + KD) + 1)
            h_tile(e, 0)
            h_tile(e, 1)
            for i in range(NT):
                if i >= 1:
                    h_tile(e, i + 1)
                dve.wait_ge(S["g_h"], e * NT + i + 1)
                rest(GL[:, i, :], B[4 + i % 2][:, :], GH[:, i, :]).then_inc(S["g_done"], 1)
                if 4 <= i < 4 + KD:
                    dve.wait_ge(S["w2_h"], e * (1 + KD) + (i - 2))
                    rest(*(t[:, bass.ds(half, 1), m, i - 4].rearrange("p o n -> p (o n)")
                           for t, m in ((WR, 1), (W, 1), (WR, 0)))).then_inc(S["w2_l"], 1)
            for i in range(NT):
                if i + 1 < NT:
                    h_tile(e, NT + i + 1)
                else:
                    with dve.If(e < GE - 1):
                        for n in range(2):
                            slab(e + 1, other, n)
                low_counts(e * NT + (i + NT), i)
                dve.wait_ge(S["e_scaled"], e * NT + i + 2)
                dve.tensor_tensor(t1[i % 2][:, :], t1[i % 2][:, :], B[6 + i % 2][:, :], ALU.add).then_inc(S["e_chain"], 1)
                if i == 0:
                    dve.wait_ge(S["b2_in"], e * 16 + 16)
                dve.wait_ge(S["e_chain"], e * (2 * NT) + (2 * i + 1))
                dve.tensor_tensor(t1[i % 2][:, :], t1[i % 2][:, :], b2[:, :], ALU.add).then_inc(S["e_chain"], 1)
                dve.wait_ge(S["e_chain"], e * (2 * NT) + (2 * i + 2))
                dve.tensor_scalar(t1[i % 2][:, :], t1[i % 2][:, :], 0.0,
                                  coef[:, i, bass.ds(e, 1)], ALU.max, ALU.mult).then_inc(S["e_gated"], 1)
                if i >= 2:
                    dve.wait_ge(S["e_done"], e * NT + (i + 1))
                    if i >= 3:
                        dve.wait_ge(S["stats_done"], e * (NT - 2) + (i - 2))
                    dve.bn_stats(stats[:, i - 2, :], X[:, i - 2, :]).then_inc(S["stats_done"], 1)

        dve.wait_ge(S["e_done"], GE * NT + 2)
        normalise(XR, "f_var", "f_std", "f_xn", first=NT - 2)
        def low_part(dest_l, dest_h, bank, done_sem):
            return dve.tensor_tensor(dest_l, bank, dest_h.bitcast(F32), ALU.subtract).then_inc(S[done_sem], 1)

        dve.wait_ge(S["fgt_pe"], 1)
        dve.tensor_copy(fgT[:, :, :], B[2][:, 0:KD * NE].rearrange("p (k e) -> p k e", e=NE)).then_inc(S["fgt_done"], 1)
        for q in range(WB):
            dve.wait_ge(S["prep_h"], q + 1)
            pair = [w[:, 0, :, cols(q)] for w in GUW] if q < GU // P else [w[:, 0, :, cols(q - GU // P)] for w in DNW]
            low_part(pair[1], pair[0], bank4(PREP_BANKS[q % PRING]), "prep_l")
        STEPS = 8

        def gates(n, c):
            def step(k, ins):
                ins.then_inc(S["t_chain"], 1)
                dve.wait_ge(S["t_chain"], c + k)
            dve.wait_ge(S["xg_in"], n * 16)
            step(1, dve.tensor_copy(y_gate[:, :], meta[:, 1, 0:1]))
            step(2, dve.tensor_copy(y_tok[:, :], meta[:, 1, 1:2]))
            step(3, dve.tensor_copy(meta[:, 1, :], meta[:, 0, :]))
            step(4, dve.tensor_copy(meta[:, 0, 1:2], xg[:, TCOL:TCOL + 1]))
            step(5, dve.scalar_tensor_tensor(gprod[:, :], xg[:, SCOL:SCOL + 4], slot[:, 0:1], xg[:, GCOL:GCOL + 4],
                                             op0=ALU.is_equal, op1=ALU.mult))
            step(6, dve.tensor_scalar(slot[:, :], slot[:, :], float(P), None, ALU.add))
            step(7, dve.tensor_reduce(meta[:, 0, 0:1], gprod[:, :], AX.X, ALU.add))
            dve.sem_inc(S["xg_read"], 1)
            dve.sem_inc(S["meta_done"], 1)

        dve.wait_ge(S["f_consts"], 2)
        dve.wait_ge(S["xt_h"], 1)
        low_part(xt[1][:, :, :], xt[0][:, :, :], bank4(2), "xt_l")
        gates(1, 0)
        dve.sem_inc(S["ht_l"], 1)
        tile_no = dve.alloc_register("dve_tile")
        dve.reg_mov(tile_no, 0)

        def tile(e, first):
            g = dve.snap(tile_no, min_val=0, max_val=TILES - 1)
            par = None if e is None else (e + 1) & 1

            def blocks(*qs):
                for q in qs if first else ():
                    dve.wait_ge(S["prep_h"], e * WB + (WB + q + 1))
                    ws, qq = (GUW, q) if q < GU // P else (DNW, q - GU // P)
                    pair = [w[:, bass.ds(par, 1), :, cols(qq)].rearrange("p o k n -> p (o k) n") for w in ws]
                    low_part(pair[1], pair[0], bank4(PREP_BANKS[q % PRING]), "prep_l")

            blocks(0, 1, 2)
            dve.wait_ge(S["sig_done"], g + 1)
            dve.tensor_tensor(ug[:, :], sig[:, :], B[0][:, :], ALU.mult).then_inc(S["t_chain"], 1)
            blocks(3, 4, 5, 6)
            dve.wait_ge(S["t_chain"], g * STEPS + STEPS)
            dve.wait_ge(S["up_pe"], g + 1)
            dve.tensor_tensor(hid[:, :], ug[:, :], B[1][:, :], ALU.mult).then_inc(S["hid_done"], 1)
            blocks(7)
            dve.wait_ge(S["xt_h"], g + 2)
            low_part(xt[1][:, :, :], xt[0][:, :, :], bank4(2), "xt_l")
            dve.wait_ge(S["y_free"], g + 1)
            dve.wait_ge(S["y_done"], g + 1)
            gates(g + 2, g * STEPS + STEPS)
            blocks(8)
            dve.wait_ge(S["ht_h"], g + 1)
            low_part(ht[1][:, :, :], ht[0][:, :, :], bank4(2), "ht_l")
            blocks(9, 10, 11)
            dve.reg_add(tile_no, tile_no, 1)

        def choose():
            dve.wait_ge(S["f_small"], 32)
            dve.wait_ge(S["f_aff"], 1)
            link(dve.tensor_tensor(score[:, :, :], aff[:, :, :], fb[:, :].unsqueeze(1).to_broadcast([P, NT, NE]), ALU.add))
            for i in range(NT):
                last = dve.max(f8[:, i, :], score[:, i, :])
            link(last)
            for i in range(NT):
                last = dve.max_index(f8i[:, i, :], f8[:, i, :], score[:, i, :])
            link(last)
            link(dve.tensor_copy(f8f[:, :, :], f8i[:, :, :]))

        def pick_gates():
            for k in range(TOPK):
                link(dve.tensor_tensor(pick[:, k, :, :], f8f[:, :, k:k + 1].to_broadcast([P, NT, NE]),
                                       io16[:, :].unsqueeze(1).to_broadcast([P, NT, NE]), ALU.is_equal))
                link(dve.tensor_tensor(tmp16[:, :, :], pick[:, k, :, :], aff[:, :, :], ALU.mult))
                link(dve.tensor_reduce(gsel[:, k, :], tmp16[:, :, :], AX.X, ALU.add))

        def count_picks():
            link(dve.tensor_tensor(gsum[:, 0, :], gsel[:, 0, :], gsel[:, 1, :], ALU.add))
            link(dve.tensor_tensor(gsum[:, 0, :], gsum[:, 0, :], gsel[:, 2, :], ALU.add))
            link(dve.tensor_scalar(gsum[:, 0, :], gsum[:, 0, :], 1e-9, None, ALU.add))
            link(dve.reciprocal(gsum[:, 1, :], gsum[:, 0, :]))
            dve.wait_ge(S["f_shared"], 16)
            for k in range(TOPK):
                link(dve.tensor_tensor(XR[:, :, GCOL + k], gsel[:, k, :], gsum[:, 1, :], ALU.mult))
            link(dve.tensor_tensor(tmp16[:, :, :], pick[:, 0, :, :], pick[:, 1, :, :], ALU.add))
            link(dve.tensor_tensor(tmp16[:, :, :], tmp16[:, :, :], pick[:, 2, :, :], ALU.add))
            link(dve.tensor_tensor(M[:, 0:NT, :], tmp16[:, :, :], valid[:, :].unsqueeze(2).to_broadcast([P, NT, NE]), ALU.mult))
            link(dve.memset(pref[:, 0, :], 0.0))
            for i in range(1, NT):
                link(dve.tensor_tensor(pref[:, i, :], pref[:, i - 1, :], M[:, i - 1, :], ALU.add))
            link(dve.tensor_tensor(M[:, NT, :], pref[:, NT - 1, :], M[:, NT - 1, :], ALU.add))
            dve.sem_inc(S["f_sel"], 1)

        def place():
            dve.wait_ge(S["f_rank"], 1)
            counts = B[3][:, NT * NE:(NT + 1) * NE]
            link(dve.tensor_scalar(cnt[:, 0, :], counts, float(P - 1), None, ALU.add))
            link(dve.tensor_copy(cnt_i[:, :], cnt[:, 0, :]))
            link(dve.tensor_scalar(cnt_i[:, :], cnt_i[:, :], 7, None, ALU.logical_shift_right))
            link(dve.tensor_copy(cnt[:, 1, :], cnt_i[:, :]))
            link(dve.tensor_scalar(cnt[:, 1, :], cnt[:, 1, :], 1.0, None, ALU.max))
            link(dve.tensor_copy(nt_i[:, 1:NE + 1], cnt[:, 1, :]))
            link(dve.memset(cnt[:, 2, :], 1.0))
            link(dve.tensor_tensor_scan(cnt[:, 3, :], cnt[:, 2, :], cnt[:, 1, :], float(NT), ALU.mult, ALU.add))
            link(dve.tensor_tensor(cnt[:, 4, :], cnt[:, 3, :], cnt[:, 1, :], ALU.subtract))
            link(dve.tensor_scalar(cnt[:, 4, :], cnt[:, 4, :], float(P), None, ALU.mult))
            ranks = B[3][:, 0:NT * NE].rearrange("p (t e) -> p t e", e=NE)
            link(dve.tensor_tensor(score[:, :, :], ranks, cnt[:, 4, :].unsqueeze(1).to_broadcast([P, NT, NE]), ALU.add))
            for k in range(TOPK):
                link(dve.tensor_tensor(tmp16[:, :, :], score[:, :, :], pick[:, k, :, :], ALU.mult))
                link(dve.tensor_reduce(sl[:, k, :], tmp16[:, :, :], AX.X, ALU.add))
                link(dve.tensor_copy(XR[:, :, SCOL + k], sl[:, k, :]))
            link(dve.tensor_copy(sl_u[:, :, :], sl[:, :, :]))
            dve.sem_inc(S["f_slots"], 1)


        routing = [(choose, pick_gates), (count_picks,), (place,)]
        experts(dve, tile, lambda i: [part() for part in routing[i]])
        g = dve.snap(tile_no, min_val=NT + NE, max_val=TILES)
        dve.wait_ge(S["y_free"], g + 1)
        gates(g + 1, g * STEPS + STEPS - 1)

    @block.tensor
    def _(pe):
        def product(bank, pairs, start=True, stop=True):
            todo = []
            for a, b in pairs:
                if isinstance(a, tuple):
                    todo += [(a[0], b[0]), (a[0], b[1]), (a[1], b[0])]
                else:
                    todo.append((a, b))
            for n, (a, b) in enumerate(todo):
                last = pe.matmul(bank, a, b, start=start and n == 0, stop=stop and n == len(todo) - 1)
            return last

        pe.wait_ge(S["consts"], 1)
        for i in range(NT):
            pe.wait_ge(S["xn_done"], i + 1)
            if i >= 2:
                pe.wait_ge(S["xt_done"], i - 1)
            for k in range(KD):
                last = pe.transpose(B[i % 2][:, cols(k)], XN[:, i, cols(k)], ident[:, :])
            last.then_inc(S["xt_pe"], 1)
        pe.wait_ge(S["edge_keys"], 1)
        pe.wait_ge(S["consts"], 1)
        T = B[2][:, :].rearrange("p (g k t) -> p g k t", g=2, k=2)
        for g, n in ((0, P), (1, ET - P)):
            pe.transpose(T[:, g, 0, 0:n], e_f[0:n, g, 3, :], ident[0:n, 0:n])
            pe.transpose(T[:, g, 1, 0:n], e_f[0:n, g, 1, :], ident[0:n, 0:n])
            for k in range(2):
                c = k * ET + g * P
                last = pe.matmul(B[3][0:NW, c:c + n], e_mm[0:n, g, k:k + 1].to_broadcast([n, NW]), ident[0:n, 0:n],
                                 start=True, stop=True)
        last.then_inc(S["edge_pe"], 1)
        pe.wait_ge(S["xt_done"], NT)
        pe.wait_ge(S["small_in"], 16 * (GE + 3))
        for i in range(NT):
            product(B[6][:, i * GE:(i + 1) * GE], [(XT[:, k, cols(i)], gw[:, k, :]) for k in range(KD)])\
                .then_inc(S["lg_pe"], 1)
        pe.transpose(B[7][:, 0:GE * KD], b1_rows[:, :], ident[0:GE * KD, 0:GE * KD]).then_inc(S["lg_pe"], 1)
        pe.wait_ge(S["edge_bounds"], 1)
        for k in range(3):
            last = pe.matmul(B[4][0:1, k * NW:(k + 1) * NW], lohi[:, 2 + k:3 + k], ident[0:NW, 0:NW], start=True, stop=True)
        last.then_inc(S["edge_pe"], 1)

        def window_pair(p):
            for w in (2 * p, 2 * p + 1):
                lo_h, b = w % 2, B[6 + w % 2][:, 0:WC]
                if w >= 2:
                    pe.wait_ge(S["win_done"], w - 1)
                for v in range(VISITS):
                    pe.wait_ge(S["hot_ready"], w * VISITS + v + 1)
                    last = pe.matmul(b, low1[:, lo_h, v, :], key1[:, lo_h, v, :], start=v == 0, stop=v == VISITS - 1)
                last.then_inc(S["win_pe"], 1)

        pe.wait_ge(S["wqkv_in"], 16)
        for n in range(12):
            (c, w), j = CHUNKS[n // KD], n % KD
            if n >= 2:
                pe.wait_ge(S["q_done"], n - 1)
            product(B[n % 2][:, 0:w], [(WQKV[:, k, cols(j)], XT[:, k, c:c + w]) for k in range(KD)])\
                .then_inc(S["q_pe"], 1)
            if n == 0:
                pe.wait_ge(S["ex_max"], 1)
            if n in PAIR_AFTER_Q:
                window_pair(PAIR_AFTER_Q[n])
        pe.wait_ge(S["bounds_out"], 1)
        for i in range(NT):
            if i >= 2:
                pe.wait_ge(S["k_done"], i - 1)
            product(B[2 + i % 2][:, :], [(XT[:, k, cols(i)], WQKV[:, k, D:2 * D]) for k in range(KD)])\
                .then_inc(S["k_pe"], 1)
            if i >= 2:
                pe.wait_ge(S["v_done"], i - 1)
            product(B[4 + i % 2][:, :], [(XT[:, k, cols(i)], WQKV[:, k, 2 * D:3 * D]) for k in range(KD)])\
                .then_inc(S["v_pe"], 1)
            window_pair(PAIR_AFTER_KV[i])
        pe.wait_ge(S["k_done"], NT)
        pe.wait_ge(S["v_done"], NT)
        pe.wait_ge(S["mix_setup"], 1)
        pe.wait_ge(S["win_done"], 2 * (PAIR_AFTER_KV[NT - 1] + 1))
        for h in range(HP):
            if h >= 2:
                pe.wait_ge(S["kv_done"], h - 1)
            product(B[6 + h % 2][:, 0:P + 1], [(K[:, i, cols(h)], V[:, i, h, 0:P + 1]) for i in range(NT)])\
                .then_inc(S["kv_pe"], 1)
        pe.wait_ge(S["kv_done"], HP)

        def denominators(chunk):
            c, w = CHUNKS[chunk]
            if chunk == 2:
                pe.wait_ge(S["den_done"], 1)
            product(B[4 + chunk % 2][0:2 * HP, 0:w], [(KS[:, h, :], QT[:, h, c:c + w]) for h in range(HP)])\
                .then_inc(S["den_pe"], 1)

        denominators(0)
        denominators(1)
        for n in range(12):
            (c, w), h = CHUNKS[n // HP], n % HP
            if n >= 2:
                pe.wait_ge(S["at_whole"], n - 1)
            product(B[n % 2][:, 0:w], [(KVB[:, h, :], QT[:, h, c:c + w])])
            if n % HP == 0:
                pe.wait_ge(S["den_done"], n // HP + 1)
            product(B[2 + n % 2][:, 0:w], [(heads[:, h, :], den[:, c:c + w])]).then_inc(S["at_pe"], 1)
            if n == 1:
                denominators(2)
        pe.wait_ge(S["wo_l"], 1)
        for i in range(NT):
            pe.wait_ge(S["at_done"], HP * sum(c < (i + 1) * P for c, w in CHUNKS))
            if i >= 2:
                pe.wait_ge(S["o_done"], i - 1)
            product(B[4 + i % 2][:, :], [((QH[:, h, cols(i)], QL[:, h, cols(i)]), (WO[1][:, h, :], WO[2][:, h, :]))
                                         for h in range(HP)]
                    ).then_inc(S["o_pe"], 1)
            if i in PAIR_AFTER_O:
                window_pair(PAIR_AFTER_O[i])

        long = pe.value_load(bounds_i[0:1, LONG:LONG + 1], min_val=0, max_val=ETP)
        with pe.If(long > 0):
            more = pe.alloc_register("pe_more")
            pe.reg_mov(more, 1)
            with pe.Fori(0, NW) as w:
                at = pe.value_load(bounds_i[0:1, bass.ds(w + NW, 1)], min_val=VISITS, max_val=ETP - 1)
                end = pe.value_load(bounds_i[0:1, bass.ds(w + 2 * NW, 1)], min_val=VISITS, max_val=ETP - 1)
                with pe.If(end > at):
                    with pe.Fori(at, end):
                        pe.wait_ge(S["lhot_ready"], pe.snap(more, min_val=1, max_val=NW * ET))
                        pe.matmul(B[6][:, 0:WC], low1[:, 0, 0, :], key1[:, 0, 0, :], start=True, stop=True)\
                            .then_inc(S["long_pe"], 1)
                        pe.reg_add(more, more, 1)

        def aggregate(n, i, bank, high, low, ones=None):
            def products(counts, parts, a, stop):
                for part in parts:
                    last = pe.matmul(bank, counts[:, a, :], part[:, a, :], start=False if started else True,
                                     stop=stop and part is parts[-1], skip_group_check=True)
                    started.append(1)
                return last
            started = []
            pe.wait_ge(S["conv_done"], n + 1)
            for a in range(NT - 1):
                products(conv[i % 2], (high, low), a, False)
            with pe.If(long > 0):
                pe.wait_ge(S["conv_l"], n + 1)
                for a in range(NT):
                    last = products(conv_low, (high,), a, False)
                if ones is None:
                    last.then_inc(S["ag_low_pe"], 1)
            if ones is not None:
                for a in range(NT):
                    pe.matmul(ones, conv[i % 2][:, a, :], ones_r[:, :], start=a == 0, stop=False, skip_group_check=True)
                with pe.If(long > 0):
                    for a in range(NT):
                        last = pe.matmul(ones, conv_low[:, a, :], ones_r[:, :], start=False, stop=False,
                                         skip_group_check=True)
                    last.then_inc(S["ag_low_pe"], 1)
            return products(conv[i % 2], (high, low), NT - 1, True)

        def transpose_rows_out(i):
            pe.wait_ge(S["ag_scaled"], i + 1)
            if i >= 2:
                pe.wait_ge(S["ag_done"], i - 1)
            for k in range(KD):
                last = pe.transpose(B[i % 2][:, cols(k)], t1[i % 2][:, cols(k)], ident[:, :])
            last.then_inc(S["ag_tpe"], 1)

        pe.wait_ge(S["xn_l"], NT)
        pe.sem_inc(S["ag_low_pe"], 1)
        pe.sem_inc(S["l1_pe"], RING)
        for i in range(NT):
            if i < 2:
                pe.wait_ge(S["o_done"], NT - 1 + i)
            else:
                pe.wait_ge(S["ag_scaled"], i - 1)
            aggregate(i, i, B[4 + i % 2][:, :], XN_H, XN_L, ones=B[2 + i % 2][:, 0:2]).then_inc(S["ag_pe"], 1)
            if i >= 1:
                transpose_rows_out(i - 1)
        transpose_rows_out(NT - 1)

        def parts(a, b):
            return (a[0], b[0]), (a[0], b[1]), (a[1], b[0])

        pe.wait_ge(S["ag_done"], NT)
        pe.sem_inc(S["g_pe"], 2)
        pe.sem_inc(S["e_pe"], 1)
        with pe.Fori(0, GE) as e:
            half = pe.snap(e & 1, min_val=0, max_val=1)
            other = pe.snap((e + 1) & 1, min_val=0, max_val=1)
            for n in range(STEPS1):
                chunk, k = n // (2 * KD), n % (2 * KD)
                if chunk == 1 and k == 0:
                    pe.wait_ge(S["e_gated"], e * NT + 2)
                c, w = HCHUNKS[chunk]
                whi, wlo, xhi, xlo = slabs[n % RING]
                if chunk == 2 and k == 0:
                    pe.wait_ge(S["h_done"], e * 12 + 4)
                pe.wait_ge(S["slab_l"], e * STEPS1 + (STEPS1 + n + 1))
                for j in range(KD):
                    if n == 0 and j == 2:
                        pe.wait_ge(S["e_scaled"], e * NT + 1)
                    for m, (a, b) in enumerate(parts((whi[:, cols(j)], wlo[:, cols(j)]), (xhi[:, 0:w], xlo[:, 0:w]))):
                        last = pe.matmul(B[4 * (chunk % 2) + j][:, 0:w], a, b, start=k == 0 and m == 0,
                                         stop=k == 2 * KD - 1 and m == 2)
                last.then_inc(S["l1_pe"], 1)

            def with_weights(bank, u, which):
                pe.wait_ge(S["hs_l"], e * (2 * NT) + (u + 1))
                for k in range(KD):
                    rows = [t[:, k, :] for t in hs[u % 2]]
                    weights = [WR[:, bass.ds(which, 1), m, k, :].rearrange("p o n -> p (o n)") for m in range(2)]
                    for m, (a, b) in enumerate(parts(rows, weights)):
                        last = pe.matmul(bank, a, b, start=k == 0 and m == 0, stop=k == KD - 1 and m == 2)
                return last

            pe.wait_ge(S["h_done"], e * 12 + 8)
            pe.wait_ge(S["w2_l"], e * (1 + KD) + 1)
            for i in range(NT):
                pe.wait_ge(S["g_done"], e * NT + i + 1)
                with_weights(B[4 + i % 2][:, :], i, other).then_inc(S["g_pe"], 1)
            pe.wait_ge(S["w2_l"], e * (1 + KD) + (1 + KD))
            for i in range(NT):
                pe.wait_ge(S["e_gated"], e * NT + i + 1)
                with_weights(B[6 + i % 2][:, :], NT + i, half).then_inc(S["own_pe"], 1)
                if i == 0:
                    pe.wait_ge(S["g_done"], e * NT + NT + 2)
                aggregate(e * NT + (i + NT), i, B[2 + i % 2][:, :], GH, GL).then_inc(S["e_pe"], 1)

        pe.wait_ge(S["e_gated"], GE * NT + 2)
        pe.wait_ge(S["f_small"], 32)
        for k in range(KD):
            last = pe.transpose(B[2][:, k * NE:(k + 1) * NE], fg_raw[:, cols(k)], ident[0:NE, 0:NE])
        last.then_inc(S["fgt_pe"], 1)
        def weight_block(q):
            for k in range(KD):
                last = pe.transpose(B[PREP_BANKS[q % PRING]][:, cols(k)], raw[:, q, cols(k)], ident[:, :])
            last.then_inc(S["prep_pe"], 1)

        def logits(i):
            if i == 0:
                pe.wait_ge(S["fgt_done"], 1)
            pe.wait_ge(S["f_tdone"], i + 1)
            if i >= 1:
                pe.wait_ge(S["f_lgdone"], i)
            product(B[5][0:NE, 0:P], [(fgT[:, k, :], xft[i % 2][:, k, :]) for k in range(KD)])\
                .then_inc(S["f_lg"], 1)

        def shared_block(q):
            if q % RB == 0:
                pe.wait_ge(raw_in[q // RB], 16)
            if q >= PRING:
                pe.wait_ge(S["prep_l"], q - PRING + 1)
            weight_block(q)

        for q in range(PRING - 1):
            shared_block(q)
        for q in range(WB):
            if q + PRING - 1 < WB:
                shared_block(q + PRING - 1)
            if q < NT:
                pe.wait_ge(S["f_xn"], q + 1)
                for k in range(KD):
                    last = pe.transpose(B[q % 2][:, cols(k)], XR[:, q, cols(k)], ident[:, :])
                last.then_inc(S["f_tpe"], 1)
            if 1 <= q <= NT:
                logits(q - 1)

        def transpose_rows(n):
            pe.wait_ge(S["xg_in"], n * 16)
            for k in range(KD):
                last = pe.transpose(B[2][:, cols(k)], xg[:, cols(k)], ident[:, :])
            last.then_inc(S["xt_tpe"], 1)

        transpose_rows(1)
        pe.wait_ge(S["f_lgdone"], NT)
        for i in range(NT):
            last = pe.transpose(B[5][:, i * NE:(i + 1) * NE], lgT[:, cols(i)], ident[0:NE, 0:NE])
        last.then_inc(S["f_lgt"], 1)
        tile_no = pe.alloc_register("pe_tile")
        pe.reg_mov(tile_no, 0)
        previous = pe.alloc_register("pe_previous")
        pe.reg_mov(previous, 1)

        def split_product(bank, rows, weights, after):
            for k in range(KD):
                for n, (a, b) in enumerate(((0, 0), (0, 1), (1, 0))):
                    last = pe.matmul(bank, rows[a][:, k, :], weights[b](k), start=k == 0 and n == 0,
                                     stop=k == KD - 1 and n == 2)
                if k < KD - 1:
                    after(k)
            return last

        def down(g, after=lambda k: None):
            pe.wait_ge(S["ht_l"], g + 1)
            pe.wait_ge(S["y_done"], g + 1)
            par = pe.snap(previous, min_val=0, max_val=1)
            split_product(B[5][:, :], ht, [lambda k, w=w: w[:, bass.ds(par, 1), k, :].rearrange("p o n -> p (o n)")
                                           for w in DNW], after).then_inc(S["dn_pe"], 1)
            after(KD - 1)

        def tile(e, first):
            g = pe.snap(tile_no, min_val=0, max_val=TILES - 1)
            ee = NE if e is None else e
            par = ee & 1

            def block(q):
                if first:
                    if q % RB == 0:
                        pe.wait_ge(raw_in[q // RB], e * 16 + 32)
                    pe.wait_ge(S["prep_l"], e * WB + (WB + q - PRING + 1))
                    weight_block(q)

            pe.wait_ge(S["xt_l"], g + 1)
            for half, done in ((0, "gate_pe"), (1, "up_pe")):
                split_product(B[half][:, :], xt,
                              [lambda k, w=w: w[:, bass.ds(par, 1), k, half * FF:(half + 1) * FF]
                               .rearrange("p o n -> p (o n)") for w in GUW],
                              lambda k: block(half * KD + k)).then_inc(S[done], 1)
                block(half * KD + KD - 1)
            pe.wait_ge(S["ht_l"], g + 1)
            transpose_rows(g + 2)
            down(g, lambda k: block(2 * KD + k))
            pe.reg_mov(previous, par)
            pe.wait_ge(S["hid_done"], g + 1)
            pe.wait_ge(S["xt_l"], g + 2)
            for k in range(KD):
                last = pe.transpose(B[2][:, cols(k)], hid[:, cols(k)], ident[:, :])
            last.then_inc(S["h_tpe"], 1)
            pe.reg_add(tile_no, tile_no, 1)

        pe.wait_ge(S["prep_l"], WB)
        pe.wait_ge(S["f_aff"], 1)

        def between(i):
            if i != SHARED_APART - 1:
                return
            pe.wait_ge(S["f_sel"], 1)
            product(B[3][:, 0:NT * NE], [(upper[:, :], M[:, 0:NT, :].rearrange("p t e -> p (t e)")),
                                         (ones2[:, :], pref[:, :, :].rearrange("p t e -> p (t e)"))])
            product(B[3][:, NT * NE:(NT + 1) * NE], [(ones2[:, :], M[:, NT, :])]).then_inc(S["f_rank"], 1)

        experts(pe, tile, between)
        down(pe.snap(tile_no, min_val=NT + NE, max_val=TILES))

    ctx.close()


_INS = ["x", "src", "dst", "L0_gnn_gate_W", "L0_gnn_gate_b", "L0_gnn_Wl", "L0_gnn_bl", "L0_gnn_Wr",
        "L0_mix_w_qkv", "L0_mix_w_out", "L0_mix_b_out", "L0_ffn_gate_w", "L0_ffn_expert_bias",
        "L0_ffn_shared_gate_up", "L0_ffn_shared_down", "L0_ffn_expert_gate_up", "L0_ffn_expert_down"]


def kernel(**inputs):
    import numpy as np
    import concourse.bacc as bacc
    from concourse.bass_utils import run_bass_kernel_spmd

    nc = bacc.Bacc("TRN2", target_bir_lowering=False, num_devices=1)
    arrays, args = {}, []
    for name in _INS:
        a = np.ascontiguousarray(inputs[name])
        arrays[f"in_{name}"] = a
        args.append(nc.dram_tensor(f"in_{name}", a.shape, mybir.dt.from_np(a.dtype), kind="ExternalInput").ap())
    args.append(nc.dram_tensor("out_rows", (N + P, D), F32, kind="ExternalOutput").ap())
    program(nc, *args)
    r = run_bass_kernel_spmd(nc, [arrays], core_ids=[0])
    return r.results[0]["out_rows"][0:N]
```
